# Optimizing a Trainium2 kernel written in Bass

```python
import numpy as np
import jax
import jax.numpy as jnp

def _softmax(x, axis=-1):
    return jax.nn.softmax(x, axis=axis)

def _gelu(x):
    return jax.nn.gelu(x, approximate=True)

def _silu(x):
    return jax.nn.silu(x)

def _sigmoid(x):
    return jax.nn.sigmoid(x)

def _layernorm(x, axis=-1, eps=1e-05):
    m = jnp.mean(x, axis=axis, keepdims=True)
    v = jnp.var(x, axis=axis, keepdims=True)
    return (x - m) / jnp.sqrt(v + eps)

def _scatter_add(tgt, idx, src, axis=0):
    return tgt.at[idx].add(src)

def _segment_sum(src, seg, n):
    return jax.ops.segment_sum(src, seg, n)
kernel_name = 'mk_xattn_ffn_d2_seqx_r4_4a5bc8'

def setup_inputs(seed: int=0):
    np.random.seed(seed)
    _w = jnp.asarray

    def _rec_inputs():
        import jax
        import jax.numpy as jnp
        _rk = jax.random.key(seed)
        x = 7.22e-05 + 1 * jax.random.normal(jax.random.fold_in(_rk, 1), (4, 512, 256), jnp.float32)
        _lenS = 512 - jax.random.randint(jax.random.fold_in(_rk, 7), (4,), 0, max(1, 512 // 4) + 1, jnp.int32)
        _lenS2 = 64 - jax.random.randint(jax.random.fold_in(_rk, 8), (4,), 0, max(1, 64 // 4) + 1, jnp.int32)
        _ctx_1024P = jax.random.normal(jax.random.fold_in(_rk, 11), (4, 16, 256), jnp.float32)
        _ctx_1024c = jax.random.dirichlet(jax.random.fold_in(_rk, 511), 0.3 * jnp.ones((16,), jnp.float32), (4, 64))
        _ctx_1024t = jnp.einsum('bsk,bkd->bsd', _ctx_1024c, _ctx_1024P)
        _ctx_1024t = _ctx_1024t * jax.lax.rsqrt(jnp.mean(jnp.square(_ctx_1024t)) + 1e-12) * 0.953939
        ctx_1024 = -1.39393e-06 + 0.999914 * (_ctx_1024t + 0.3 * jax.random.normal(jax.random.fold_in(_rk, 611), (4, 64, 256), jnp.float32))
        return (x, ctx_1024)
    x, ctx_1024 = _rec_inputs()

    def _L0_xattn_setup():
        import jax, jax.numpy as jnp
        import numpy as np
        EPS = 1e-05

        def layernorm(x, g, b):
            mu = jnp.mean(x, axis=-1, keepdims=True)
            var = jnp.var(x, axis=-1, keepdims=True)
            return (x - mu) * jax.lax.rsqrt(var + EPS) * g + b
        DIM = 256
        CTX = 256
        HEADS = 12
        DHEAD = 64
        INNER = HEADS * DHEAD
        B = 4
        F = 512
        J = 256
        key = jax.random.key(seed)
        ks = jax.random.split(key, 8)
        s = lambda d: 1.0 / np.sqrt(d)
        return {'x': jax.random.normal(ks[0], (B, F, DIM), jnp.float32), 'tab_x': jax.random.normal(ks[1], (B, J, CTX), jnp.float32), 'tab_g': jnp.ones((CTX,), jnp.float32), 'tab_b': jnp.zeros((CTX,), jnp.float32), 'vid_g': jnp.ones((DIM,), jnp.float32), 'vid_b': jnp.zeros((DIM,), jnp.float32), 'Wq': jax.random.normal(ks[2], (DIM, INNER), jnp.float32) * s(DIM), 'Wk': jax.random.normal(ks[3], (CTX, INNER), jnp.float32) * s(CTX), 'Wv': jax.random.normal(ks[4], (CTX, INNER), jnp.float32) * s(CTX), 'q_g': jnp.ones((INNER,), jnp.float32), 'q_b': jnp.zeros((INNER,), jnp.float32), 'k_g': jnp.ones((INNER,), jnp.float32), 'k_b': jnp.zeros((INNER,), jnp.float32), 'Wo': jax.random.normal(ks[5], (INNER, DIM), jnp.float32) * s(INNER), 'bo': jnp.zeros((DIM,), jnp.float32)}
    _L0_xattn_all = _L0_xattn_setup()
    _L0_xattn_in = {k: v for k, v in _L0_xattn_all.items() if k in ('tab_g', 'tab_b', 'vid_g', 'vid_b', 'Wq', 'Wk', 'Wv', 'q_g', 'q_b', 'k_g', 'k_b', 'Wo', 'bo')}
    del _L0_xattn_all

    def _L0_ffn_setup():
        import jax, jax.numpy as jnp
        import numpy as np
        HIDDEN = 256
        INNER = 1024

        def _weight_quant(w):
            scale = 1.0 / jnp.clip(jnp.mean(jnp.abs(w)), 1e-05)
            wq = jnp.clip(jnp.round(w * scale), -1.0, 1.0) / scale
            return w + jax.lax.stop_gradient(wq - w)

        def _act_quant(x):
            scale = 127.0 / jnp.clip(jnp.max(jnp.abs(x), axis=-1, keepdims=True), 1e-05)
            xq = jnp.clip(jnp.round(x * scale), -128.0, 127.0) / scale
            return x + jax.lax.stop_gradient(xq - x)

        def _bitlinear(x, w):
            return jnp.einsum('bsi,oi->bso', _act_quant(x), _weight_quant(w))
        key = jax.random.key(seed)
        k0, k1, k2, k3 = jax.random.split(key, 4)
        x = jax.random.normal(k0, (4, 512, HIDDEN), dtype=jnp.float32)
        w_gate = jax.random.normal(k1, (INNER, HIDDEN), dtype=jnp.float32) / np.sqrt(HIDDEN)
        w_up = jax.random.normal(k2, (INNER, HIDDEN), dtype=jnp.float32) / np.sqrt(HIDDEN)
        w_down = jax.random.normal(k3, (HIDDEN, INNER), dtype=jnp.float32) / np.sqrt(INNER)
        return {'x': x, 'w_gate': w_gate, 'w_up': w_up, 'w_down': w_down}
    _L0_ffn_all = _L0_ffn_setup()
    _L0_ffn_in = {k: v for k, v in _L0_ffn_all.items() if k in ('w_gate', 'w_up', 'w_down')}
    del _L0_ffn_all

    def _L1_xattn_setup():
        import jax, jax.numpy as jnp
        import numpy as np
        D1, D2, D3 = (256, 256, 256)
        key = jax.random.key(seed)
        k1, k2, kw, kb = jax.random.split(key, 4)
        x1 = jax.random.normal(k1, (8, 512, D1), dtype=jnp.float32)
        x2 = jax.random.normal(k2, (8, 512, D2), dtype=jnp.float32)
        bound = 1.0 / np.sqrt(D1 + D2)
        W = jax.random.uniform(kw, (D3, D1 + D2), minval=-bound, maxval=bound, dtype=jnp.float32)
        b = jax.random.uniform(kb, (D3,), minval=-bound, maxval=bound, dtype=jnp.float32)
        return {'x1': x1, 'x2': x2, 'W': W, 'b': b}
    _L1_xattn_all = _L1_xattn_setup()
    _L1_xattn_in = {k: v for k, v in _L1_xattn_all.items() if k in ('W', 'b')}
    del _L1_xattn_all

    def _L1_ffn_setup():
        import jax, jax.numpy as jnp
        import numpy as np
        TOP_K = 2
        EPS = 1e-20
        key = jax.random.key(seed)
        ks = jax.random.split(key, 8)
        B, S, H, E, D = (4, 512, 256, 8, 512)
        s = 0.02
        return {'x': jax.random.normal(ks[0], (B, S, H), dtype=jnp.float32), 'Wr': jax.random.normal(ks[1], (H, E), dtype=jnp.float32) * s, 'Wg': jax.random.normal(ks[2], (E, H, D), dtype=jnp.float32) * s, 'Wu': jax.random.normal(ks[3], (E, H, D), dtype=jnp.float32) * s, 'Wd': jax.random.normal(ks[4], (E, D, H), dtype=jnp.float32) * s, 'Sg': jax.random.normal(ks[5], (H, D), dtype=jnp.float32) * s, 'Su': jax.random.normal(ks[6], (H, D), dtype=jnp.float32) * s, 'Sd': jax.random.normal(ks[7], (D, H), dtype=jnp.float32) * s}
    _L1_ffn_all = _L1_ffn_setup()
    _L1_ffn_in = {k: v for k, v in _L1_ffn_all.items() if k in ('Wr', 'Wg', 'Wu', 'Wd', 'Sg', 'Su', 'Sd')}
    del _L1_ffn_all
    return {'x': x, 'ctx_1024': ctx_1024, 'L0_xattn_tab_g': _L0_xattn_in['tab_g'], 'L0_xattn_tab_b': _L0_xattn_in['tab_b'], 'L0_xattn_vid_g': _L0_xattn_in['vid_g'], 'L0_xattn_vid_b': _L0_xattn_in['vid_b'], 'L0_xattn_Wq': _L0_xattn_in['Wq'], 'L0_xattn_Wk': _L0_xattn_in['Wk'], 'L0_xattn_Wv': _L0_xattn_in['Wv'], 'L0_xattn_q_g': _L0_xattn_in['q_g'], 'L0_xattn_q_b': _L0_xattn_in['q_b'], 'L0_xattn_k_g': _L0_xattn_in['k_g'], 'L0_xattn_k_b': _L0_xattn_in['k_b'], 'L0_xattn_Wo': _L0_xattn_in['Wo'], 'L0_xattn_bo': _L0_xattn_in['bo'], 'L0_ffn_w_gate': _L0_ffn_in['w_gate'], 'L0_ffn_w_up': _L0_ffn_in['w_up'], 'L0_ffn_w_down': _L0_ffn_in['w_down'], 'L1_xattn_W': _L1_xattn_in['W'], 'L1_xattn_b': _L1_xattn_in['b'], 'L1_ffn_Wr': _L1_ffn_in['Wr'], 'L1_ffn_Wg': _L1_ffn_in['Wg'], 'L1_ffn_Wu': _L1_ffn_in['Wu'], 'L1_ffn_Wd': _L1_ffn_in['Wd'], 'L1_ffn_Sg': _L1_ffn_in['Sg'], 'L1_ffn_Su': _L1_ffn_in['Su'], 'L1_ffn_Sd': _L1_ffn_in['Sd']}

def reference(x, ctx_1024, L0_xattn_tab_g, L0_xattn_tab_b, L0_xattn_vid_g, L0_xattn_vid_b, L0_xattn_Wq, L0_xattn_Wk, L0_xattn_Wv, L0_xattn_q_g, L0_xattn_q_b, L0_xattn_k_g, L0_xattn_k_b, L0_xattn_Wo, L0_xattn_bo, L0_ffn_w_gate, L0_ffn_w_up, L0_ffn_w_down, L1_xattn_W, L1_xattn_b, L1_ffn_Wr, L1_ffn_Wg, L1_ffn_Wu, L1_ffn_Wd, L1_ffn_Sg, L1_ffn_Su, L1_ffn_Sd):
    import jax
    import jax.numpy as jnp

    def _L0_xattn_ref(x, tab_x, tab_g, tab_b, vid_g, vid_b, Wq, Wk, Wv, q_g, q_b, k_g, k_b, Wo, bo):
        import jax, jax.numpy as jnp
        import numpy as np
        EPS = 1e-05

        def layernorm(x, g, b):
            mu = jnp.mean(x, axis=-1, keepdims=True)
            var = jnp.var(x, axis=-1, keepdims=True)
            return (x - mu) * jax.lax.rsqrt(var + EPS) * g + b
        DIM = 256
        CTX = 256
        HEADS = 12
        DHEAD = 64
        INNER = HEADS * DHEAD
        B = 4
        F = 512
        J = 256
        scale = DHEAD ** (-0.5)
        kv_in = layernorm(tab_x, tab_g, tab_b)
        q = layernorm(layernorm(x, vid_g, vid_b) @ Wq, q_g, q_b)
        k = layernorm(kv_in @ Wk, k_g, k_b)
        v = kv_in @ Wv
        split = lambda t: t.reshape(t.shape[0], t.shape[1], HEADS, DHEAD).transpose(0, 2, 1, 3)
        q, k, v = (split(q) * scale, split(k), split(v))
        sim = jnp.einsum('bhid,bhjd->bhij', q, k)
        attn = jax.nn.softmax(sim, axis=-1)
        out = jnp.einsum('bhij,bhjd->bhid', attn, v)
        out = out.transpose(0, 2, 1, 3).reshape(x.shape[0], x.shape[1], INNER)
        return out @ Wo + bo

    def _L0_ffn_ref(x, w_gate, w_up, w_down):
        import jax, jax.numpy as jnp
        import numpy as np
        HIDDEN = 256
        INNER = 1024

        def _weight_quant(w):
            scale = 1.0 / jnp.clip(jnp.mean(jnp.abs(w)), 1e-05)
            wq = jnp.clip(jnp.round(w * scale), -1.0, 1.0) / scale
            return w + jax.lax.stop_gradient(wq - w)

        def _act_quant(x):
            scale = 127.0 / jnp.clip(jnp.max(jnp.abs(x), axis=-1, keepdims=True), 1e-05)
            xq = jnp.clip(jnp.round(x * scale), -128.0, 127.0) / scale
            return x + jax.lax.stop_gradient(xq - x)

        def _bitlinear(x, w):
            return jnp.einsum('bsi,oi->bso', _act_quant(x), _weight_quant(w))
        gate = jax.nn.silu(_bitlinear(x, w_gate))
        up = _bitlinear(x, w_up)
        return _bitlinear(gate * up, w_down)

    def _L1_xattn_ref(x1, x2, W, b):
        import jax, jax.numpy as jnp
        import numpy as np
        D1, D2, D3 = (256, 256, 256)
        d1 = x1.shape[-1]
        W1 = W[:, :d1]
        W2 = W[:, d1:]
        part1 = jnp.einsum('bld,ed->ble', x1, W1)
        part2 = jnp.einsum('bld,ed->be', x2, W2) / x2.shape[1]
        return part1 + part2[:, None, :] + b

    def _L1_ffn_ref(x, Wr, Wg, Wu, Wd, Sg, Su, Sd):
        import jax, jax.numpy as jnp
        import numpy as np
        TOP_K = 2
        EPS = 1e-20
        B, S, H = x.shape
        T = B * S
        xt = x.reshape(T, H)
        scores = jax.nn.softmax(xt @ Wr, axis=-1)
        topk_w, topk_idx = jax.lax.top_k(scores, TOP_K)
        topk_w = topk_w / (topk_w.sum(axis=-1, keepdims=True) + EPS)
        g = jax.nn.silu(jnp.einsum('th,ehd->etd', xt, Wg))
        u = jnp.einsum('th,ehd->etd', xt, Wu)
        out_all = jnp.einsum('etd,edh->eth', g * u, Wd)
        tok = jnp.arange(T)[:, None]
        gathered = out_all[topk_idx, tok, :]
        out = jnp.sum(gathered * topk_w[..., None], axis=1).reshape(B, S, H)
        shared = jax.nn.silu(x @ Sg) * (x @ Su) @ Sd
        return out + shared
    x = x + _L0_xattn_ref(_layernorm(x, axis=-1), ctx_1024, L0_xattn_tab_g, L0_xattn_tab_b, L0_xattn_vid_g, L0_xattn_vid_b, L0_xattn_Wq, L0_xattn_Wk, L0_xattn_Wv, L0_xattn_q_g, L0_xattn_q_b, L0_xattn_k_g, L0_xattn_k_b, L0_xattn_Wo, L0_xattn_bo)
    x = x + _L0_ffn_ref(_layernorm(x, axis=-1), L0_ffn_w_gate, L0_ffn_w_up, L0_ffn_w_down)
    x = x + _L1_xattn_ref(_layernorm(x, axis=-1), ctx_1024, L1_xattn_W, L1_xattn_b)
    x = x + _L1_ffn_ref(_layernorm(x, axis=-1), L1_ffn_Wr, L1_ffn_Wg, L1_ffn_Wu, L1_ffn_Wd, L1_ffn_Sg, L1_ffn_Su, L1_ffn_Sd)
    return x

_drawn_inputs = setup_inputs


def setup_inputs(seed=0):
    import zlib

    import numpy as np

    out = dict(_drawn_inputs(seed))
    spreads = {'L0_xattn_tab_g': (1.0, 0.2),
     'L0_xattn_tab_b': (0.0, 0.1),
     'L0_xattn_vid_g': (1.0, 0.2),
     'L0_xattn_vid_b': (0.0, 0.343),
     'L0_xattn_q_g': (1.0, 0.2),
     'L0_xattn_q_b': (0.0, 0.428),
     'L0_xattn_k_g': (1.0, 0.2),
     'L0_xattn_k_b': (0.0, 0.8),
     'L0_xattn_bo': (0.0, 0.1)}
    factors = {'L1_xattn_b': 3.025,
     'L1_ffn_Wr': 4.806,
     'L1_ffn_Wg': 4.273,
     'L1_ffn_Wu': 4.21,
     'L1_ffn_Wd': 4.206,
     'L1_ffn_Sg': 3.054,
     'L1_ffn_Su': 3.018,
     'L1_ffn_Sd': 3.015}
    for name, (base, spread) in spreads.items():
        noise = np.random.default_rng([zlib.crc32(name.encode()), seed]).standard_normal(out[name].shape)
        drawn = base * np.exp(spread * noise) if base else spread * noise
        out[name] = jnp.asarray(drawn.astype(out[name].dtype))
    for name, factor in factors.items():
        out[name] = (out[name] * factor).astype(out[name].dtype)
    return out
```

```python
import concourse.bass as bass
from concourse import mybir
from contextlib import ExitStack


class Steps:

    def __init__(self, sem, per=1):
        self.sem = sem
        self.per = per

    def upto(self, tile, step=None):
        return tile * self.per + (self.per if step is None else step)


def skewed(engine, stages, count, unroll):
    deepest = max(lag for lag, _ in stages)

    def step(j, at, block):
        for lag, stage in stages:
            if at is None:
                if 0 <= j - lag < count:
                    stage(j - lag, (j - lag) // unroll, (j - lag) % unroll)
            else:
                tile = at - lag
                stage(unroll * block + tile, block + tile // unroll, tile % unroll)

    first = deepest + 2
    rounds = (count - first) // unroll
    for j in range(first):
        step(j, None, None)
    if rounds > 0:
        with engine.Fori(0, rounds) as i:
            for k in range(unroll):
                step(None, first + k, i)
    for j in range(first + rounds * unroll, count + deepest):
        step(j, None, None)


def build(nc, x, ctx_in, tab_g, tab_b, vid_g, vid_b, Wq, Wk, Wv, q_g, q_b, k_g, k_b, Wo, bo,
          w_gate, w_up, w_down, W_l1, b_l1, Wr, Wg, Wu, Wd, Sg, Su, Sd, out):
    fp32, f16, i32 = mybir.dt.float32, mybir.dt.float16, mybir.dt.int32
    ALU = mybir.AluOpType
    ACT = mybir.ActivationFunctionType
    X = mybir.AxisListType.X

    P = 128
    B, F, D = x.shape
    LC = ctx_in.shape[1]
    NT = B * F // P
    TB = F // P
    KC = D // P
    INNER = Wq.shape[1]
    DH = 64
    H = INNER // DH
    QC = INNER // P
    CT = B * LC // P
    FI = w_gate.shape[0]
    IC = FI // P
    BANK = 512
    EPS = 1e-5
    MAGIC = 1.5 * 2.0 ** 23
    WS = 2.0 ** 8
    HI, LO = 0, 1
    E, DE = Wr.shape[1], Sg.shape[1]
    EC = DE // P
    WIDE = 3 * KC * DE
    TOP = 2
    NS = (TOP * B * F) // P + E - 1
    YR = 8

    es = ExitStack()
    with es:
        def sb(name, shape, dt=fp32, scope=None):
            return (scope or es).enter_context(nc.sbuf_tensor(name, shape, dt))

        def sem(name):
            return es.enter_context(nc.semaphore(name))

        def steps(name, per=1):
            return Steps(sem(name), per)

        waits_passed = sem("waits_passed")

        def wait_apart(engine, sem, value):
            engine.wait_ge(sem, value)
            engine.sem_inc(waits_passed, 1)

        def one(t):
            return bass.ds(t, 1)

        def tile_cols(t):
            return bass.ds(t * P, P)

        xs = sb("xs", [P, NT, D])
        zT = sb("zT", [P, 2, KC, NT * P], f16)
        ident = sb("ident", [P, P])
        ident16 = sb("ident16", [P, P], f16)
        ones64 = sb("ones64", [P, P], f16)
        ones16 = sb("ones16", [P, P], f16)
        before16 = sb("before16", [P, P], f16)
        nhalf = sb("nhalf", [P, NT])
        ones = sb("ones", [P, P])
        stage = sb("stage", [P, 2, WIDE])
        wr = sb("wr", [P, 2, KC, E], f16)
        mv = sb("mv", [P, 2, 2])
        st = sb("st", [P, 2, 12])
        small = sb("small", [P, 2, 16])
        z = sb("z", [P, 2, D])

        early = es.enter_context(ExitStack())
        gT = sb("gT", [P, 2, KC, FI], f16, early)
        dT = sb("dT", [P, IC, D], f16, early)
        wl1 = sb("wl1", [P, 2, 2 * KC, D], f16, early)
        wsc = sb("wsc", [P, 12], fp32, early)
        bias_l1 = sb("bias_l1", [P, B, D], fp32, early)
        bo_b = sb("bo_b", [P, D], fp32, early)
        vecs = sb("vecs", [P, 4, KC], fp32, early)
        hvec = sb("hvec", [P, 4, QC], fp32, early)
        csum = sb("csum", [P, KC, B], fp32, early)
        csum_rep = sb("csum_rep", [P, 2, KC, P], f16, early)
        st_all = sb("st_all", [P, NT, 6], fp32, early)
        ln_all = sb("ln_all", [P, 10, NT], fp32, early)
        zeros = sb("zeros", [P, 2 * D], f16, early)

        att = es.enter_context(ExitStack())
        con = att.enter_context(ExitStack())
        zf = sb("zf", [P, 2, D], fp32, con)
        cx = sb("cx", [P, CT, D], fp32, con)
        cTk = sb("cTk", [P, 2, KC, CT * P], f16, con)
        cf = sb("cf", [P, KC, CT * P], fp32, con)
        cT = sb("cT", [P, 2, KC, B, P], f16, con)
        kf = sb("kf", [P, QC, CT * P], fp32, con)
        kq = sb("kq", [P, QC, CT * P], fp32, con)
        wk = sb("wk", [P, 2, KC * INNER], f16, con)
        wv = sb("wv", [P, 2, KC * INNER], f16, con)
        qbm = sb("qbm", [P, QC, 2, P], fp32, con)
        bhi = sb("bhi", [P, B, INNER], f16, con)
        con.close()
        qT = sb("qT", [P, 2, QC, NT * P], f16, att)
        wq = sb("wq", [P, 2, KC * INNER], f16, att)
        wo = sb("wo", [P, 2, QC * D], f16, att)
        Kbd = sb("Kbd", [P, 2, B, QC, P], f16, att)
        Vbd = sb("Vbd", [P, 2, B, QC, P], f16, att)
        SB = sb("SB", [P, B, INNER], f16, att)
        nq = sb("nq", [P, 2, INNER], fp32, att)
        sm = sb("sm", [P, 2, INNER], fp32, att)
        red = sb("red", [P, 2, 2, H], fp32, att)
        pT = sb("pT", [P, 2, INNER], f16, att)
        oT = sb("oT", [P, 2, INNER], f16, att)
        qnt = att.enter_context(ExitStack())
        wtern = sb("wtern", [P, 2, FI * D // P], f16, qnt)
        xrep = sb("xrep", [P, KC, P], fp32, qnt)
        qnt.close()
        att.close()

        f0 = es.enter_context(ExitStack())
        xc = sb("xc", [P, 2, D], fp32, f0)
        zq = sb("zq", [P, 2, D], f16, f0)
        zqT = sb("zqT", [P, 2, D], f16, f0)
        hg = sb("hg", [P, FI], fp32, f0)
        hh = sb("hh", [P, 2, FI], fp32, f0)
        hq = sb("hq", [P, FI], f16, f0)
        hqT = sb("hqT", [P, 2, FI], f16, f0)
        sc0 = sb("sc0", [P, 2, 8], fp32, f0)
        sc1 = sb("sc1", [P, 2, 8], fp32, f0)
        f0.close()
        early.close()

        wflat = sb("wflat", [P, (E + 1) * 2 * WIDE + NT * 2 * D - 2 * WIDE], f16)
        wexp = wflat[:, 0:(E + 1) * 2 * WIDE].rearrange("p (e s n) -> p e s n", s=2, n=WIDE)
        zrow = wflat[:, E * 2 * WIDE:E * 2 * WIDE + NT * 2 * D].rearrange("p (t n) -> p t n", t=NT)
        xg = sb("xg", [P, 4, 2 * D], f16)
        xgT = sb("xgT", [P, 2, 2 * D], f16)
        eg = sb("eg", [P, 2, DE])
        eh = sb("eh", [P, 2, DE])
        ehT = sb("ehT", [P, 2, 2, DE], f16)
        yb = sb("yb", [P, 2, D])
        logits = sb("logits", [P, NT, E])
        r3 = sb("r3", [P, 5, NT, E])
        r2 = sb("r2", [P, 12, NT])
        r1 = sb("r1", [P, 6, E])
        w8i = sb("w8i", [P, E], i32)
        w8 = sb("w8", [P, E])
        A16 = sb("A16", [P, NT, E], f16)
        idx = sb("idx", [P, 2, NT], i32)
        tile_no = sb("tile_no", [P, NS])
        tcmp = sb("tcmp", [P, NS, E - 1])
        tsum = sb("tsum", [P, NS])
        tile_e = sb("tile_e", [P, NS], i32)
        yg = stage[:].rearrange("p a n -> p (a n)")[:, 0:YR * 2 * D].rearrange("p (r k d) -> p r k d", k=2, d=D)

        ps = es.enter_context(nc.psum_tensor("ps", [P, 8 * BANK], fp32))

        def banks(a, n=1):
            return ps[:, a * BANK:(a + n) * BANK]

        s_x, s_ctx, s_vec = sem("s_x"), sem("s_ctx"), sem("s_vec")
        s_stage = [sem("s_stage0"), sem("s_stage1")]
        s_const, s_fill, s_fill2, s_late = sem("s_const"), sem("s_fill"), sem("s_fill2"), sem("s_late")
        split_hi, split_lo = steps("split_hi"), steps("split_lo")
        d_chain = sem("d_chain")
        ctx_var, ctx_rstd, ctx_z, ctx_t, ctx_sum = (sem(n) for n in ("ctx_var", "ctx_rstd", "ctx_z", "ctx_t", "ctx_sum"))
        cf_ready, cT_hi, cT_lo = sem("cf_ready"), sem("cT_hi"), sem("cT_lo")
        k_mm, k_var, k_rstd, k_bias, k_norm, k_t = (sem(n) for n in ("k_mm", "k_var", "k_rstd", "k_bias", "k_norm", "k_t"))
        kq_ready, K_hi, K_lo, v_mm, V_hi, V_lo = (sem(n) for n in ("kq_ready", "K_hi", "K_lo", "v_mm", "V_hi", "V_lo"))
        qb_ready, qb_mm, SB_hi, SB_lo = sem("qb_ready"), sem("qb_mm"), sem("SB_hi"), sem("SB_lo")
        lnb_dve, lnb_pool = steps("lnb_dve"), steps("lnb_pool")
        A_z, A_t, A_f, A_hi, A_lo = steps("A_z"), steps("A_t"), steps("A_f", 2), steps("A_hi"), steps("A_lo")
        B_q, B_s, B_r, B_n, B_t, B_hi, B_lo = (steps("B_q"), steps("B_s", 6), steps("B_r"), steps("B_n"),
                                               steps("B_t"), steps("B_hi"), steps("B_lo"))
        C_s, C_m, C_e, C_r, C_p, C_t = (steps("C_s"), steps("C_m", 2), steps("C_e"), steps("C_r", 2),
                                        steps("C_p"), steps("C_t"))
        C_phi, C_plo, C_o, C_ohi, C_olo, C_w, C_x = (steps("C_phi"), steps("C_plo"), steps("C_o"),
                                                     steps("C_ohi"), steps("C_olo"), steps("C_w"), steps("C_x"))
        C_b = steps("C_b")
        q_dve, q_pe, q_act = steps("q_dve"), steps("q_pe"), steps("q_act")
        D_s, D_r, D_z, D_t, D_c, D_g = (steps("D_s", 3), steps("D_r"), steps("D_z", 9), steps("D_t"),
                                        steps("D_c"), steps("D_g"))
        D_a, D_h, D_1, D_2, D_u, D_v, D_y, D_x = (steps("D_a"), steps("D_h", 7), steps("D_1"), steps("D_2"),
                                                  steps("D_u"), steps("D_v"), steps("D_y"), steps("D_x"))
        EF = []
        for n in "EF":
            EF.append({k: steps(f"{n}_{k}", per) for k, per in
                       (("s", 3), ("r", 1), ("z", 1), ("t", 1), ("hi", 1), ("lo", 1), ("b", 1), ("m", 1), ("x", 1))})
        s_out = sem("s_out")

        f_row_hi, f_row, f_log = steps("f_row_hi"), steps("f_row"), steps("f_log")
        g_chain, g_pe, g_act = sem("g_chain"), sem("g_pe"), sem("g_act")
        routed = sem("routed")
        s_zero, s_scatter = sem("s_zero"), sem("s_scatter")
        x_hi, x_lo = steps("x_hi"), steps("x_lo")
        RUNS = {}
        for n in ("sa", "ex", "sb"):
            RUNS[n] = {k: steps(f"{n}_{k}") for k in ("g", "a", "h", "t", "hi", "lo", "y", "o")}
        x_t, x_c = steps("x_t"), steps("x_c")
        s_xg = [sem(f"s_xg{i}") for i in range(4)]
        s_ys = [sem(f"s_ys{i}") for i in range(2)]
        s_yg = [sem(f"s_yg{i}") for i in range(YR)]
        comb = steps("comb", 2)

        xrows = nc.dram_tensor("xrows", [NS * P, 2 * D], f16, kind="Internal").ap()
        yrows = nc.dram_tensor("yrows", [NS * P, D], fp32, kind="Internal").ap()

        block = es.enter_context(nc.Block())

        xt = x.rearrange("b (t p) d -> p (b t) d", p=P)
        ctx_v = ctx_in.rearrange("(t two) l d -> (two l) t d", t=CT)

        def chunks(w, n):
            return w.rearrange("(k p) n -> p k n", p=P)

        PIECES = [[(Wk, 0)], [(Wv, 0)], [(Wq, 0)], [(Wo, 0)],
                  [(w_gate, 0)], [(w_up, 0)], [(w_down, 0)], [(W_l1, 0), (Wr, 2 * D * KC)]]
        PIECE_DMAS = [len(p) for p in PIECES]

        staged0 = 16 * (sum(PIECE_DMAS[0::2]) + 3)

        def staged(n):
            return 16 * sum(PIECE_DMAS[m] for m in range(n % 2, n + 1, 2))

        VEC_DONE = 16 * (8 + B + 1)

        @block.sync
        def _(sp):
            sp.dma_start(cx[:], ctx_v).then_inc(s_ctx, 16)
            with nc.allow_non_contiguous_dma(reason="a few short vectors, features onto partitions"):
                for k, v in enumerate((tab_g, tab_b, vid_g, vid_b)):
                    sp.dma_start(vecs[:, k, :], v.rearrange("(c p) -> p c", p=P)).then_inc(s_vec, 16)
                for k, v in enumerate((q_g, q_b, k_g, k_b)):
                    sp.dma_start(hvec[:, k, :], v.rearrange("(c p) -> p c", p=P)).then_inc(s_vec, 16)
            for b in range(B):
                sp.dma_start(bias_l1[:, b, :], b_l1.rearrange("(o d) -> o d", o=1).to_broadcast([P, D])).then_inc(s_vec, 16)
            sp.dma_start(bo_b[:], bo.rearrange("(o d) -> o d", o=1).to_broadcast([P, D])).then_inc(s_vec, 16)
            for n, parts in enumerate(PIECES):
                if 2 <= n < 6:
                    sp.wait_ge(split_lo.sem, n - 1)
                elif n >= 6:
                    sp.wait_ge(q_dve.sem, 6 * (n - 5))
                for w, at in parts:
                    size = w.shape[0] // P * w.shape[1]
                    with nc.allow_non_contiguous_dma(reason="rows of the router's weights are short"):
                        sp.dma_start(stage[:, n % 2, at:at + size].rearrange("p (k n) -> p k n", n=w.shape[1]),
                                     chunks(w, 0)).then_inc(s_stage[n % 2], 16)
                if n == 1:
                    for g in range(4):
                        sp.dma_start(xs[:, g * NT // 4:(g + 1) * NT // 4, :],
                                     xt[:, g * NT // 4:(g + 1) * NT // 4, :]).then_inc(s_x, 16)
            def load_expert(slot, parts):
                for k, w in enumerate(parts):
                    sp.dma_start(stage[:, slot, k * KC * DE:(k + 1) * KC * DE].rearrange("p (k n) -> p k n", n=w.shape[1]),
                                 w.rearrange("(k p) n -> p k n", p=P)).then_inc(s_stage[slot], 16)
            sp.wait_ge(q_dve.sem, 18)
            load_expert(0, (Sg, Su, Sd))
            sp.wait_ge(q_dve.sem, 21)

            def load_nth(e, slot):
                load_expert(slot, [w[one(e)].rearrange("e h n -> (e h) n") for w in (Wg, Wu, Wd)])
            load_nth(0, 1)
            with sp.Fori(0, E // 2 - 1) as i:
                for k in range(2):
                    sp.wait_ge(x_lo.sem, 2 * i + k + 1)
                    load_nth(2 * i + k + 1, k)
            sp.wait_ge(x_lo.sem, E - 1)
            load_nth(E - 1, 0)

            def load_rows(t, b, m):
                if not isinstance(t, int) or t >= 4:
                    sp.wait_ge(x_t.sem, x_t.upto(t - 4))
                sp.dma_start(xg[:, m, :], xrows[bass.ds(t * P, P), :]).then_inc(s_xg[m], 16)

            def store_rows(t, b, m):
                sp.wait_ge(RUNS["ex"]["o"].sem, RUNS["ex"]["o"].upto(t))
                sp.dma_start(yrows[bass.ds(t * P, P), :], yb[:, m % 2, :]).then_inc(s_ys[m % 2], 16)
            sp.wait_ge(s_scatter, 16 * TOP * NT)
            skewed(sp, [(0, load_rows), (6, store_rows)], NS, 4)
            ot = out.rearrange("b (t p) d -> p (b t) d", p=P)

            def store_out(t, b, m):
                sp.wait_ge(comb.sem, comb.upto(t))
                sp.dma_start(ot[:, one(t), :], xs[:, one(t), :]).then_inc(s_out, 16)
            skewed(sp, [(0, store_out)], NT, 2)
            sp.wait_ge(s_out, 16 * NT)

        @block.gpsimd
        def _(pool):
            nc.gpsimd.memset(ident[:], 0.0).then_inc(s_fill, 1)
            nc.gpsimd.memset(ones[:], 1.0).then_inc(s_const, 1)
            nc.gpsimd.memset(ones64[:], 2.0 ** -6).then_inc(s_const, 1)
            nc.gpsimd.memset(nhalf[:], -0.5).then_inc(s_const, 1)
            nc.gpsimd.memset(zeros[:], 0.0).then_inc(s_fill2, 1)
            pool.wait_ge(s_fill, 1)
            nc.gpsimd.affine_select(out=ident[:], in_=ident[:], compare_op=ALU.not_equal, fill=1.0,
                                    base=0, pattern=[[-1, P]], channel_multiplier=1).then_inc(s_fill, 1)
            pool.wait_ge(s_fill, 2)
            nc.gpsimd.tensor_copy(ident16[:], ident[:]).then_inc(s_const, 1)
            nc.gpsimd.memset(Kbd[:].bitcast(fp32), 0.0).then_inc(s_const, 1)
            nc.gpsimd.memset(Vbd[:].bitcast(fp32), 0.0).then_inc(s_const, 1)
            nc.gpsimd.memset(qbm[:], 0.0).then_inc(s_const, 1)
            nc.gpsimd.memset(ones16[:], 1.0).then_inc(s_fill2, 1)
            nc.gpsimd.memset(before16[:], 1.0).then_inc(s_fill2, 1)
            pool.wait_ge(s_fill2, 3)
            nc.gpsimd.affine_select(out=before16[:], in_=before16[:], compare_op=ALU.is_ge, fill=0.0,
                                    base=-1, pattern=[[1, P]], channel_multiplier=-1).then_inc(s_fill2, 1)

            def rsqrt(dst, src):
                return nc.gpsimd.tensor_tensor(dst, src, nhalf[:, 0:src.shape[-1]], ALU.pow)

            pool.wait_ge(ctx_var, 1)
            rsqrt(small[:, 0, 2:4], small[:, 0, 0:2]).then_inc(ctx_rstd, 1)
            pool.wait_ge(lnb_dve.sem, 7)
            rsqrt(ln_all[:, 5, :], ln_all[:, 4, :]).then_inc(lnb_pool.sem, 1)
            pool.wait_ge(lnb_dve.sem, 10)
            rsqrt(ln_all[:, 7, :], ln_all[:, 6, :]).then_inc(lnb_pool.sem, 1)
            for c in range(CT):
                pool.wait_ge(k_var, c + 1)
                rsqrt(small[:, c, 5:6], small[:, c, 4:5]).then_inc(k_rstd, 1)

            def b_r(t, b, m):
                pool.wait_ge(B_s.sem, B_s.upto(t, 4))
                rsqrt(small[:, m, 1:2], small[:, m, 0:1]).then_inc(B_r.sem, 1)
            skewed(pool, [(0, b_r)], NT, 2)

            def c_p(t, b, m):
                k = m % 2
                pool.wait_ge(C_r.sem, C_r.upto(t))
                nc.gpsimd.tensor_tensor(sm[:, k, :].rearrange("p (h j) -> p h j", j=DH),
                                        sm[:, k, :].rearrange("p (h j) -> p h j", j=DH),
                                        red[:, k, 1, :].unsqueeze(2).to_broadcast([P, H, DH]),
                                        ALU.mult).then_inc(C_p.sem, 1)
                nc.gpsimd.tensor_tensor(xs[:, one(t), :], xs[:, one(t), :], bo_b[:].unsqueeze(1),
                                        ALU.add).then_inc(C_b.sem, 1)
            skewed(pool, [(1, c_p)], NT, 4)

            def d_r(t, b, m):
                pool.wait_ge(D_s.sem, D_s.upto(t))
                rsqrt(small[:, m, 1:2], small[:, m, 0:1]).then_inc(D_r.sem, 1)
            skewed(pool, [(0, d_r)], NT, 2)
            for S in EF:
                def ef_r(t, b, m):
                    pool.wait_ge(S["s"].sem, S["s"].upto(t))
                    rsqrt(small[:, m % 2, 1:2], small[:, m % 2, 0:1]).then_inc(S["r"].sem, 1)

                def e_b(t, b, m):
                    wait_apart(pool, S["z"].sem, S["z"].upto(t))
                    nc.gpsimd.tensor_tensor(xs[:, one(t), :], xs[:, one(t), :], bias_l1[:, one(b), :],
                                            ALU.add).then_inc(S["b"].sem, 1)

                def f_r(t, b, m):
                    k = m % 2
                    wait_apart(pool, S["z"].sem, S["z"].upto(t))
                    nc.gpsimd.tensor_copy(zrow[:, one(t), 0:D], z[:, k, :].unsqueeze(1)).then_inc(f_row_hi.sem, 1)
                    wait_apart(pool, f_row_hi.sem, f_row_hi.upto(t))
                    nc.gpsimd.tensor_tensor(zrow[:, one(t), D:2 * D], z[:, k, :].unsqueeze(1), zrow[:, one(t), 0:D],
                                            ALU.subtract).then_inc(f_row.sem, 1)
                if S is EF[0]:
                    skewed(pool, [(1, e_b), (0, ef_r)], NT, 4)
                    pool.wait_ge(S["x"].sem, NT)
                    nc.gpsimd.iota(w8i[:], pattern=[[-1, E]], base=E, channel_multiplier=0).then_inc(s_late, 1)
                    nc.gpsimd.iota(tile_e[:], pattern=[[1, NS]], base=0, channel_multiplier=0).then_inc(s_late, 1)
                    pool.wait_ge(s_late, 2)
                    nc.gpsimd.tensor_copy(w8[:], w8i[:]).then_inc(s_late, 1)
                    nc.gpsimd.tensor_copy(tile_no[:], tile_e[:]).then_inc(s_late, 1)
                else:
                    skewed(pool, [(1, f_r), (0, ef_r)], NT, 4)

            pool.wait_ge(f_row.sem, NT)
            pool.wait_ge(routed, 3)
            pool.wait_ge(s_zero, 16)
            for t in range(NT):
                for k in range(TOP):
                    nc.gpsimd.indirect_dma_start(xrows, bass.IndirectOffsetOnAxis(idx[:, k, t:t + 1], 0),
                                                 zrow[:, t, :], None).then_inc(s_scatter, 16)
            for i in range(2):
                pool.wait_ge(s_ys[i], 16 * ((NS + 1 - i) // 2))
            pool.wait_ge(x_lo.sem, E + 1)
            for t in range(NT):
                if t >= YR:
                    pool.wait_ge(comb.sem, comb.upto(t - YR))
                for k in range(TOP):
                    nc.gpsimd.indirect_dma_start(yg[:, t % YR, k, :], None, yrows,
                                                 bass.IndirectOffsetOnAxis(idx[:, k, t:t + 1], 0)).then_inc(s_yg[t % YR], 16)

        @block.vector
        def _(dve):
            v = nc.vector
            n = [0]

            def chain(ins):
                n[0] += 1
                ins.then_inc(d_chain, 1)
                dve.wait_ge(d_chain, n[0])

            dve.wait_ge(s_ctx, 16)
            for c in range(CT):
                chain(v.bn_stats(st[:, c, 0:6], cx[:, c, :]))
                chain(v.bn_aggr(mv[:, c, :], st[:, c, 0:6]))
            v.tensor_scalar(small[:, 0, 0:2], mv[:, :, 1], EPS, None, ALU.add).then_inc(ctx_var, 1)
            dve.wait_ge(ctx_rstd, 1)
            for c in range(CT):
                v.tensor_scalar(z[:, c, :], cx[:, c, :], mv[:, c, 0:1], small[:, 0, 2 + c:3 + c],
                                ALU.subtract, ALU.mult).then_inc(ctx_z, 1)
            dve.wait_ge(ctx_t, 1)
            v.tensor_reduce(csum[:], banks(1).rearrange("p (k b l) -> p k b l", k=KC, l=LC), X,
                            ALU.add).then_inc(ctx_sum, 1)
            for i in range(2):
                dve.wait_ge(split_hi.sem, i + 1)
                w = (wk, wv)[i]
                v.scalar_tensor_tensor(w[:, LO, :], stage[:, i, 0:KC * INNER], WS, w[:, HI, :],
                                       ALU.mult, ALU.subtract).then_inc(split_lo.sem, 1)
            dve.wait_ge(cT_hi, 3)
            v.tensor_tensor(cTk[:, LO, :, :], cf[:], cTk[:, HI, :, :], ALU.subtract).then_inc(cT_lo, 1)
            for k in range(2):
                v.tensor_tensor(cT[:, LO, :, :, k * LC:(k + 1) * LC],
                                cf[:].rearrange("p k (b l) -> p k b l", l=LC),
                                cT[:, HI, :, :, k * LC:(k + 1) * LC], ALU.subtract).then_inc(cT_lo, 1)

            ln = 0

            def link(ins):
                nonlocal ln
                ln += 1
                ins.then_inc(lnb_dve.sem, 1)
                dve.wait_ge(lnb_dve.sem, ln)
            dve.wait_ge(s_x, 64)
            with dve.Fori(0, NT - 1) as t:
                v.bn_stats(st_all[:, one(t), :], xs[:, one(t), :])
            v.bn_stats(st_all[:, NT - 1, :], xs[:, NT - 1, :]).then_inc(lnb_dve.sem, 1)
            ln += 1
            dve.wait_ge(lnb_dve.sem, 1)
            link(v.tensor_tensor(ln_all[:, 0, :], st_all[:, :, 1], st_all[:, :, 4], ALU.add))
            link(v.tensor_tensor(ln_all[:, 1, :], st_all[:, :, 1], st_all[:, :, 4], ALU.subtract))
            link(v.tensor_tensor(ln_all[:, 2, :], st_all[:, :, 2], st_all[:, :, 5], ALU.add))
            link(v.scalar_tensor_tensor(ln_all[:, 3, :], ln_all[:, 1, :], 0.25, ln_all[:, 1, :], ALU.mult, ALU.mult))
            link(v.scalar_tensor_tensor(ln_all[:, 8, :], ln_all[:, 2, :], 1.0 / D, ln_all[:, 3, :], ALU.mult, ALU.add))
            link(v.tensor_scalar(ln_all[:, 4, :], ln_all[:, 8, :], EPS, None, ALU.add))
            dve.wait_ge(lnb_pool.sem, 1)
            link(v.tensor_tensor(ln_all[:, 9, :], ln_all[:, 8, :], ln_all[:, 5, :], ALU.mult))
            link(v.tensor_tensor(ln_all[:, 9, :], ln_all[:, 9, :], ln_all[:, 5, :], ALU.mult))
            link(v.tensor_scalar(ln_all[:, 6, :], ln_all[:, 9, :], EPS, None, ALU.add))
            link(v.tensor_scalar(ln_all[:, 0, :], ln_all[:, 0, :], 0.5, None, ALU.mult))
            dve.wait_ge(lnb_pool.sem, 2)
            link(v.tensor_tensor(ln_all[:, 9, :], ln_all[:, 5, :], ln_all[:, 7, :], ALU.mult))

            def a_lo(t, b, m):
                dve.wait_ge(A_hi.sem, A_hi.upto(t))
                v.tensor_tensor(zT[:, LO, :, tile_cols(t)], zf[:, m, :].rearrange("p (k n) -> p k n", k=KC),
                                zT[:, HI, :, tile_cols(t)], ALU.subtract).then_inc(A_lo.sem, 1)

            def a_z(t, b, m):
                if not isinstance(t, int) or t >= 2:
                    dve.wait_ge(A_t.sem, A_t.upto(t - 2))
                v.tensor_scalar(z[:, m, :], xs[:, one(t), :], ln_all[:, 0, one(t)], ln_all[:, 9, one(t)],
                                ALU.subtract, ALU.mult).then_inc(A_z.sem, 1)
            skewed(dve, [(1, a_lo), (0, a_z)], NT, 2)

            dve.wait_ge(s_vec, VEC_DONE)
            dve.wait_ge(s_const, 7)
            for k in range(2):
                h = slice(k * DH, (k + 1) * DH)
                v.tensor_copy(qbm[h, :, k, :],
                              hvec[h, 1, :].unsqueeze(2).to_broadcast([DH, QC, P])).then_inc(qb_ready, 1)
            for c in range(CT):
                dve.wait_ge(k_mm, c + 1)
                chain(v.bn_stats(st[:, c, 0:6], banks(2 * c)))
                chain(v.bn_stats(st[:, c, 6:12], banks(2 * c, 2)[:, BANK:INNER]))
                chain(v.bn_aggr(mv[:, c, :], st[:, c, :]))
                v.tensor_scalar(small[:, c, 4:5], mv[:, c, 1:2], WS ** -2, EPS, ALU.mult,
                                ALU.add).then_inc(k_var, 1)
                dve.wait_ge(k_rstd, c + 1)
                chain(v.tensor_scalar(small[:, c, 6:7], small[:, c, 5:6], 1.0 / WS, None, ALU.mult))
                v.scalar_tensor_tensor(small[:, c, 7:8], mv[:, c, 0:1], -1.0, small[:, c, 6:7], ALU.mult,
                                       ALU.mult).then_inc(k_bias, 1)
            for c in range(CT):
                dve.wait_ge(k_t, c + 1)
                T = banks(4 + 2 * c, 2)[:, 0:INNER].rearrange("p (q n) -> p q n", n=P)
                for q in range(QC - 1):
                    v.tensor_scalar(kf[:, q, c * P:(c + 1) * P], T[:, q, :], hvec[:, 2, q:q + 1],
                                    hvec[:, 3, q:q + 1], ALU.mult, ALU.add)
                chain(v.tensor_scalar(kf[:, QC - 1, c * P:(c + 1) * P], T[:, QC - 1, :], hvec[:, 2, QC - 1:QC],
                                      hvec[:, 3, QC - 1:QC], ALU.mult, ALU.add))
            for q in range(QC):
                v.tensor_scalar(kq[:, q, :], kf[:, q, :], hvec[:, 0, q:q + 1], None, ALU.mult).then_inc(kq_ready, 1)
            dve.wait_ge(K_hi, 2)
            for k in range(2):
                h = slice(k * DH, (k + 1) * DH)
                v.tensor_tensor(Kbd[h, LO, :, :, k * DH:(k + 1) * DH],
                                kq[h, :, :].rearrange("p q (b l) -> p b q l", l=LC),
                                Kbd[h, HI, :, :, k * DH:(k + 1) * DH], ALU.subtract).then_inc(K_lo, 1)
            for b in range(B):
                dve.wait_ge(V_hi, 2 * (b + 1))
                for k in range(2):
                    h = slice(k * DH, (k + 1) * DH)
                    src = banks(2 * (b % 2), 2)[h, 0:INNER].rearrange("p (q n) -> p q n", n=P)[:, :, k * DH:(k + 1) * DH]
                    v.scalar_tensor_tensor(Vbd[h, LO, b, :, k * DH:(k + 1) * DH], src, 1.0 / WS,
                                           Vbd[h, HI, b, :, k * DH:(k + 1) * DH], ALU.mult,
                                           ALU.subtract).then_inc(V_lo, 1)
            for r in range(2):
                dve.wait_ge(SB_hi, 2 * (r + 1))
                heads = slice(r * H // 2 * DH, (r + 1) * H // 2 * DH)
                src = banks(4 * r, 3)[DH:P, :].rearrange("p (h b l) -> p b h l", b=B, l=LC)
                for b in range(B):
                    v.tensor_tensor(SB[DH:P, b, heads].rearrange("p (h l) -> p h l", l=LC), src[:, b],
                                    bhi[DH:P, b, heads].rearrange("p (h l) -> p h l", l=LC),
                                    ALU.subtract).then_inc(SB_lo, 1)

            for i in range(2, 4):
                dve.wait_ge(split_hi.sem, i + 1)
                w = (wq, wo)[i - 2]
                v.scalar_tensor_tensor(w[:, LO, :], stage[:, i % 2, 0:KC * INNER], WS, w[:, HI, :],
                                       ALU.mult, ALU.subtract).then_inc(split_lo.sem, 1)

            def b_s(t, b, m):
                dve.wait_ge(B_q.sem, B_q.upto(t))
                q = banks(2 * m, 2)
                v.bn_stats(st[:, m, 0:6], q[:, 0:BANK]).then_inc(B_s.sem, 1)
                v.bn_stats(st[:, m, 6:12], q[:, BANK:INNER]).then_inc(B_s.sem, 1)
                wait_apart(dve, B_s.sem, B_s.upto(t, 2))
                v.bn_aggr(mv[:, m, :], st[:, m, :]).then_inc(B_s.sem, 1)
                dve.wait_ge(B_s.sem, B_s.upto(t, 3))
                v.tensor_scalar(small[:, m, 0:1], mv[:, m, 1:2], WS ** -2, EPS, ALU.mult, ALU.add).then_inc(B_s.sem, 1)

            def b_s2(t, b, m):
                dve.wait_ge(B_r.sem, B_r.upto(t))
                v.tensor_scalar(small[:, m, 2:3], small[:, m, 1:2], 1.0 / WS, None, ALU.mult).then_inc(B_s.sem, 1)
                dve.wait_ge(B_s.sem, B_s.upto(t, 5))
                v.scalar_tensor_tensor(small[:, m, 3:4], mv[:, m, 0:1], -1.0, small[:, m, 2:3],
                                       ALU.mult, ALU.mult).then_inc(B_s.sem, 1)

            def b_lo(t, b, m):
                dve.wait_ge(B_hi.sem, B_hi.upto(t))
                v.tensor_tensor(qT[:, LO, :, tile_cols(t)],
                                banks(4 + 2 * m, 2)[:, 0:INNER].rearrange("p (q n) -> p q n", n=P),
                                qT[:, HI, :, tile_cols(t)], ALU.subtract).then_inc(B_lo.sem, 1)
            skewed(dve, [(0, b_s), (1, b_lo), (0, b_s2)], NT, 2)

            nq_ = [0]

            def qtick(ins, wait=True):
                ins.then_inc(q_dve.sem, 1)
                nq_[0] += 1
                if wait:
                    dve.wait_ge(q_dve.sem, nq_[0])
            for i in range(3):
                src = stage[:, i % 2, 0:FI * D // P]
                dve.wait_ge(s_stage[i % 2], staged(4 + i))
                qtick(v.tensor_reduce(wsc[:, i:i + 1], src, X, ALU.add, apply_absolute_value=True))
                dve.wait_ge(q_pe.sem, 1 + 2 * i)
                qtick(v.tensor_scalar(wsc[:, 4 + i:5 + i], banks(0)[:, 0:1], 1.0 / (FI * D), 1e-5, ALU.mult, ALU.max))
                qtick(v.reciprocal(wsc[:, 8 + i:9 + i], wsc[:, 4 + i:5 + i]))
                qtick(v.tensor_scalar(src, src, wsc[:, 8 + i:9 + i], MAGIC, ALU.mult, ALU.add))
                qtick(v.tensor_scalar(src, src, MAGIC + 1.0, MAGIC - 1.0, ALU.min, ALU.max))
                w16 = wtern[:, i % 2, :]
                if i == 2:
                    dve.wait_ge(q_pe.sem, 2)
                qtick(v.tensor_scalar(w16, src, MAGIC, None, ALU.subtract), wait=False)
            qtick(v.tensor_scalar(wsc[:, 4:7], wsc[:, 4:7], 1.0 / 127.0, None, ALU.mult))
            dve.wait_ge(q_act.sem, 5)
            T = banks(1, 2).rearrange("p (k e) -> p k e", e=D)
            qtick(v.scalar_tensor_tensor(wl1[:, LO, :, :], T, WS, wl1[:, HI, :, :], ALU.mult, ALU.subtract))
            qtick(v.scalar_tensor_tensor(wr[:, LO, :, :], stage[:, 1, 2 * D * KC:2 * D * KC + KC * 8].rearrange(
                "p (k e) -> p k e", k=KC), WS, wr[:, HI, :, :], ALU.mult, ALU.subtract))
            for b in range(B):
                for k in range(KC):
                    qtick(v.tensor_scalar(csum_rep[:, HI, k, :], ones[:], csum[:, k, b:b + 1], 1.0 / LC, ALU.mult, ALU.mult))
                    qtick(v.tensor_scalar(xrep[:, k, :], ones[:], csum[:, k, b:b + 1], 1.0 / LC, ALU.mult, ALU.mult))
                qtick(v.tensor_tensor(csum_rep[:, LO, :, :], xrep[:], csum_rep[:, HI, :, :], ALU.subtract))
                dve.wait_ge(q_pe.sem, 8 + b)
                qtick(v.scalar_tensor_tensor(bias_l1[:, b, :], banks(3)[:, 0:D], 1.0 / WS, bias_l1[:, b, :], ALU.mult, ALU.add))

            def c_r(t, b, m):
                k = m % 2
                dve.wait_ge(C_e.sem, C_e.upto(t))
                v.tensor_reduce(red[:, k, 0, :], sm[:, k, :].rearrange("p (h j) -> p h j", j=DH), X,
                                ALU.add).then_inc(C_r.sem, 1)
                dve.wait_ge(C_r.sem, C_r.upto(t, 1))
                v.reciprocal(red[:, k, 1, :], red[:, k, 0, :]).then_inc(C_r.sem, 1)

            def c_x(t, b, m):
                dve.wait_ge(C_b.sem, C_b.upto(t))
                dve.wait_ge(C_w.sem, C_w.upto(t))
                v.scalar_tensor_tensor(xs[:, one(t), :], banks(6)[:, 0:D].unsqueeze(1), 1.0 / WS, xs[:, one(t), :],
                                       ALU.mult, ALU.add).then_inc(C_x.sem, 1)

            def c_olo(t, b, m):
                dve.wait_ge(C_ohi.sem, C_ohi.upto(t))
                v.tensor_tensor(oT[:, LO, :], banks(4, 2)[:, 0:INNER], oT[:, HI, :], ALU.subtract).then_inc(C_olo.sem, 1)

            def c_plo(t, b, m):
                dve.wait_ge(C_phi.sem, C_phi.upto(t))
                v.tensor_tensor(pT[:, LO, :], banks(2, 2)[:, 0:INNER], pT[:, HI, :], ALU.subtract).then_inc(C_plo.sem, 1)

            def c_m(t, b, m):
                k = m % 2
                dve.wait_ge(C_s.sem, C_s.upto(t))
                S = banks(0, 2)[:, 0:INNER].rearrange("p (h j) -> p h j", j=DH)
                v.tensor_reduce(red[:, k, 0, :], S, X, ALU.max).then_inc(C_m.sem, 1)
                dve.wait_ge(C_m.sem, C_m.upto(t, 1))
                v.tensor_tensor(sm[:, k, :].rearrange("p (h j) -> p h j", j=DH), S,
                                red[:, k, 0, :].unsqueeze(2).to_broadcast([P, H, DH]),
                                ALU.subtract).then_inc(C_m.sem, 1)
            skewed(dve, [(1, c_r), (3, c_x), (2, c_olo), (1, c_plo), (0, c_m)], NT, 4)

            def d_x(t, b, m):
                dve.wait_ge(D_y.sem, D_y.upto(t))
                v.scalar_tensor_tensor(xs[:, one(t), :], banks(6)[:, 0:D].unsqueeze(1), sc1[:, m, 4:5], xs[:, one(t), :],
                                       ALU.mult, ALU.add).then_inc(D_x.sem, 1)

            def d_q(t, b, m):
                dve.wait_ge(D_1.sem, D_1.upto(t))
                if not isinstance(t, int) or t >= 1:
                    dve.wait_ge(D_u.sem, D_u.upto(t - 1))
                v.tensor_scalar(hq[:], hh[:, m, :], MAGIC + 127.0, MAGIC, ALU.min, ALU.subtract).then_inc(D_2.sem, 1)

            def d_h(t, b, m):
                s = sc1[:, m, :]
                dve.wait_ge(D_a.sem, D_a.upto(t))
                v.tensor_tensor(hh[:, m, :], banks(2, 2), hg[:], ALU.mult).then_inc(D_h.sem, 1)
                dve.wait_ge(D_h.sem, D_h.upto(t, 1))
                v.tensor_reduce(s[:, 0:1], hh[:, m, :], X, ALU.max, apply_absolute_value=True).then_inc(D_h.sem, 1)
                dve.wait_ge(D_h.sem, D_h.upto(t, 2))
                v.tensor_scalar(s[:, 1:2], s[:, 0:1], sc0[:, m, 5:6], 1e-5, ALU.mult, ALU.max).then_inc(D_h.sem, 1)
                dve.wait_ge(D_h.sem, D_h.upto(t, 3))
                v.reciprocal(s[:, 2:3], s[:, 1:2]).then_inc(D_h.sem, 1)
                v.tensor_scalar(s[:, 4:5], s[:, 1:2], wsc[:, 6:7], None, ALU.mult).then_inc(D_h.sem, 1)
                dve.wait_ge(D_h.sem, D_h.upto(t, 5))
                v.tensor_scalar(s[:, 5:6], s[:, 2:3], 127.0, None, ALU.mult).then_inc(D_h.sem, 1)
                dve.wait_ge(D_h.sem, D_h.upto(t, 6))
                v.tensor_scalar(s[:, 3:4], s[:, 5:6], sc0[:, m, 5:6], None, ALU.mult).then_inc(D_h.sem, 1)

            def d_z(t, b, m):
                s = sc0[:, m, :]
                k = 0

                def go(ins, wait=True):
                    nonlocal k
                    k += 1
                    ins.then_inc(D_z.sem, 1)
                    if wait:
                        dve.wait_ge(D_z.sem, D_z.upto(t, k))
                dve.wait_ge(D_r.sem, D_r.upto(t))
                go(v.tensor_scalar(xc[:, m, :], xs[:, one(t), :].rearrange("p o d -> p (o d)"), mv[:, m, 0:1],
                                   small[:, m, 1:2], ALU.subtract, ALU.mult))
                go(v.tensor_reduce(s[:, 0:1], xc[:, m, :], X, ALU.max, apply_absolute_value=True))
                go(v.tensor_scalar(s[:, 1:2], s[:, 0:1], 1e-5, None, ALU.max))
                go(v.reciprocal(s[:, 2:3], s[:, 1:2]), wait=False)
                go(v.tensor_scalar(s[:, 4:5], s[:, 1:2], wsc[:, 4:5], None, ALU.mult), wait=False)
                go(v.tensor_scalar(s[:, 5:6], s[:, 1:2], wsc[:, 5:6], None, ALU.mult))
                go(v.tensor_scalar(s[:, 3:4], s[:, 2:3], 127.0, None, ALU.mult))
                go(v.tensor_scalar(xc[:, m, :], xc[:, m, :], s[:, 3:4], MAGIC, ALU.mult, ALU.add))
                if not isinstance(t, int) or t >= 2:
                    dve.wait_ge(D_t.sem, D_t.upto(t - 2))
                go(v.tensor_scalar(zq[:, m, :], xc[:, m, :], MAGIC + 127.0, MAGIC, ALU.min, ALU.subtract), wait=False)
                assert k == D_z.per

            def layer_stats(S):
                def stats(t, b, m):
                    k = m % 2
                    v.bn_stats(st[:, k, 0:6], xs[:, one(t), :]).then_inc(S.sem, 1)
                    wait_apart(dve, S.sem, S.upto(t, 1))
                    v.bn_aggr(mv[:, k, :], st[:, k, 0:6]).then_inc(S.sem, 1)
                    dve.wait_ge(S.sem, S.upto(t, 2))
                    v.tensor_scalar(small[:, k, 0:1], mv[:, k, 1:2], EPS, None, ALU.add).then_inc(S.sem, 1)
                return stats
            dve.wait_ge(C_x.sem, NT)
            skewed(dve, [(4, d_x), (3, d_q), (2, d_h), (1, d_z), (0, layer_stats(D_s))], NT, 2)

            def split_expert(e, slot):
                dve.wait_ge(x_hi.sem, x_hi.upto(e))
                v.scalar_tensor_tensor(wexp[:, one(e), LO, :], stage[:, slot, :].unsqueeze(1), WS, wexp[:, one(e), HI, :],
                                       ALU.mult, ALU.subtract).then_inc(x_lo.sem, 1)

            for S in EF:
                def ef_x(t, b, m):
                    dve.wait_ge(S["b"].sem, S["b"].upto(t))
                    dve.wait_ge(S["m"].sem, S["m"].upto(t))
                    v.scalar_tensor_tensor(xs[:, one(t), :], banks(2 + m % 2)[:, 0:D].unsqueeze(1), 1.0 / WS, xs[:, one(t), :],
                                           ALU.mult, ALU.add).then_inc(S["x"].sem, 1)

                def ef_lo(t, b, m):
                    dve.wait_ge(S["hi"].sem, S["hi"].upto(t))
                    v.tensor_tensor(zT[:, LO, :, tile_cols(t)], banks(m % 2)[:, 0:D].rearrange("p (k n) -> p k n", k=KC),
                                    zT[:, HI, :, tile_cols(t)], ALU.subtract).then_inc(S["lo"].sem, 1)

                def ef_z(t, b, m):
                    k = m % 2
                    if not isinstance(t, int) or t >= 2:
                        dve.wait_ge(S["t"].sem, S["t"].upto(t - 2))
                    dve.wait_ge(S["r"].sem, S["r"].upto(t))
                    v.tensor_scalar(z[:, k, :], xs[:, one(t), :].rearrange("p o d -> p (o d)"), mv[:, k, 0:1],
                                    small[:, k, 1:2], ALU.subtract, ALU.mult).then_inc(S["z"].sem, 1)

                def f_l(t, b, m):
                    dve.wait_ge(S["m"].sem, S["m"].upto(t))
                    v.tensor_scalar(logits[:, one(t), :], banks(2 + m % 2)[:, 0:E].unsqueeze(1), 1.0 / WS, None,
                                    ALU.mult).then_inc(f_log.sem, 1)
                if S is EF[0]:
                    dve.wait_ge(D_x.sem, NT)
                    skewed(dve, [(3, ef_x), (2, ef_lo), (1, ef_z), (0, layer_stats(S["s"]))], NT, 4)
                    dve.wait_ge(S["x"].sem, NT)
                    split_expert(0, 0)
                else:
                    def ef_z2(t, b, m):
                        if not isinstance(t, int) or t >= 2:
                            dve.wait_ge(f_row.sem, f_row.upto(t - 2))
                        ef_z(t, b, m)
                    skewed(dve, [(3, f_l), (2, ef_lo), (1, ef_z2), (0, layer_stats(S["s"]))], NT, 4)

            gn = [0]

            def g(ins):
                gn[0] += 1
                ins.then_inc(g_chain, 1)
                dve.wait_ge(g_chain, gn[0])

            def over_e(a):
                return a.unsqueeze(2).to_broadcast([P, NT, E])

            def over_t(a):
                return a.unsqueeze(1).to_broadcast([P, NT, E])
            sh, eq, oh1, oh2, sl = (r3[:, k] for k in range(5))
            m1, b1, m2, b2, zs, e2, rz, p2, w1, w2, sl1, sl2 = (r2[:, k] for k in range(12))
            dve.wait_ge(f_log.sem, NT)
            dve.wait_ge(s_late, 4)
            g(v.tensor_reduce(m1, logits[:], X, ALU.max))
            g(v.tensor_tensor(sh, logits[:], over_e(m1), ALU.subtract))
            g(v.tensor_scalar(eq, sh, 0.0, None, ALU.is_equal))
            g(v.tensor_tensor(eq, eq, over_t(w8[:]), ALU.mult))
            g(v.tensor_reduce(b1, eq, X, ALU.max))
            g(v.tensor_tensor(oh1, over_t(w8[:]), over_e(b1), ALU.is_equal))
            g(v.scalar_tensor_tensor(sl, oh1, -1e30, sh, ALU.mult, ALU.add))
            g(v.tensor_reduce(m2, sl, X, ALU.max))
            g(v.tensor_tensor(eq, sl, over_e(m2), ALU.is_equal))
            g(v.tensor_tensor(eq, eq, over_t(w8[:]), ALU.mult))
            g(v.tensor_reduce(b2, eq, X, ALU.max))
            g(v.tensor_tensor(oh2, over_t(w8[:]), over_e(b2), ALU.is_equal))
            g(v.tensor_tensor(A16[:], oh1, oh2, ALU.add))
            n8, t8, i8, s8, o8 = (r1[:, k] for k in range(5))
            dve.wait_ge(g_pe, 1)
            g(v.tensor_scalar(n8, banks(5)[:, 0:E], 1.0 / P, (P - 1.0) / P - 0.5 + 0.5 / P, ALU.mult, ALU.add))
            g(v.tensor_scalar(n8, n8, MAGIC, None, ALU.add))
            g(v.tensor_scalar(t8, n8, MAGIC, None, ALU.subtract))
            g(v.tensor_tensor_scan(i8, ones[:, 0:E], t8, 0.0, ALU.mult, ALU.add))
            g(v.tensor_tensor(s8, i8, t8, ALU.subtract))
            g(v.tensor_scalar(o8, s8, float(P), None, ALU.mult))
            g(v.tensor_tensor(sl, banks(4)[:, 0:NT * E].rearrange("p (t e) -> p t e", e=E), over_t(o8), ALU.add))
            g(v.tensor_tensor(oh1, oh1, sl, ALU.mult))
            g(v.tensor_tensor(oh2, oh2, sl, ALU.mult))
            g(v.tensor_reduce(sl1, oh1, X, ALU.add))
            g(v.tensor_reduce(sl2, oh2, X, ALU.add))
            v.tensor_copy(idx[:, 0, :], sl1).then_inc(routed, 1)
            v.tensor_copy(idx[:, 1, :], sl2).then_inc(routed, 1)
            g(v.tensor_tensor(tcmp[:], tile_no[:].unsqueeze(2).to_broadcast([P, NS, E - 1]),
                              s8[:, 1:E].unsqueeze(1).to_broadcast([P, NS, E - 1]), ALU.is_ge))
            g(v.tensor_reduce(tsum[:], tcmp[:], X, ALU.add))
            v.tensor_copy(tile_e[:], tsum[:]).then_inc(routed, 1)
            dve.wait_ge(g_act, 2)
            g(v.tensor_reduce(zs, r3[:, 1], X, ALU.add))
            g(v.reciprocal(rz, zs))
            g(v.tensor_tensor(p2, e2, rz, ALU.mult))
            g(v.tensor_tensor(zs, rz, p2, ALU.add))
            g(v.tensor_scalar(zs, zs, 1e-20, None, ALU.add))
            g(v.reciprocal(zs, zs))
            g(v.tensor_tensor(w1, rz, zs, ALU.mult))
            g(v.tensor_tensor(w2, p2, zs, ALU.mult))

            def run(R, count, first_tile, experts):
                d = 1 if experts else 0

                def out_(t, b, m):
                    k = m % 2
                    dve.wait_ge(R["y"].sem, R["y"].upto(t))
                    if experts:
                        if not isinstance(t, int) or t >= 2:
                            dve.wait_ge(s_ys[k], 16 * ((t - k) // 2) if isinstance(t, int) else 16 * (2 * b + (m - k) // 2))
                        v.tensor_scalar(yb[:, k, :], banks(6)[:, 0:D], 1.0 / WS, None, ALU.mult).then_inc(R["o"].sem, 1)
                    else:
                        at = t + first_tile
                        v.scalar_tensor_tensor(xs[:, one(at), :], banks(6)[:, 0:D].unsqueeze(1), 1.0 / WS,
                                               xs[:, one(at), :], ALU.mult, ALU.add).then_inc(R["o"].sem, 1)

                def lo(t, b, m):
                    k = m % 2
                    dve.wait_ge(R["hi"].sem, R["hi"].upto(t))
                    v.tensor_tensor(ehT[:, k, LO, :], banks(4 + k), ehT[:, k, HI, :], ALU.subtract).then_inc(R["lo"].sem, 1)

                def h(t, b, m):
                    k = m % 2
                    dve.wait_ge(R["a"].sem, R["a"].upto(t))
                    v.scalar_tensor_tensor(eh[:, k, :], banks(2 + k), 1.0 / WS, eg[:, k, :], ALU.mult,
                                           ALU.mult).then_inc(R["h"].sem, 1)

                def copy_x(t, b, m):
                    dve.wait_ge(x_t.sem, x_t.upto(t))
                    v.tensor_copy(xgT[:, m % 2, :], banks(7).bitcast(f16)[:, 0:2 * D]).then_inc(x_c.sem, 1)

                def split(t, b, m):
                    split_expert(1 + t, (1 + m) % 2)
                stages = [(2 + d, out_), (1 + d, lo), (d, h)]
                if experts:
                    stages.append((0, copy_x))
                elif not first_tile:
                    stages.append((0, split))
                skewed(dve, stages, count, 4)
            run(RUNS["sa"], NT // 2, 0, False)
            run(RUNS["ex"], NS, 0, True)
            run(RUNS["sb"], NT // 2, NT // 2, False)

            def comb_(t, b, m):
                dve.wait_ge(s_yg[m], 32 * (b + 1))
                v.scalar_tensor_tensor(xs[:, one(t), :], yg[:, m, 0, :].unsqueeze(1), r2[:, 8, one(t)], xs[:, one(t), :],
                                       ALU.mult, ALU.add).then_inc(comb.sem, 1)
                dve.wait_ge(comb.sem, comb.upto(t, 1))
                v.scalar_tensor_tensor(xs[:, one(t), :], yg[:, m, 1, :].unsqueeze(1), r2[:, 9, one(t)], xs[:, one(t), :],
                                       ALU.mult, ALU.add).then_inc(comb.sem, 1)
            dve.wait_ge(RUNS["sa"]["o"].sem, NT // 2)
            dve.wait_ge(RUNS["sb"]["o"].sem, NT // 2)
            skewed(dve, [(0, comb_)], NT, YR)

        @block.scalar
        def _(act):
            act.wait_ge(s_fill2, 1)
            act.dma_start(xrows.rearrange("(i p) d -> p i d", p=P),
                          zeros[:].unsqueeze(1).to_broadcast([P, NS, 2 * D])).then_inc(s_zero, 16)

            def copy(dst, src, scale=1.0):
                return nc.scalar.activation(dst, src, ACT.Copy, scale=scale)

            act.wait_ge(s_vec, VEC_DONE)
            act.wait_ge(ctx_t, 1)
            for k in range(KC):
                nc.scalar.activation(cf[:, k, :], banks(0)[:, k * CT * P:(k + 1) * CT * P], ACT.Identity,
                                     bias=vecs[:, 1, k:k + 1], scale=vecs[:, 0, k:k + 1]).then_inc(cf_ready, 1)
            act.wait_ge(cf_ready, 2)
            copy(cTk[:, HI, :, :], cf[:]).then_inc(cT_hi, 1)
            for k in range(2):
                copy(cT[:, HI, :, :, k * LC:(k + 1) * LC],
                     cf[:].rearrange("p k (b l) -> p k b l", l=LC)).then_inc(cT_hi, 1)
            for i in range(2):
                act.wait_ge(s_stage[i], staged(i))
                copy((wk, wv)[i][:, HI, :], stage[:, i, 0:KC * INNER], WS).then_inc(split_hi.sem, 1)

            def a_f(t, b, m):
                act.wait_ge(A_t.sem, A_t.upto(t))
                if not isinstance(t, int) or t >= 2:
                    act.wait_ge(A_lo.sem, A_lo.upto(t - 2))
                for k in range(KC):
                    nc.scalar.activation(zf[:, m, k * P:(k + 1) * P], banks(m)[:, k * P:(k + 1) * P], ACT.Identity,
                                         bias=vecs[:, 3, k:k + 1], scale=vecs[:, 2, k:k + 1]).then_inc(A_f.sem, 1)

            def a_hi(t, b, m):
                wait_apart(act, A_f.sem, A_f.upto(t))
                copy(zT[:, HI, :, tile_cols(t)], zf[:, m, :].rearrange("p (k n) -> p k n", k=KC)).then_inc(A_hi.sem, 1)
            skewed(act, [(0, a_f), (0, a_hi)], NT, 2)

            for c in range(CT):
                act.wait_ge(k_bias, c + 1)
                nc.scalar.activation(nq[:, c, :], banks(2 * c, 2)[:, 0:INNER], ACT.Identity,
                                     bias=small[:, c, 7:8], scale=small[:, c, 6:7]).then_inc(k_norm, 1)
            act.wait_ge(kq_ready, QC)
            act.wait_ge(s_const, 7)
            for k in range(2):
                h = slice(k * DH, (k + 1) * DH)
                copy(Kbd[h, HI, :, :, k * DH:(k + 1) * DH],
                     kq[h, :, :].rearrange("p q (b l) -> p b q l", l=LC)).then_inc(K_hi, 1)
            for b in range(B):
                act.wait_ge(v_mm, b + 1)
                for k in range(2):
                    h = slice(k * DH, (k + 1) * DH)
                    src = banks(2 * (b % 2), 2)[h, 0:INNER].rearrange("p (q n) -> p q n", n=P)[:, :, k * DH:(k + 1) * DH]
                    copy(Vbd[h, HI, b, :, k * DH:(k + 1) * DH], src, 1.0 / WS).then_inc(V_hi, 1)
            for r in range(2):
                act.wait_ge(qb_mm, r + 1)
                heads = slice(r * H // 2 * DH, (r + 1) * H // 2 * DH)
                src = banks(4 * r, 3)[:, :].rearrange("p (h b l) -> p b h l", b=B, l=LC)
                copy(SB[0:DH, :, heads].rearrange("p b (h l) -> p b h l", l=LC), src[0:DH]).then_inc(SB_hi, 1)
                copy(bhi[DH:P, :, heads].rearrange("p b (h l) -> p b h l", l=LC), src[DH:P]).then_inc(SB_hi, 1)
            for i in range(2, 4):
                act.wait_ge(s_stage[i % 2], staged(i))
                copy((wq, wo)[i - 2][:, HI, :], stage[:, i % 2, 0:KC * INNER], WS).then_inc(split_hi.sem, 1)

            def b_n(t, b, m):
                if not isinstance(t, int) or t >= 2:
                    act.wait_ge(B_t.sem, B_t.upto(t - 2))
                act.wait_ge(B_s.sem, B_s.upto(t))
                nc.scalar.activation(nq[:, m, :], banks(2 * m, 2)[:, 0:INNER], ACT.Identity,
                                     bias=small[:, m, 3:4], scale=small[:, m, 2:3]).then_inc(B_n.sem, 1)

            def b_hi(t, b, m):
                wait_apart(act, B_t.sem, B_t.upto(t))
                copy(qT[:, HI, :, tile_cols(t)],
                     banks(4 + 2 * m, 2)[:, 0:INNER].rearrange("p (q n) -> p q n", n=P)).then_inc(B_hi.sem, 1)
            skewed(act, [(1, b_hi), (0, b_n)], NT, 2)

            for i in range(3):
                act.wait_ge(q_pe.sem, 2 + 2 * i)
                src = banks(4, 2).bitcast(f16)
                if i < 2:
                    copy(gT[:, i, :, :], src[:, 0:KC * FI].rearrange("p (k n) -> p k n", k=KC)).then_inc(q_act.sem, 1)
                else:
                    copy(dT[:], src[:, 0:IC * D].rearrange("p (c d) -> p c d", c=IC)).then_inc(q_act.sem, 1)
            act.wait_ge(q_pe.sem, 7)
            copy(wl1[:, HI, :, :], banks(1, 2).rearrange("p (k e) -> p k e", e=D), WS).then_inc(q_act.sem, 1)
            copy(wr[:, HI, :, :], stage[:, 1, 2 * D * KC:2 * D * KC + KC * 8].rearrange("p (k e) -> p k e", k=KC),
                 WS).then_inc(q_act.sem, 1)

            def c_ohi(t, b, m):
                act.wait_ge(C_o.sem, C_o.upto(t))
                if not isinstance(t, int) or t >= 1:
                    act.wait_ge(C_w.sem, C_w.upto(t - 1))
                copy(oT[:, HI, :], banks(4, 2)[:, 0:INNER]).then_inc(C_ohi.sem, 1)

            def c_phi(t, b, m):
                act.wait_ge(C_t.sem, C_t.upto(t))
                if not isinstance(t, int) or t >= 1:
                    act.wait_ge(C_o.sem, C_o.upto(t - 1))
                copy(pT[:, HI, :], banks(2, 2)[:, 0:INNER]).then_inc(C_phi.sem, 1)

            def c_e(t, b, m):
                act.wait_ge(C_m.sem, C_m.upto(t))
                nc.scalar.activation(sm[:, m % 2, :], sm[:, m % 2, :], ACT.Exp, scale=DH ** -0.5).then_inc(C_e.sem, 1)
            skewed(act, [(2, c_ohi), (1, c_phi), (0, c_e)], NT, 4)

            def d_c2(t, b, m):
                act.wait_ge(D_u.sem, D_u.upto(t))
                copy(hqT[:, m, :], banks(7).bitcast(f16)).then_inc(D_v.sem, 1)

            def d_a(t, b, m):
                act.wait_ge(D_g.sem, D_g.upto(t))
                nc.scalar.activation(hg[:], banks(0, 2), ACT.Silu, scale=sc0[:, m, 4:5]).then_inc(D_a.sem, 1)

            def d_1(t, b, m):
                act.wait_ge(D_h.sem, D_h.upto(t))
                nc.scalar.activation(hh[:, m, :], hh[:, m, :], ACT.Copy, bias=MAGIC, scale=sc1[:, m, 3:4]).then_inc(D_1.sem, 1)

            def d_c(t, b, m):
                act.wait_ge(D_t.sem, D_t.upto(t))
                copy(zqT[:, m, :], banks(4 + m).bitcast(f16)[:, 0:D]).then_inc(D_c.sem, 1)
            skewed(act, [(3, d_c2), (2, d_a), (2, d_1), (1, d_c)], NT, 2)
            for S in EF:
                def ef_hi(t, b, m):
                    wait_apart(act, S["t"].sem, S["t"].upto(t))
                    copy(zT[:, HI, :, tile_cols(t)],
                         banks(m % 2)[:, 0:D].rearrange("p (k n) -> p k n", k=KC)).then_inc(S["hi"].sem, 1)
                skewed(act, [(1, ef_hi)], NT, 4)
                if S is EF[0]:
                    act.wait_ge(S["x"].sem, NT)
                    act.wait_ge(s_zero, 16)
                    act.wait_ge(s_stage[0], staged0)
                    copy(wexp[:, 0, HI, :], stage[:, 0, :], WS).then_inc(x_hi.sem, 1)

            act.wait_ge(g_chain, 10)
            nc.scalar.activation(r2[:, 5], r2[:, 2], ACT.Exp).then_inc(g_act, 1)
            act.wait_ge(g_chain, 13)
            nc.scalar.activation(r3[:, 1], r3[:, 0], ACT.Exp).then_inc(g_act, 1)

            def run(R, count, first_tile, experts):
                d = 1 if experts else 0

                def hi(t, b, m):
                    k = m % 2
                    act.wait_ge(R["t"].sem, R["t"].upto(t))
                    if not isinstance(t, int) or t >= 2:
                        act.wait_ge(R["y"].sem, R["y"].upto(t - 2))
                    copy(ehT[:, k, HI, :], banks(4 + k)).then_inc(R["hi"].sem, 1)

                def silu(t, b, m):
                    k = m % 2
                    act.wait_ge(R["g"].sem, R["g"].upto(t))
                    nc.scalar.activation(eg[:, k, :], banks(k), ACT.Silu, scale=1.0 / WS).then_inc(R["a"].sem, 1)

                def split_hi_(t, b, m):
                    slot = (1 + m) % 2
                    base = staged(7) if slot else staged0
                    wait_apart(act, s_stage[slot], base + 48 * ((t - m % 2) // 2 + 1) if isinstance(t, int) else
                               base + 48 * (2 * b + m // 2 + 1))
                    if isinstance(t, int) and t == E - 1:
                        act.wait_ge(s_scatter, 16 * TOP * NT)
                    copy(wexp[:, one(1 + t), HI, :], stage[:, slot, :].unsqueeze(1), WS).then_inc(x_hi.sem, 1)
                stages = [(1 + d, hi), (d, silu)]
                if not experts and not first_tile:
                    stages.append((0, split_hi_))
                skewed(act, stages, count, 4)
            run(RUNS["sa"], NT // 2, 0, False)
            run(RUNS["ex"], NS, 0, True)
            run(RUNS["sb"], NT // 2, NT // 2, False)

        @block.tensor
        def _(pe):
            def mm(dst, a, w, start=True, stop=True):
                return nc.tensor.matmul(dst, a, w, start=start, stop=stop)

            def product(dst, parts):
                for n, (ah, al, wh, wl) in enumerate(parts):
                    mm(dst, ah, wh, start=(n == 0), stop=False)
                    mm(dst, ah, wl, start=False, stop=False)
                    last = mm(dst, al, wh, start=False, stop=(n == len(parts) - 1))
                return last

            def transposes(dst, src, n, idn):
                for k in range(n):
                    last = nc.tensor.transpose(dst[:, k * P:(k + 1) * P], src[:, k * P:(k + 1) * P], idn[:])
                return last

            pe.wait_ge(s_const, 4)
            pe.wait_ge(ctx_z, CT)
            for c in range(CT):
                for k in range(KC):
                    at = k * CT * P + c * P
                    nc.tensor.transpose(banks(0)[:, at:at + P], z[:, c, k * P:(k + 1) * P], ident[:])
                    last = nc.tensor.transpose(banks(1)[:, at:at + P], cx[:, c, k * P:(k + 1) * P], ident[:])
            last.then_inc(ctx_t, 1)
            pe.wait_ge(ctx_sum, 1)
            pe.wait_ge(cf_ready, 2)

            def a_t(t, b, m):
                pe.wait_ge(A_z.sem, A_z.upto(t))
                if not isinstance(t, int) or t >= 2:
                    pe.wait_ge(A_f.sem, A_f.upto(t - 2))
                transposes(banks(m), z[:, m, :], KC, ident).then_inc(A_t.sem, 1)
            skewed(pe, [(0, a_t)], NT, 2)

            def wide(w, hl):
                return w[:, hl, :].rearrange("p (k n) -> p k n", k=KC)

            def project(dst, a_of, w):
                for lo, hi in ((0, BANK), (BANK, INNER)):
                    last = product(dst[:, lo:hi], [(a_of(HI, k), a_of(LO, k), wide(w, HI)[:, k, lo:hi],
                                                    wide(w, LO)[:, k, lo:hi]) for k in range(KC)])
                return last
            pe.wait_ge(cT_lo, 3)
            pe.wait_ge(split_lo.sem, 1)
            pe.wait_ge(A_f.sem, A_f.upto(NT - 1))
            for c in range(CT):
                project(banks(2 * c, 2), lambda hl, k: cTk[:, hl, k, c * P:(c + 1) * P], wk).then_inc(k_mm, 1)
            for c in range(CT):
                pe.wait_ge(k_norm, c + 1)
                transposes(banks(4 + 2 * c, 2), nq[:, c, :], QC, ident).then_inc(k_t, 1)
            pe.wait_ge(split_lo.sem, 2)
            for b in range(B):
                if b >= 2:
                    pe.wait_ge(V_lo, 2 * (b - 1))
                project(banks(2 * (b % 2), 2), lambda hl, k: cT[:, hl, k, b, :], wv).then_inc(v_mm, 1)
            pe.wait_ge(V_lo, 2 * B)
            pe.wait_ge(qb_ready, 2)
            pe.wait_ge(kq_ready, QC)
            for r in range(2):
                for hd in range(H // 2):
                    h = r * (H // 2) + hd
                    last = mm(banks(4 * r, 3)[:, hd * B * LC:(hd + 1) * B * LC], qbm[:, h // 2, h % 2, :], kf[:, h // 2, :])
                last.then_inc(qb_mm, 1)

            pe.wait_ge(split_lo.sem, 3)
            pe.wait_ge(A_lo.sem, NT)
            pe.wait_ge(SB_lo, 2 * B)

            def b_q(t, b, m):
                if not isinstance(t, int) or t >= 2:
                    wait_apart(pe, B_n.sem, B_n.upto(t - 2))
                project(banks(2 * m, 2), lambda hl, k: zT[:, hl, k, tile_cols(t)], wq).then_inc(B_q.sem, 1)

            def b_t(t, b, m):
                pe.wait_ge(B_n.sem, B_n.upto(t))
                if not isinstance(t, int) or t >= 2:
                    pe.wait_ge(B_lo.sem, B_lo.upto(t - 2))
                transposes(banks(4 + 2 * m, 2), nq[:, m, :], QC, ident).then_inc(B_t.sem, 1)
            skewed(pe, [(0, b_q), (1, b_t)], NT, 2)

            pe.wait_ge(B_lo.sem, NT)
            for i in range(3):
                pe.wait_ge(q_dve.sem, 6 * i + 1)
                mm(banks(0)[:, 0:1], ones[:], wsc[:, i:i + 1]).then_inc(q_pe.sem, 1)
                pe.wait_ge(q_dve.sem, 6 * i + 6)
                if i >= 1:
                    pe.wait_ge(q_act.sem, i)
                w16 = wtern[:, i % 2, :]
                dst = banks(4, 2).bitcast(f16)
                for c in range(IC):
                    for k in range(KC):
                        if i < 2:
                            last = nc.tensor.transpose(dst[:, k * FI + c * P:k * FI + (c + 1) * P],
                                                       w16[:, c * D + k * P:c * D + (k + 1) * P], ident16[:])
                        else:
                            last = nc.tensor.transpose(dst[:, c * D + k * P:c * D + (k + 1) * P],
                                                       w16[:, k * FI + c * P:k * FI + (c + 1) * P], ident16[:])
                last.then_inc(q_pe.sem, 1)
            pe.wait_ge(s_stage[1], staged(7))
            for k in range(2 * KC):
                for e in range(KC):
                    last = nc.tensor.transpose(banks(1, 2)[:, k * D + e * P:k * D + (e + 1) * P],
                                               stage[:, 1, e * 2 * D + k * P:e * 2 * D + (k + 1) * P], ident[:])
            last.then_inc(q_pe.sem, 1)
            for b in range(B):
                pe.wait_ge(q_dve.sem, 18 + 1 + 2 + 6 * b + 5)
                product(banks(3)[:, 0:D], [(csum_rep[:, HI, k, :], csum_rep[:, LO, k, :], wl1[:, HI, KC + k, :],
                                            wl1[:, LO, KC + k, :]) for k in range(KC)]).then_inc(q_pe.sem, 1)

            pe.wait_ge(split_lo.sem, 4)
            pe.wait_ge(q_dve.sem, 18 + 1 + 2 + 6 * B)

            def c_w(t, b, m):
                pe.wait_ge(C_olo.sem, C_olo.upto(t))
                if not isinstance(t, int) or t >= 1:
                    pe.wait_ge(C_x.sem, C_x.upto(t - 1))
                product(banks(6)[:, 0:D], [(oT[:, HI, c * P:(c + 1) * P], oT[:, LO, c * P:(c + 1) * P],
                                            wo[:, HI, c * D:(c + 1) * D], wo[:, LO, c * D:(c + 1) * D])
                                           for c in range(QC)]).then_inc(C_w.sem, 1)

            def c_o(t, b, m):
                wait_apart(pe, C_plo.sem, C_plo.upto(t))
                if not isinstance(t, int) or t >= 1:
                    wait_apart(pe, C_olo.sem, C_olo.upto(t - 1))
                for c in range(QC):
                    last = product(banks(4, 2)[:, c * P:(c + 1) * P],
                                   [(Vbd[:, HI, one(b), c, :], Vbd[:, LO, one(b), c, :],
                                     pT[:, HI, c * P:(c + 1) * P], pT[:, LO, c * P:(c + 1) * P])])
                last.then_inc(C_o.sem, 1)

            def c_t(t, b, m):
                pe.wait_ge(C_p.sem, C_p.upto(t))
                if not isinstance(t, int) or t >= 1:
                    pe.wait_ge(C_plo.sem, C_plo.upto(t - 1))
                transposes(banks(2, 2), sm[:, m % 2, :], QC, ident).then_inc(C_t.sem, 1)

            def c_s(t, b, m):
                if not isinstance(t, int) or t >= 1:
                    wait_apart(pe, C_m.sem, C_m.upto(t - 1))
                for lo, hi in ((0, BANK), (BANK, INNER)):
                    mm(banks(0, 2)[:, lo:hi], ones64[:], SB[:, one(b), lo:hi], start=True, stop=False)
                    for c in range(lo // P, hi // P):
                        dst = banks(0, 2)[:, c * P:(c + 1) * P]
                        mm(dst, qT[:, HI, c, tile_cols(t)], Kbd[:, HI, one(b), c, :], start=False, stop=False)
                        mm(dst, qT[:, HI, c, tile_cols(t)], Kbd[:, LO, one(b), c, :], start=False, stop=False)
                        last = mm(dst, qT[:, LO, c, tile_cols(t)], Kbd[:, HI, one(b), c, :], start=False,
                                  stop=(c == hi // P - 1))
                last.then_inc(C_s.sem, 1)
            skewed(pe, [(3, c_w), (2, c_o), (1, c_t), (0, c_s)], NT, 4)

            pe.wait_ge(C_x.sem, NT)

            def d_y(t, b, m):
                pe.wait_ge(D_v.sem, D_v.upto(t))
                if not isinstance(t, int) or t >= 1:
                    pe.wait_ge(D_x.sem, D_x.upto(t - 1))
                for c in range(IC):
                    last = mm(banks(6)[:, 0:D], hqT[:, m, c * P:(c + 1) * P], dT[:, c, :], start=(c == 0), stop=(c == IC - 1))
                last.then_inc(D_y.sem, 1)

            def d_u(t, b, m):
                pe.wait_ge(D_2.sem, D_2.upto(t))
                if not isinstance(t, int) or t >= 1:
                    pe.wait_ge(D_v.sem, D_v.upto(t - 1))
                transposes(banks(7).bitcast(f16), hq, IC, ident16).then_inc(D_u.sem, 1)

            def d_g(t, b, m):
                pe.wait_ge(D_c.sem, D_c.upto(t))
                if not isinstance(t, int) or t >= 1:
                    pe.wait_ge(D_h.sem, D_h.upto(t - 1, 1))
                for g in range(2):
                    for half in range(FI // BANK):
                        for k in range(KC):
                            last = mm(banks(2 * g + half), zqT[:, m, k * P:(k + 1) * P],
                                      gT[:, g, k, half * BANK:(half + 1) * BANK], start=(k == 0), stop=(k == KC - 1))
                last.then_inc(D_g.sem, 1)

            def d_t(t, b, m):
                pe.wait_ge(D_z.sem, D_z.upto(t))
                if not isinstance(t, int) or t >= 2:
                    pe.wait_ge(D_c.sem, D_c.upto(t - 2))
                transposes(banks(4 + m).bitcast(f16), zq[:, m, :], KC, ident16).then_inc(D_t.sem, 1)
            skewed(pe, [(4, d_y), (3, d_u), (2, d_g), (1, d_t)], NT, 2)

            pe.wait_ge(D_x.sem, NT)
            for S in EF:
                if S is EF[1]:
                    pe.wait_ge(EF[0]["x"].sem, NT)

                def e_m(t, b, m):
                    wait_apart(pe, S["lo"].sem, S["lo"].upto(t))
                    if not isinstance(t, int) or t >= 2:
                        wait_apart(pe, S["x"].sem, S["x"].upto(t - 2))
                    product(banks(2 + m % 2)[:, 0:D], [(zT[:, HI, k, tile_cols(t)], zT[:, LO, k, tile_cols(t)],
                                                        wl1[:, HI, k, :], wl1[:, LO, k, :])
                                                       for k in range(KC)]).then_inc(S["m"].sem, 1)

                def ef_t(t, b, m):
                    pe.wait_ge(S["z"].sem, S["z"].upto(t))
                    if not isinstance(t, int) or t >= 2:
                        pe.wait_ge(S["lo"].sem, S["lo"].upto(t - 2))
                    transposes(banks(m % 2), z[:, m % 2, :], KC, ident).then_inc(S["t"].sem, 1)

                def f_m(t, b, m):
                    wait_apart(pe, S["lo"].sem, S["lo"].upto(t))
                    if not isinstance(t, int) or t >= 2:
                        wait_apart(pe, f_log.sem, f_log.upto(t - 2))
                    product(banks(2 + m % 2)[:, 0:E], [(zT[:, HI, k, tile_cols(t)], zT[:, LO, k, tile_cols(t)],
                                                        wr[:, HI, k, :], wr[:, LO, k, :])
                                                       for k in range(KC)]).then_inc(S["m"].sem, 1)
                skewed(pe, [(2, e_m if S is EF[0] else f_m), (1, ef_t)], NT, 4)

            pe.wait_ge(g_chain, 13)
            pe.wait_ge(s_fill2, 4)
            A = A16[:].rearrange("p t e -> p (t e)")
            mm(banks(4)[:, 0:NT * E], before16[:], A, start=True, stop=False)
            for k in range(1, NT):
                mm(banks(4)[:, k * E:NT * E], ones16[:], A[:, 0:(NT - k) * E], start=False, stop=(k == NT - 1))
            for k in range(NT):
                last = mm(banks(5)[:, 0:E], ones16[:], A[:, k * E:(k + 1) * E], start=(k == 0), stop=(k == NT - 1))
            last.then_inc(g_pe, 1)

            def run(R, count, first_tile, experts, a_of):
                d = 1 if experts else 0

                def expert(t):
                    return pe.value_load(tile_e[0:1, one(t)], min_val=0, max_val=E - 1) + 1 if experts else 0

                def down(t, b, m):
                    k = m % 2
                    e = expert(t)
                    wait_apart(pe, R["lo"].sem, R["lo"].upto(t))
                    if not isinstance(t, int) or t >= 1:
                        wait_apart(pe, R["o"].sem, R["o"].upto(t - 1))
                    w = wexp[:, one(e), :, 2 * KC * DE:WIDE].rearrange("p o s (c n) -> p (o s) c n", n=D)
                    product(banks(6)[:, 0:D], [(ehT[:, k, HI, c * P:(c + 1) * P], ehT[:, k, LO, c * P:(c + 1) * P],
                                                w[:, HI, c, :], w[:, LO, c, :]) for c in range(EC)]).then_inc(R["y"].sem, 1)

                def turn(t, b, m):
                    k = m % 2
                    pe.wait_ge(R["h"].sem, R["h"].upto(t))
                    if not isinstance(t, int) or t >= 2:
                        pe.wait_ge(R["lo"].sem, R["lo"].upto(t - 2))
                    transposes(banks(4 + k), eh[:, k, :], EC, ident).then_inc(R["t"].sem, 1)

                def gate_up(t, b, m):
                    k = m % 2
                    e = expert(t)
                    if experts:
                        wait_apart(pe, x_c.sem, x_c.upto(t))
                    if not isinstance(t, int) or t >= 2:
                        wait_apart(pe, R["h"].sem, R["h"].upto(t - 2))
                    for g in range(2):
                        w = wexp[:, one(e), :, g * KC * DE:(g + 1) * KC * DE].rearrange("p o s (c n) -> p (o s) c n", n=DE)
                        last = product(banks(2 * g + k), [(a_of(t, k, HI, c), a_of(t, k, LO, c), w[:, HI, c, :], w[:, LO, c, :])
                                                          for c in range(KC)])
                    last.then_inc(R["g"].sem, 1)

                def turn_x(t, b, m):
                    pe.wait_ge(s_xg[m], 16 * (b + 1))
                    if not isinstance(t, int) or t >= 1:
                        pe.wait_ge(x_c.sem, x_c.upto(t - 1))
                    transposes(banks(7).bitcast(f16), xg[:, m, :], 2 * KC, ident16).then_inc(x_t.sem, 1)
                stages = [(2 + d, down), (1 + d, turn), (d, gate_up)]
                if experts:
                    stages.append((0, turn_x))
                skewed(pe, stages, count, 4)

            pe.wait_ge(x_lo.sem, 1)
            pe.wait_ge(g_chain, 20)
            run(RUNS["sa"], NT // 2, 0, False, lambda t, k, hl, c: zT[:, hl, c, tile_cols(t)])
            pe.wait_ge(RUNS["sa"]["o"].sem, NT // 2)
            pe.wait_ge(x_lo.sem, E + 1)
            pe.wait_ge(routed, 3)
            run(RUNS["ex"], NS, 0, True, lambda t, k, hl, c: xgT[:, k, hl * D + c * P:hl * D + (c + 1) * P])
            pe.wait_ge(RUNS["ex"]["o"].sem, NS)
            run(RUNS["sb"], NT // 2, NT // 2, False, lambda t, k, hl, c: zT[:, hl, c, tile_cols(t + NT // 2)])


_INS = ['x', 'ctx_1024', 'L0_xattn_tab_g', 'L0_xattn_tab_b', 'L0_xattn_vid_g', 'L0_xattn_vid_b', 'L0_xattn_Wq', 'L0_xattn_Wk', 'L0_xattn_Wv', 'L0_xattn_q_g', 'L0_xattn_q_b', 'L0_xattn_k_g', 'L0_xattn_k_b', 'L0_xattn_Wo', 'L0_xattn_bo', 'L0_ffn_w_gate', 'L0_ffn_w_up', 'L0_ffn_w_down', 'L1_xattn_W', 'L1_xattn_b', 'L1_ffn_Wr', 'L1_ffn_Wg', 'L1_ffn_Wu', 'L1_ffn_Wd', 'L1_ffn_Sg', 'L1_ffn_Su', 'L1_ffn_Sd']
_OUTS = [((4, 512, 256), 'float32')]


def kernel(**inputs):
    import numpy as _np
    import concourse.bacc as _bacc
    from concourse import mybir as _mybir
    from concourse.bass_utils import run_bass_kernel_spmd as _run

    nc = _bacc.Bacc("TRN2", target_bir_lowering=False, num_devices=1)
    arrays, args = {}, []
    for name in _INS:
        a = _np.ascontiguousarray(inputs[name])
        arrays[f"in_{name}_dram"] = a
        args.append(nc.dram_tensor(f"in_{name}_dram", a.shape, _mybir.dt.from_np(a.dtype), kind="ExternalInput").ap())
    for i, (shape, dtype) in enumerate(_OUTS):
        dt = _mybir.dt.from_np(_np.dtype(dtype))
        args.append(nc.dram_tensor(f"out_{i}_dram", shape, dt, kind="ExternalOutput").ap())
    build(nc, *args)
    r = _run(nc, [arrays], core_ids=[0])
    return r.results[0]["out_0_dram"]
```

```python
import concourse.bass as bass
from concourse import mybir
from contextlib import ExitStack


class Steps:

    def __init__(self, sem, per=1, earlier=0):
        self.sem = sem
        self.per = per
        self.earlier = earlier

    def upto(self, tile, step=None):
        return (tile + self.earlier) * self.per + (self.per if step is None else step)


def skewed(engine, stages, count, unroll):
    deepest = max(lag for lag, _ in stages)

    def step(j, at, block):
        for lag, stage in stages:
            if at is None:
                if 0 <= j - lag < count:
                    stage(j - lag, (j - lag) // unroll, (j - lag) % unroll)
            else:
                tile = at - lag
                stage(unroll * block + tile, block + tile // unroll, tile % unroll)

    first = deepest + 2
    rounds = (count - first) // unroll
    for j in range(first):
        step(j, None, None)
    if rounds > 0:
        with engine.Fori(0, rounds) as i:
            for k in range(unroll):
                step(None, first + k, i)
    for j in range(first + rounds * unroll, count + deepest):
        step(j, None, None)


def build(nc, x, ctx_in, tab_g, tab_b, vid_g, vid_b, Wq, Wk, Wv, q_g, q_b, k_g, k_b, Wo, bo,
          w_gate, w_up, w_down, W_l1, b_l1, Wr, Wg, Wu, Wd, Sg, Su, Sd, out):
    fp32, f16, i32 = mybir.dt.float32, mybir.dt.float16, mybir.dt.int32
    ALU = mybir.AluOpType
    ACT = mybir.ActivationFunctionType
    X = mybir.AxisListType.X

    P = 128
    B, F, D = x.shape
    LC = ctx_in.shape[1]
    NT = B * F // P
    TB = F // P
    KC = D // P
    INNER = Wq.shape[1]
    DH = 64
    H = INNER // DH
    QC = INNER // P
    CT = B * LC // P
    FI = w_gate.shape[0]
    IC = FI // P
    BANK = 512
    EPS = 1e-5
    MAGIC = 1.5 * 2.0 ** 23
    WS = 2.0 ** 8
    HI, LO = 0, 1
    E, DE = Wr.shape[1], Sg.shape[1]
    EC = DE // P
    WIDE = 3 * KC * DE
    TOP = 2
    NS = (TOP * B * F) // P + E - 1
    YR = 8

    es = ExitStack()
    with es:
        def sb(name, shape, dt=fp32, scope=None):
            return (scope or es).enter_context(nc.sbuf_tensor(name, shape, dt))

        def sem(name):
            return es.enter_context(nc.semaphore(name))

        def steps(name, per=1):
            return Steps(sem(name), per)

        waits_passed = sem("waits_passed")

        def wait_apart(engine, sem, value):
            engine.wait_ge(sem, value)
            engine.sem_inc(waits_passed, 1)

        def one(t):
            return bass.ds(t, 1)

        def tile_cols(t):
            return bass.ds(t * P, P)

        xs = sb("xs", [P, NT, D])
        zT = sb("zT", [P, 2, KC, NT * P], f16)
        ident = sb("ident", [P, P])
        ident16 = sb("ident16", [P, P], f16)
        ones64 = sb("ones64", [P, P], f16)
        ones16 = sb("ones16", [P, P], f16)
        before16 = sb("before16", [P, P], f16)
        nhalf = sb("nhalf", [P, NT])
        ones = sb("ones", [P, P])
        stage = sb("stage", [P, 2, WIDE])
        wr = sb("wr", [P, 2, KC, E], f16)
        mv = sb("mv", [P, 2, 2])
        st = sb("st", [P, 2, 12])
        small = sb("small", [P, 2, 16])
        z = sb("z", [P, 2, D])

        early = es.enter_context(ExitStack())
        wT = sb("wT", [P, 3, KC * IC, P], f16, early)
        wl1 = sb("wl1", [P, 2, 2 * KC, D], f16, early)
        wsc = sb("wsc", [P, 12], fp32, early)
        bias_l1 = sb("bias_l1", [P, B, D], fp32, early)
        bo_b = sb("bo_b", [P, D], fp32, early)
        vecs = sb("vecs", [P, 4, KC], fp32, early)
        hvec = sb("hvec", [P, 4, QC], fp32, early)
        csum = sb("csum", [P, KC, B], fp32, early)
        bl_b = sb("bl_b", [P, D], fp32, early)
        st_all = sb("st_all", [P, NT, 6], fp32, early)
        ln_all = sb("ln_all", [P, 10, NT], fp32, early)
        zeros = sb("zeros", [P, 2 * D], f16, early)

        att = es.enter_context(ExitStack())
        con = att.enter_context(ExitStack())
        zf = sb("zf", [P, 2, D], fp32, con)
        cx = sb("cx", [P, CT, D], fp32, con)
        cTk = sb("cTk", [P, 2, KC, CT * P], f16, con)
        cf = sb("cf", [P, KC, CT * P], fp32, con)
        kf = sb("kf", [P, QC, CT * P], fp32, con)
        kq = sb("kq", [P, QC, CT * P], fp32, con)
        wk = sb("wk", [P, 2, KC * INNER], f16, con)
        wv = sb("wv", [P, 2, KC * INNER], f16, con)
        wo = sb("wo", [P, 2, QC * D], f16, con)
        qbm = sb("qbm", [P, QC, 2, P], fp32, con)
        VTbd = sb("VTbd", [P, 2, B, QC, P], f16, con)
        wl_raw = sb("wl_raw", [P, 2 * D * KC + KC * E], fp32, con)
        crep = sb("crep", [P, 2, KC, B, P], f16, con)
        nk = sb("nk", [P, CT, INNER], fp32, con)
        con.close()
        qT = sb("qT", [P, 2, QC, NT * P], f16, att)
        nq = sb("nq", [P, 2, INNER], fp32, att)
        sm = sb("sm", [P, 2, INNER], fp32, att)
        qy = sb("qy", [P, 2, 3, P], fp32, att)
        qr = sb("qr", [P, 2, 3, P], fp32, att)
        w16 = sb("w16", [P, 2, 3, P], f16, att)
        pT = sb("pT", [P, 2, 2, INNER], f16, att)
        wq = sb("wq", [P, 2, KC * INNER], f16, att)
        Kbd = sb("Kbd", [P, 2, B, QC, P], f16, att)
        VW = sb("VW", [P, 2, B, QC, D], f16, att)
        SB = sb("SB", [P, B, INNER], f16, att)
        red = sb("red", [P, 2, 2, H], fp32, att)
        att.close()

        f0 = es.enter_context(ExitStack())
        xc = sb("xc", [P, 2, D], fp32, f0)
        zq = sb("zq", [P, 2, D], f16, f0)
        zqT = sb("zqT", [P, 2, D], f16, f0)
        hg = sb("hg", [P, FI], fp32, f0)
        hh = sb("hh", [P, 2, FI], fp32, f0)
        hq = sb("hq", [P, FI], f16, f0)
        hqT = sb("hqT", [P, 2, FI], f16, f0)
        sc0 = sb("sc0", [P, 2, 8], fp32, f0)
        sc1 = sb("sc1", [P, 4, 4], fp32, f0)
        f0.close()
        early.close()

        wflat = sb("wflat", [P, (E + 1) * 2 * WIDE + NT * 2 * D - 2 * WIDE], f16)
        wexp = wflat[:, 0:(E + 1) * 2 * WIDE].rearrange("p (e s n) -> p e s n", s=2, n=WIDE)
        zrow = wflat[:, E * 2 * WIDE:E * 2 * WIDE + NT * 2 * D].rearrange("p (t n) -> p t n", t=NT)
        xg = sb("xg", [P, 4, 2 * D], f16)
        xgT = sb("xgT", [P, 2, 2 * D], f16)
        eg = sb("eg", [P, 2, DE])
        eh = sb("eh", [P, 2, DE])
        ehT = sb("ehT", [P, 2, 2, DE], f16)
        yb = sb("yb", [P, 2, D])
        logits = sb("logits", [P, NT, E])
        r3 = sb("r3", [P, 5, NT, E])
        r2 = sb("r2", [P, 12, NT])
        r1 = sb("r1", [P, 6, E])
        w8i = sb("w8i", [P, E], i32)
        w8 = sb("w8", [P, E])
        A16 = sb("A16", [P, NT, E], f16)
        idx = sb("idx", [P, 2, NT], i32)
        tile_no = sb("tile_no", [P, NS])
        tcmp = sb("tcmp", [P, NS, E - 1])
        tsum = sb("tsum", [P, NS])
        tile_e = sb("tile_e", [P, NS], i32)
        yg = stage[:].rearrange("p a n -> p (a n)")[:, 0:YR * 2 * D].rearrange("p (r k d) -> p r k d", k=2, d=D)

        ps = es.enter_context(nc.psum_tensor("ps", [P, 8 * BANK], fp32))

        def banks(a, n=1):
            return ps[:, a * BANK:(a + n) * BANK]

        s_x, s_ctx, s_vec, s_bias = sem("s_x"), sem("s_ctx"), sem("s_vec"), sem("s_bias")
        s_w = [sem(f"s_w{i}") for i in range(4)]
        s_tern, s_l1 = sem("s_tern"), sem("s_l1")
        l1_t, l1_hi, l1_ready = sem("l1_t"), sem("l1_hi"), sem("l1_ready")
        bias_mm, bias_done, x_stats = sem("bias_mm"), sem("bias_done"), sem("x_stats")
        VW_mm, VW_hi, VW_lo = sem("VW_mm"), sem("VW_hi"), sem("VW_lo")
        q_sum, q_mean, q_scale = sem("q_sum"), sem("q_mean"), sem("q_scale")
        Q_y, Q_c, Q_r, Q_w, Q_t, Q_o = (steps(n) for n in ("Q_y", "Q_c", "Q_r", "Q_w", "Q_t", "Q_o"))
        s_stage = [sem("s_stage0"), sem("s_stage1")]
        s_const, s_fill, s_fill2, s_late = sem("s_const"), sem("s_fill"), sem("s_fill2"), sem("s_late")
        split_hi, split_lo = steps("split_hi"), steps("split_lo")
        d_chain = sem("d_chain")
        ctx_var, ctx_rstd, ctx_z, ctx_t, ctx_sum = (sem(n) for n in ("ctx_var", "ctx_rstd", "ctx_z", "ctx_t", "ctx_sum"))
        cf_ready, cT_hi, cT_lo = sem("cf_ready"), sem("cT_hi"), sem("cT_lo")
        k_mm, k_var, k_rstd, k_bias, k_norm, k_t = (sem(n) for n in ("k_mm", "k_var", "k_rstd", "k_bias", "k_norm", "k_t"))
        kf_ready, kq_ready, v_mm, VK_hi, VK_lo = (sem(n) for n in ("kf_ready", "kq_ready", "v_mm", "VK_hi", "VK_lo"))
        qb_ready, qb_mm, SB_hi, SB_lo = sem("qb_ready"), sem("qb_mm"), sem("SB_hi"), sem("SB_lo")
        lnb_dve, lnb_pool = steps("lnb_dve"), steps("lnb_pool")
        A_z, A_t, A_f, A_hi, A_lo = steps("A_z"), steps("A_t"), steps("A_f", 2), steps("A_hi"), steps("A_lo")
        B_q, B_s, B_r, B_n, B_t, B_hi, B_lo = (steps("B_q"), steps("B_s", 6), steps("B_r"), steps("B_n"),
                                               steps("B_t"), steps("B_hi"), steps("B_lo"))
        C_s, C_m, C_e, C_r, C_p, C_t = (steps("C_s"), steps("C_m", 2), steps("C_e"), steps("C_r", 2),
                                        steps("C_p"), steps("C_t"))
        C_phi, C_plo, C_w, C_x = steps("C_phi"), steps("C_plo"), steps("C_w"), steps("C_x")
        C_b = steps("C_b")
        D_s, D_r, D_z, D_t, D_c, D_g = (steps("D_s", 3), steps("D_r"), steps("D_z", 7), steps("D_t"),
                                        steps("D_c"), steps("D_g"))
        D_a, D_h, D_1, D_2, D_u, D_v, D_y, D_x = (steps("D_a"), steps("D_h", 5), steps("D_1"), steps("D_2"),
                                                  steps("D_u"), steps("D_v"), steps("D_y"), steps("D_x"))
        E_ = {k: steps(f"EF_{k}", per) for k, per in
              (("s", 3), ("r", 1), ("z", 1), ("t", 1), ("hi", 1), ("lo", 1), ("b", 1), ("m", 1), ("x", 1))}
        EF = [E_, {k: Steps(c.sem, c.per, NT) for k, c in E_.items()}]
        s_out = sem("s_out")

        f_row_hi, f_row, f_log = steps("f_row_hi"), steps("f_row"), steps("f_log")
        g_chain, g_pe, g_act = sem("g_chain"), sem("g_pe"), sem("g_act")
        routed = sem("routed")
        s_zero, s_scatter = sem("s_zero"), sem("s_scatter")
        x_hi, x_lo = steps("x_hi"), steps("x_lo")
        RUNS = {}
        for n in ("sa", "ex"):
            RUNS[n] = {k: steps(f"{n}_{k}") for k in ("g", "a", "h", "t", "hi", "lo", "y", "o")}
        RUNS["sb"] = {k: Steps(c.sem, 1, NT // 2) for k, c in RUNS["sa"].items()}
        x_t, x_c = steps("x_t"), steps("x_c")
        s_xg = [sem(f"s_xg{i}") for i in range(4)]
        s_ys = [sem(f"s_ys{i}") for i in range(2)]
        s_yg = [sem(f"s_yg{i}") for i in range(YR)]
        comb = steps("comb", 2)

        xrows = nc.dram_tensor("xrows", [NS * P, 2 * D], f16, kind="Internal").ap()
        yrows = nc.dram_tensor("yrows", [NS * P, D], fp32, kind="Internal").ap()

        wr_raw = wl_raw[:, 2 * D * KC:].rearrange("p (k e) -> p k e", k=KC)
        gate_up_T = wT[:, 0:2].rearrange("p i (c k) n -> p i k c n", k=KC)
        down_T = wT[:, 2].rearrange("p (k c) n -> p c k n", k=KC)

        def vT_of(h):
            return banks(0, 3)[h, :].rearrange("p (c b l) -> p b c l", c=QC, l=LC)

        def VW_part(hl, r):
            return VW[:, hl].rearrange("p b c d -> p (b c d)")[:, r * 8 * D:(r + 1) * 8 * D]

        def SB_part(parts, r):
            return SB[parts, :, r * H // 2 * DH:(r + 1) * H // 2 * DH].rearrange("p b (h l) -> p b h l", l=LC)

        def qb_of(parts, r):
            return banks(4 * r, 3)[parts, :].rearrange("p (h b l) -> p b h l", b=B, l=LC)

        block = es.enter_context(nc.Block())

        xt = x.rearrange("b (t p) d -> p (b t) d", p=P)
        ctx_v = ctx_in.rearrange("(t two) l d -> (two l) t d", t=CT)

        flat = stage[:].rearrange("p a n -> p (a n)")
        WA, WF = KC * INNER, FI * D // P

        def att_w(i):
            return flat[:, i * WA:(i + 1) * WA]
        VEC_DONE = 16 * 8
        ffn_w = flat[:, 0:3 * WF].rearrange("p (i n) -> p i n", n=WF)

        @block.sync
        def _(sp):
            sp.dma_start(cx[:], ctx_v).then_inc(s_ctx, 16)
            for g in range(4):
                sp.dma_start(xs[:, g * NT // 4:(g + 1) * NT // 4, :],
                             xt[:, g * NT // 4:(g + 1) * NT // 4, :]).then_inc(s_x, 16)

            def rows(w):
                return w.rearrange("(k p) n -> p k n", p=P)
            for i, w in enumerate((Wk, Wv, Wq, Wo)):
                sp.dma_start(att_w(i).rearrange("p (k n) -> p k n", n=w.shape[1]), rows(w)).then_inc(s_w[i], 16)
            for i, w in enumerate((w_gate, w_up, w_down)):
                sp.wait_ge(split_lo.sem, i + 2)
                sp.dma_start(ffn_w[:, i, :].rearrange("p (k n) -> p k n", n=w.shape[1]), rows(w)).then_inc(s_tern, 16)

            def load_expert(slot, parts):
                for k, w in enumerate(parts):
                    sp.dma_start(stage[:, slot, k * KC * DE:(k + 1) * KC * DE].rearrange("p (k n) -> p k n", n=w.shape[1]),
                                 w.rearrange("(k p) n -> p k n", p=P)).then_inc(s_stage[slot], 16)
            sp.wait_ge(Q_y.sem, NT)
            load_expert(0, (Sg, Su, Sd))

            def load_nth(e, slot):
                load_expert(slot, [w[one(e)].rearrange("e h n -> (e h) n") for w in (Wg, Wu, Wd)])
            load_nth(0, 1)
            with sp.Fori(0, E // 2 - 1) as i:
                for k in range(2):
                    sp.wait_ge(x_lo.sem, 2 * i + k + 1)
                    load_nth(2 * i + k + 1, k)
            sp.wait_ge(x_lo.sem, E - 1)
            load_nth(E - 1, 0)

            def load_rows(t, b, m):
                if not isinstance(t, int) or t >= 4:
                    sp.wait_ge(x_t.sem, x_t.upto(t - 4))
                sp.dma_start(xg[:, m, :], xrows[bass.ds(t * P, P), :]).then_inc(s_xg[m], 16)

            def store_rows(t, b, m):
                sp.wait_ge(RUNS["ex"]["o"].sem, RUNS["ex"]["o"].upto(t))
                sp.dma_start(yrows[bass.ds(t * P, P), :], yb[:, m % 2, :]).then_inc(s_ys[m % 2], 16)
            sp.wait_ge(s_scatter, 16 * TOP * NT)
            skewed(sp, [(0, load_rows), (6, store_rows)], NS, 4)
            ot = out.rearrange("b (t p) d -> p (b t) d", p=P)

            def store_out(t, b, m):
                sp.wait_ge(comb.sem, comb.upto(t))
                sp.dma_start(ot[:, one(t), :], xs[:, one(t), :]).then_inc(s_out, 16)
            skewed(sp, [(0, store_out)], NT, 2)
            sp.wait_ge(s_out, 16 * NT)

        @block.gpsimd
        def _(pool):
            nc.gpsimd.memset(ident[:], 0.0).then_inc(s_fill, 1)
            nc.gpsimd.memset(ones[:], 1.0).then_inc(s_const, 1)
            nc.gpsimd.memset(ones64[:], 2.0 ** -6).then_inc(s_const, 1)
            nc.gpsimd.memset(nhalf[:], -0.5).then_inc(s_const, 1)
            nc.gpsimd.memset(zeros[:], 0.0).then_inc(s_fill2, 1)
            pool.wait_ge(s_fill, 1)
            nc.gpsimd.affine_select(out=ident[:], in_=ident[:], compare_op=ALU.not_equal, fill=1.0,
                                    base=0, pattern=[[-1, P]], channel_multiplier=1).then_inc(s_fill, 1)
            pool.wait_ge(s_fill, 2)
            nc.gpsimd.tensor_copy(ident16[:], ident[:]).then_inc(s_const, 1)
            nc.gpsimd.memset(ones16[:], 1.0).then_inc(s_fill2, 1)
            nc.gpsimd.memset(before16[:], 1.0).then_inc(s_fill2, 1)
            pool.wait_ge(s_fill2, 3)
            nc.gpsimd.affine_select(out=before16[:], in_=before16[:], compare_op=ALU.is_ge, fill=0.0,
                                    base=-1, pattern=[[1, P]], channel_multiplier=-1).then_inc(s_fill2, 1)

            def rsqrt(dst, src):
                return nc.gpsimd.tensor_tensor(dst, src, nhalf[:, 0:src.shape[-1]], ALU.pow)

            pool.wait_ge(ctx_var, 1)
            rsqrt(small[:, 0, 2:4], small[:, 0, 0:2]).then_inc(ctx_rstd, 1)
            nc.gpsimd.memset(VTbd[:].bitcast(fp32), 0.0).then_inc(s_const, 1)
            nc.gpsimd.memset(Kbd[:].bitcast(fp32), 0.0).then_inc(s_const, 1)
            nc.gpsimd.memset(qbm[:], 0.0).then_inc(s_const, 1)
            pool.wait_ge(lnb_dve.sem, 6)
            rsqrt(ln_all[:, 5, :], ln_all[:, 4, :]).then_inc(lnb_pool.sem, 1)
            pool.wait_ge(lnb_dve.sem, 9)
            rsqrt(ln_all[:, 7, :], ln_all[:, 6, :]).then_inc(lnb_pool.sem, 1)
            for c in range(CT):
                pool.wait_ge(k_var, c + 1)
                rsqrt(small[:, c, 5:6], small[:, c, 4:5]).then_inc(k_rstd, 1)
            pool.wait_ge(s_vec, VEC_DONE)
            pool.wait_ge(s_const, 7)
            for k in range(2):
                h = slice(k * DH, (k + 1) * DH)
                if k == 0:
                    pool.wait_ge(k_rstd, CT)
                else:
                    pool.wait_ge(qb_ready, 1)
                nc.gpsimd.tensor_copy(qbm[h, :, k, :],
                                      hvec[h, 1, :].unsqueeze(2).to_broadcast([DH, QC, P])).then_inc(qb_ready, 1)
            pool.wait_ge(qb_ready, 2)

            def b_r(t, b, m):
                pool.wait_ge(B_s.sem, B_s.upto(t, 4))
                rsqrt(small[:, m, 1:2], small[:, m, 0:1]).then_inc(B_r.sem, 1)
            skewed(pool, [(0, b_r)], NT, 2)

            def c_p(t, b, m):
                k = m % 2
                pool.wait_ge(C_r.sem, C_r.upto(t))
                nc.gpsimd.tensor_tensor(sm[:, k, :].rearrange("p (h j) -> p h j", j=DH),
                                        sm[:, k, :].rearrange("p (h j) -> p h j", j=DH),
                                        red[:, k, 1, :].unsqueeze(2).to_broadcast([P, H, DH]),
                                        ALU.mult).then_inc(C_p.sem, 1)
                nc.gpsimd.tensor_tensor(xs[:, one(t), :], xs[:, one(t), :], bo_b[:].unsqueeze(1),
                                        ALU.add).then_inc(C_b.sem, 1)

            def q_y(t, b, m):
                k = m % 2
                if not isinstance(t, int) or t >= 2:
                    wait_apart(pool, Q_r.sem, Q_r.upto(t - 2))
                nc.gpsimd.tensor_tensor(qy[:, k], ffn_w[:, :, tile_cols(t)], wsc[:, 8:11].unsqueeze(2).to_broadcast([P, 3, P]),
                                        ALU.mult).then_inc(Q_y.sem, 1)
                wait_apart(pool, Q_y.sem, Q_y.upto(t))
                nc.gpsimd.tensor_scalar(qy[:, k], qy[:, k], 1.0, -1.0, ALU.min, ALU.max).then_inc(Q_c.sem, 1)
            pool.wait_ge(q_scale, 2)
            skewed(pool, [(1, c_p), (1, q_y)], NT, 4)

            def d_r(t, b, m):
                pool.wait_ge(D_s.sem, D_s.upto(t))
                rsqrt(small[:, m % 2, 1:2], small[:, m % 2, 0:1]).then_inc(D_r.sem, 1)
            skewed(pool, [(0, d_r)], NT, 4)
            for S in EF:
                def ef_r(t, b, m):
                    pool.wait_ge(S["s"].sem, S["s"].upto(t))
                    rsqrt(small[:, m % 2, 1:2], small[:, m % 2, 0:1]).then_inc(S["r"].sem, 1)

                def e_b(t, b, m):
                    wait_apart(pool, S["z"].sem, S["z"].upto(t))
                    nc.gpsimd.tensor_tensor(xs[:, one(t), :], xs[:, one(t), :], bias_l1[:, one(b), :],
                                            ALU.add).then_inc(S["b"].sem, 1)

                def f_r(t, b, m):
                    k = m % 2
                    wait_apart(pool, S["z"].sem, S["z"].upto(t))
                    nc.gpsimd.tensor_copy(zrow[:, one(t), 0:D], z[:, k, :].unsqueeze(1)).then_inc(f_row_hi.sem, 1)
                    wait_apart(pool, f_row_hi.sem, f_row_hi.upto(t))
                    nc.gpsimd.tensor_tensor(zrow[:, one(t), D:2 * D], z[:, k, :].unsqueeze(1), zrow[:, one(t), 0:D],
                                            ALU.subtract).then_inc(f_row.sem, 1)
                if S is EF[0]:
                    skewed(pool, [(1, e_b), (0, ef_r)], NT, 4)
                    pool.wait_ge(S["x"].sem, NT)
                    nc.gpsimd.iota(w8i[:], pattern=[[-1, E]], base=E, channel_multiplier=0).then_inc(s_late, 1)
                    nc.gpsimd.iota(tile_e[:], pattern=[[1, NS]], base=0, channel_multiplier=0).then_inc(s_late, 1)
                    pool.wait_ge(s_late, 2)
                    nc.gpsimd.tensor_copy(w8[:], w8i[:]).then_inc(s_late, 1)
                    nc.gpsimd.tensor_copy(tile_no[:], tile_e[:]).then_inc(s_late, 1)
                else:
                    skewed(pool, [(1, f_r), (0, ef_r)], NT, 4)

            pool.wait_ge(f_row.sem, NT)
            pool.wait_ge(routed, 3)
            pool.wait_ge(s_zero, 16)
            for t in range(NT):
                for k in range(TOP):
                    nc.gpsimd.indirect_dma_start(xrows, bass.IndirectOffsetOnAxis(idx[:, k, t:t + 1], 0),
                                                 zrow[:, t, :], None).then_inc(s_scatter, 16)
            for i in range(2):
                pool.wait_ge(s_ys[i], 16 * ((NS + 1 - i) // 2))
            pool.wait_ge(x_lo.sem, E + 1)
            for t in range(NT):
                if t >= YR:
                    pool.wait_ge(comb.sem, comb.upto(t - YR))
                for k in range(TOP):
                    nc.gpsimd.indirect_dma_start(yg[:, t % YR, k, :], None, yrows,
                                                 bass.IndirectOffsetOnAxis(idx[:, k, t:t + 1], 0)).then_inc(s_yg[t % YR], 16)

        @block.vector
        def _(dve):
            v = nc.vector
            n = [0]

            def chain(ins):
                n[0] += 1
                ins.then_inc(d_chain, 1)
                dve.wait_ge(d_chain, n[0])

            dve.wait_ge(s_ctx, 16)
            for c in range(CT):
                chain(v.bn_stats(st[:, c, 0:6], cx[:, c, :]))
                chain(v.bn_aggr(mv[:, c, :], st[:, c, 0:6]))
            v.tensor_scalar(small[:, 0, 0:2], mv[:, :, 1], EPS, None, ALU.add).then_inc(ctx_var, 1)
            dve.wait_ge(ctx_rstd, 1)
            for c in range(CT):
                v.tensor_scalar(z[:, c, :], cx[:, c, :], mv[:, c, 0:1], small[:, 0, 2 + c:3 + c],
                                ALU.subtract, ALU.mult).then_inc(ctx_z, 1)

            ln = 0

            def link(ins):
                nonlocal ln
                ln += 1
                ins.then_inc(lnb_dve.sem, 1)
                dve.wait_ge(lnb_dve.sem, ln)
            dve.wait_ge(s_x, 64)
            with dve.Fori(0, NT // 4) as i:
                for k in range(4):
                    v.bn_stats(st_all[:, one(4 * i + k), :], xs[:, one(4 * i + k), :]).then_inc(x_stats, 1)
            dve.wait_ge(x_stats, NT)
            link(v.tensor_tensor(ln_all[:, 0, :], st_all[:, :, 1], st_all[:, :, 4], ALU.add))
            link(v.tensor_tensor(ln_all[:, 1, :], st_all[:, :, 1], st_all[:, :, 4], ALU.subtract))
            link(v.tensor_tensor(ln_all[:, 2, :], st_all[:, :, 2], st_all[:, :, 5], ALU.add))
            link(v.scalar_tensor_tensor(ln_all[:, 3, :], ln_all[:, 1, :], 0.25, ln_all[:, 1, :], ALU.mult, ALU.mult))
            link(v.scalar_tensor_tensor(ln_all[:, 8, :], ln_all[:, 2, :], 1.0 / D, ln_all[:, 3, :], ALU.mult, ALU.add))
            link(v.tensor_scalar(ln_all[:, 4, :], ln_all[:, 8, :], EPS, None, ALU.add))

            dve.wait_ge(ctx_t, 1)
            v.tensor_reduce(csum[:], banks(1).rearrange("p (k b l) -> p k b l", k=KC, l=LC), X,
                            ALU.add).then_inc(ctx_sum, 1)
            dve.wait_ge(ctx_sum, 1)
            chain(v.tensor_scalar(csum[:], csum[:], 1.0 / LC, None, ALU.mult))
            csum_rep = csum[:].unsqueeze(3).to_broadcast([P, KC, B, P])
            v.tensor_copy(crep[:, HI], csum_rep).then_inc(l1_ready, 1)
            dve.wait_ge(l1_ready, 1)
            v.tensor_tensor(crep[:, LO], csum_rep, crep[:, HI], ALU.subtract).then_inc(l1_ready, 1)
            dve.wait_ge(cT_hi, 1)
            v.tensor_tensor(cTk[:, LO, :, :], cf[:], cTk[:, HI, :, :], ALU.subtract).then_inc(cT_lo, 1)
            dve.wait_ge(l1_hi, 2)
            v.scalar_tensor_tensor(wl1[:, LO, :, :], banks(2, 2).rearrange("p (k e) -> p k e", e=D), WS,
                                   wl1[:, HI, :, :], ALU.mult, ALU.subtract).then_inc(l1_ready, 1)
            v.scalar_tensor_tensor(wr[:, LO, :, :], wr_raw, WS, wr[:, HI, :, :], ALU.mult, ALU.subtract).then_inc(l1_ready, 1)

            def split_low(w, i):
                dve.wait_ge(split_hi.sem, i + 1)
                v.scalar_tensor_tensor(w[:, LO, :], att_w(i), WS, w[:, HI, :], ALU.mult,
                                       ALU.subtract).then_inc(split_lo.sem, 1)
            split_low(wk, 0)

            dve.wait_ge(lnb_pool.sem, 1)
            link(v.tensor_tensor(ln_all[:, 9, :], ln_all[:, 8, :], ln_all[:, 5, :], ALU.mult))
            link(v.tensor_tensor(ln_all[:, 9, :], ln_all[:, 9, :], ln_all[:, 5, :], ALU.mult))
            link(v.tensor_scalar(ln_all[:, 6, :], ln_all[:, 9, :], EPS, None, ALU.add))
            link(v.tensor_scalar(ln_all[:, 0, :], ln_all[:, 0, :], 0.5, None, ALU.mult))
            split_low(wv, 1)
            for c in range(CT):
                dve.wait_ge(k_mm, c + 1)
                chain(v.bn_stats(st[:, c, 0:6], banks(2 * c)))
                chain(v.bn_stats(st[:, c, 6:12], banks(2 * c, 2)[:, BANK:INNER]))
                chain(v.bn_aggr(mv[:, c, :], st[:, c, :]))
                v.tensor_scalar(small[:, c, 4:5], mv[:, c, 1:2], WS ** -2, EPS, ALU.mult,
                                ALU.add).then_inc(k_var, 1)
            for c in range(CT):
                dve.wait_ge(k_rstd, c + 1)
                chain(v.tensor_scalar(small[:, c, 6:7], small[:, c, 5:6], 1.0 / WS, None, ALU.mult))
                v.scalar_tensor_tensor(small[:, c, 7:8], mv[:, c, 0:1], -1.0, small[:, c, 6:7], ALU.mult,
                                       ALU.mult).then_inc(k_bias, 1)
            dve.wait_ge(bias_mm, 1)
            dve.wait_ge(s_bias, 32)
            v.scalar_tensor_tensor(bias_l1[:], banks(4, 2).rearrange("p (b d) -> p b d", d=D), 1.0 / WS,
                                   bl_b[:].unsqueeze(1).to_broadcast([P, B, D]), ALU.mult, ALU.add).then_inc(bias_done, 1)
            split_low(wq, 2)
            split_low(wo, 3)
            dve.wait_ge(s_vec, VEC_DONE)
            for c in range(CT):
                dve.wait_ge(k_t, c + 1)
                T = banks(4 + 2 * c, 2)[:, 0:INNER].rearrange("p (q n) -> p q n", n=P)
                for q in range(QC):
                    v.tensor_scalar(kf[:, q, c * P:(c + 1) * P], T[:, q, :], hvec[:, 2, q:q + 1],
                                    hvec[:, 3, q:q + 1], ALU.mult, ALU.add).then_inc(kf_ready, 1)
            dve.wait_ge(lnb_pool.sem, 2)
            link(v.tensor_tensor(ln_all[:, 9, :], ln_all[:, 5, :], ln_all[:, 7, :], ALU.mult))

            def a_lo(t, b, m):
                dve.wait_ge(A_hi.sem, A_hi.upto(t))
                v.tensor_tensor(zT[:, LO, :, tile_cols(t)], zf[:, m, :].rearrange("p (k n) -> p k n", k=KC),
                                zT[:, HI, :, tile_cols(t)], ALU.subtract).then_inc(A_lo.sem, 1)

            def a_z(t, b, m):
                if not isinstance(t, int) or t >= 2:
                    dve.wait_ge(A_t.sem, A_t.upto(t - 2))
                v.tensor_scalar(z[:, m, :], xs[:, one(t), :], ln_all[:, 0, one(t)], ln_all[:, 9, one(t)],
                                ALU.subtract, ALU.mult).then_inc(A_z.sem, 1)
            skewed(dve, [(4, a_lo), (0, a_z)], NT, 2)

            dve.wait_ge(kf_ready, CT * QC)
            for q in range(QC):
                v.tensor_scalar(kq[:, q, :], kf[:, q, :], hvec[:, 0, q:q + 1], None, ALU.mult).then_inc(kq_ready, 1)
            dve.wait_ge(VK_hi, 2)
            for k in range(2):
                h = slice(k * DH, (k + 1) * DH)
                v.tensor_tensor(VTbd[h, LO, :, :, k * DH:(k + 1) * DH], vT_of(h),
                                VTbd[h, HI, :, :, k * DH:(k + 1) * DH], ALU.subtract).then_inc(VK_lo, 1)
            dve.wait_ge(VK_hi, 4)
            for k in range(2):
                h = slice(k * DH, (k + 1) * DH)
                v.tensor_tensor(Kbd[h, LO, :, :, k * DH:(k + 1) * DH],
                                kq[h, :, :].rearrange("p q (b l) -> p b q l", l=LC),
                                Kbd[h, HI, :, :, k * DH:(k + 1) * DH], ALU.subtract).then_inc(VK_lo, 1)
            for r in range(3):
                dve.wait_ge(VW_hi, r + 1)
                v.scalar_tensor_tensor(VW_part(LO, r), banks(4 * ((r + 1) % 2), 4), 1.0 / WS, VW_part(HI, r), ALU.mult,
                                       ALU.subtract).then_inc(VW_lo, 1)
            for r in range(2):
                dve.wait_ge(SB_hi, r + 1)
                v.tensor_tensor(SB_part(slice(DH, P), r), qb_of(slice(DH, P), r), SB_part(slice(DH, P), r),
                                ALU.subtract).then_inc(SB_lo, 1)
            dve.wait_ge(q_mean, 1)
            v.tensor_scalar(wsc[:, 4:7], banks(7)[:, 0:3], 1.0 / (FI * D), 1e-5, ALU.mult, ALU.max).then_inc(q_scale, 1)
            dve.wait_ge(q_scale, 1)
            v.reciprocal(wsc[:, 8:11], wsc[:, 4:7]).then_inc(q_scale, 1)

            def b_s(t, b, m):
                dve.wait_ge(B_q.sem, B_q.upto(t))
                q = banks(2 * m, 2)
                v.bn_stats(st[:, m, 0:6], q[:, 0:BANK]).then_inc(B_s.sem, 1)
                v.bn_stats(st[:, m, 6:12], q[:, BANK:INNER]).then_inc(B_s.sem, 1)
                wait_apart(dve, B_s.sem, B_s.upto(t, 2))
                v.bn_aggr(mv[:, m, :], st[:, m, :]).then_inc(B_s.sem, 1)
                dve.wait_ge(B_s.sem, B_s.upto(t, 3))
                v.tensor_scalar(small[:, m, 0:1], mv[:, m, 1:2], WS ** -2, EPS, ALU.mult, ALU.add).then_inc(B_s.sem, 1)

            def b_s2(t, b, m):
                dve.wait_ge(B_r.sem, B_r.upto(t))
                v.tensor_scalar(small[:, m, 2:3], small[:, m, 1:2], 1.0 / WS, None, ALU.mult).then_inc(B_s.sem, 1)
                dve.wait_ge(B_s.sem, B_s.upto(t, 5))
                v.scalar_tensor_tensor(small[:, m, 3:4], mv[:, m, 0:1], -1.0, small[:, m, 2:3],
                                       ALU.mult, ALU.mult).then_inc(B_s.sem, 1)

            def b_lo(t, b, m):
                dve.wait_ge(B_hi.sem, B_hi.upto(t))
                v.tensor_tensor(qT[:, LO, :, tile_cols(t)],
                                banks(4 + 2 * m, 2)[:, 0:INNER].rearrange("p (q n) -> p q n", n=P),
                                qT[:, HI, :, tile_cols(t)], ALU.subtract).then_inc(B_lo.sem, 1)
            skewed(dve, [(1, b_s), (3, b_lo), (1, b_s2)], NT, 2)

            def c_r(t, b, m):
                k = m % 2
                dve.wait_ge(C_e.sem, C_e.upto(t))
                v.tensor_reduce(red[:, k, 0, :], sm[:, k, :].rearrange("p (h j) -> p h j", j=DH), X,
                                ALU.add).then_inc(C_r.sem, 1)
                dve.wait_ge(C_r.sem, C_r.upto(t, 1))
                v.reciprocal(red[:, k, 1, :], red[:, k, 0, :]).then_inc(C_r.sem, 1)

            def c_x(t, b, m):
                dve.wait_ge(C_b.sem, C_b.upto(t))
                dve.wait_ge(C_w.sem, C_w.upto(t))
                v.scalar_tensor_tensor(xs[:, one(t), :], banks(4 + m % 2)[:, 0:D].unsqueeze(1), 1.0 / WS,
                                       xs[:, one(t), :], ALU.mult, ALU.add).then_inc(C_x.sem, 1)

            def c_plo(t, b, m):
                dve.wait_ge(C_phi.sem, C_phi.upto(t))
                v.tensor_tensor(pT[:, m % 2, LO, :], banks(2, 2)[:, 0:INNER], pT[:, m % 2, HI, :], ALU.subtract).then_inc(C_plo.sem, 1)

            def c_m(t, b, m):
                k = m % 2
                dve.wait_ge(C_s.sem, C_s.upto(t))
                S = banks(0, 2)[:, 0:INNER].rearrange("p (h j) -> p h j", j=DH)
                v.tensor_reduce(red[:, k, 0, :], S, X, ALU.max).then_inc(C_m.sem, 1)
                dve.wait_ge(C_m.sem, C_m.upto(t, 1))
                v.tensor_tensor(sm[:, k, :].rearrange("p (h j) -> p h j", j=DH), S,
                                red[:, k, 0, :].unsqueeze(2).to_broadcast([P, H, DH]),
                                ALU.subtract).then_inc(C_m.sem, 1)
            skewed(dve, [(4, c_x), (1, c_r), (2, c_plo), (0, c_m)], NT, 4)

            def d_x(t, b, m):
                dve.wait_ge(D_y.sem, D_y.upto(t))
                v.scalar_tensor_tensor(xs[:, one(t), :], banks(6)[:, 0:D].unsqueeze(1), sc1[:, m, 3:4], xs[:, one(t), :],
                                       ALU.mult, ALU.add).then_inc(D_x.sem, 1)

            def d_q(t, b, m):
                dve.wait_ge(D_1.sem, D_1.upto(t))
                if not isinstance(t, int) or t >= 1:
                    dve.wait_ge(D_u.sem, D_u.upto(t - 1))
                v.tensor_scalar(hq[:], hh[:, m % 2, :], MAGIC + 127.0, MAGIC, ALU.min, ALU.subtract).then_inc(D_2.sem, 1)

            def d_h(t, b, m):
                s = sc1[:, m, :]
                dve.wait_ge(D_a.sem, D_a.upto(t))
                v.scalar_tensor_tensor(hh[:, m % 2, :], banks(2, 2), sc0[:, m % 2, 4:5], hg[:], ALU.mult,
                                       ALU.mult).then_inc(D_h.sem, 1)
                dve.wait_ge(D_h.sem, D_h.upto(t, 1))
                v.tensor_reduce(s[:, 0:1], hh[:, m % 2, :], X, ALU.max, apply_absolute_value=True).then_inc(D_h.sem, 1)
                dve.wait_ge(D_h.sem, D_h.upto(t, 2))
                v.tensor_scalar(s[:, 1:2], s[:, 0:1], 1.0 / 127.0, 1e-5 / 127.0, ALU.mult, ALU.max).then_inc(D_h.sem, 1)
                dve.wait_ge(D_h.sem, D_h.upto(t, 3))
                v.reciprocal(s[:, 2:3], s[:, 1:2]).then_inc(D_h.sem, 1)
                v.tensor_scalar(s[:, 3:4], s[:, 1:2], wsc[:, 6:7], None, ALU.mult).then_inc(D_h.sem, 1)

            def d_z(t, b, m):
                k = m % 2
                s = sc0[:, k, :]
                n = 0

                def go(ins, wait=True):
                    nonlocal n
                    n += 1
                    ins.then_inc(D_z.sem, 1)
                    if wait:
                        dve.wait_ge(D_z.sem, D_z.upto(t, n))
                dve.wait_ge(D_r.sem, D_r.upto(t))
                go(v.tensor_scalar(xc[:, k, :], xs[:, one(t), :].rearrange("p o d -> p (o d)"), mv[:, k, 0:1],
                                   small[:, k, 1:2], ALU.subtract, ALU.mult))
                go(v.tensor_reduce(s[:, 0:1], xc[:, k, :], X, ALU.max, apply_absolute_value=True))
                go(v.tensor_scalar(s[:, 1:2], s[:, 0:1], 1.0 / 127.0, 1e-5 / 127.0, ALU.mult, ALU.max))
                go(v.reciprocal(s[:, 2:3], s[:, 1:2]), wait=False)
                go(v.tensor_scalar(s[:, 3:5], wsc[:, 4:6], s[:, 1:2], None, ALU.mult))
                go(v.tensor_scalar(xc[:, k, :], xc[:, k, :], s[:, 2:3], MAGIC, ALU.mult, ALU.add))
                if not isinstance(t, int) or t >= 2:
                    dve.wait_ge(D_t.sem, D_t.upto(t - 2))
                go(v.tensor_scalar(zq[:, k, :], xc[:, k, :], MAGIC + 127.0, MAGIC, ALU.min, ALU.subtract), wait=False)
                assert n == D_z.per

            def layer_stats(S):
                def first(t, b, m):
                    v.bn_stats(st[:, m % 2, 0:6], xs[:, one(t), :]).then_inc(S.sem, 1)

                def second(t, b, m):
                    wait_apart(dve, S.sem, S.upto(t, 1))
                    v.bn_aggr(mv[:, m % 2, :], st[:, m % 2, 0:6]).then_inc(S.sem, 1)

                def third(t, b, m):
                    dve.wait_ge(S.sem, S.upto(t, 2))
                    v.tensor_scalar(small[:, m % 2, 0:1], mv[:, m % 2, 1:2], EPS, None, ALU.add).then_inc(S.sem, 1)
                return first, second, third
            dve.wait_ge(C_x.sem, NT)
            d_s1, d_s2, d_s3 = layer_stats(D_s)
            skewed(dve, [(0, d_s1), (1, d_z), (0, d_s2), (3, d_q), (0, d_s3), (2, d_h), (4, d_x)], NT, 4)

            def split_expert(e, slot):
                dve.wait_ge(x_hi.sem, x_hi.upto(e))
                v.scalar_tensor_tensor(wexp[:, one(e), LO, :], stage[:, slot, :].unsqueeze(1), WS, wexp[:, one(e), HI, :],
                                       ALU.mult, ALU.subtract).then_inc(x_lo.sem, 1)

            for S in EF:
                def ef_x(t, b, m):
                    dve.wait_ge(S["b"].sem, S["b"].upto(t))
                    dve.wait_ge(S["m"].sem, S["m"].upto(t))
                    v.scalar_tensor_tensor(xs[:, one(t), :], banks(2 + m % 2)[:, 0:D].unsqueeze(1), 1.0 / WS, xs[:, one(t), :],
                                           ALU.mult, ALU.add).then_inc(S["x"].sem, 1)

                def ef_lo(t, b, m):
                    dve.wait_ge(S["hi"].sem, S["hi"].upto(t))
                    v.tensor_tensor(zT[:, LO, :, tile_cols(t)], banks(m % 2)[:, 0:D].rearrange("p (k n) -> p k n", k=KC),
                                    zT[:, HI, :, tile_cols(t)], ALU.subtract).then_inc(S["lo"].sem, 1)

                def ef_z(t, b, m):
                    k = m % 2
                    if not isinstance(t, int) or t >= 2:
                        dve.wait_ge(S["t"].sem, S["t"].upto(t - 2))
                    dve.wait_ge(S["r"].sem, S["r"].upto(t))
                    v.tensor_scalar(z[:, k, :], xs[:, one(t), :].rearrange("p o d -> p (o d)"), mv[:, k, 0:1],
                                    small[:, k, 1:2], ALU.subtract, ALU.mult).then_inc(S["z"].sem, 1)

                def f_l(t, b, m):
                    dve.wait_ge(S["m"].sem, S["m"].upto(t))
                    v.tensor_scalar(logits[:, one(t), :], banks(2 + m % 2)[:, 0:E].unsqueeze(1), 1.0 / WS, None,
                                    ALU.mult).then_inc(f_log.sem, 1)
                def ef_order(z_stage, last):
                    s1, s2, s3 = layer_stats(S["s"])
                    return [(0, s1), (5, last), (0, s2), (3, ef_lo), (0, s3), (1, z_stage)]
                if S is EF[0]:
                    dve.wait_ge(D_x.sem, NT)
                    skewed(dve, ef_order(ef_z, ef_x), NT, 4)
                    dve.wait_ge(S["x"].sem, NT)
                    split_expert(0, 0)
                else:
                    def ef_z2(t, b, m):
                        if not isinstance(t, int) or t >= 2:
                            dve.wait_ge(f_row.sem, f_row.upto(t - 2))
                        ef_z(t, b, m)
                    skewed(dve, ef_order(ef_z2, f_l), NT, 4)

            gn = [0]

            def g(ins):
                gn[0] += 1
                ins.then_inc(g_chain, 1)
                dve.wait_ge(g_chain, gn[0])

            def over_e(a):
                return a.unsqueeze(2).to_broadcast([P, NT, E])

            def over_t(a):
                return a.unsqueeze(1).to_broadcast([P, NT, E])
            sh, eq, oh1, oh2, sl = (r3[:, k] for k in range(5))
            m1, b1, m2, b2, zs, e2, rz, p2, w1, w2, sl1, sl2 = (r2[:, k] for k in range(12))
            dve.wait_ge(f_log.sem, NT)
            dve.wait_ge(s_late, 4)
            g(v.tensor_reduce(m1, logits[:], X, ALU.max))
            g(v.tensor_tensor(sh, logits[:], over_e(m1), ALU.subtract))
            g(v.tensor_scalar(eq, sh, 0.0, None, ALU.is_equal))
            g(v.tensor_tensor(eq, eq, over_t(w8[:]), ALU.mult))
            g(v.tensor_reduce(b1, eq, X, ALU.max))
            g(v.tensor_tensor(oh1, over_t(w8[:]), over_e(b1), ALU.is_equal))
            g(v.scalar_tensor_tensor(sl, oh1, -1e30, sh, ALU.mult, ALU.add))
            g(v.tensor_reduce(m2, sl, X, ALU.max))
            g(v.tensor_tensor(eq, sl, over_e(m2), ALU.is_equal))
            g(v.tensor_tensor(eq, eq, over_t(w8[:]), ALU.mult))
            g(v.tensor_reduce(b2, eq, X, ALU.max))
            g(v.tensor_tensor(oh2, over_t(w8[:]), over_e(b2), ALU.is_equal))
            g(v.tensor_tensor(A16[:], oh1, oh2, ALU.add))
            n8, t8, i8, s8, o8 = (r1[:, k] for k in range(5))
            dve.wait_ge(g_pe, 1)
            g(v.tensor_scalar(n8, banks(5)[:, 0:E], 1.0 / P, (P - 1.0) / P - 0.5 + 0.5 / P, ALU.mult, ALU.add))
            g(v.tensor_scalar(n8, n8, MAGIC, None, ALU.add))
            g(v.tensor_scalar(t8, n8, MAGIC, None, ALU.subtract))
            g(v.tensor_tensor_scan(i8, ones[:, 0:E], t8, 0.0, ALU.mult, ALU.add))
            g(v.tensor_tensor(s8, i8, t8, ALU.subtract))
            g(v.tensor_scalar(o8, s8, float(P), None, ALU.mult))
            g(v.tensor_tensor(sl, banks(4)[:, 0:NT * E].rearrange("p (t e) -> p t e", e=E), over_t(o8), ALU.add))
            g(v.tensor_tensor(oh1, oh1, sl, ALU.mult))
            g(v.tensor_tensor(oh2, oh2, sl, ALU.mult))
            g(v.tensor_reduce(sl1, oh1, X, ALU.add))
            g(v.tensor_reduce(sl2, oh2, X, ALU.add))
            v.tensor_copy(idx[:, 0, :], sl1).then_inc(routed, 1)
            v.tensor_copy(idx[:, 1, :], sl2).then_inc(routed, 1)
            g(v.tensor_tensor(tcmp[:], tile_no[:].unsqueeze(2).to_broadcast([P, NS, E - 1]),
                              s8[:, 1:E].unsqueeze(1).to_broadcast([P, NS, E - 1]), ALU.is_ge))
            g(v.tensor_reduce(tsum[:], tcmp[:], X, ALU.add))
            v.tensor_copy(tile_e[:], tsum[:]).then_inc(routed, 1)
            dve.wait_ge(g_act, 2)
            g(v.tensor_reduce(zs, r3[:, 1], X, ALU.add))
            g(v.reciprocal(rz, zs))
            g(v.tensor_tensor(p2, e2, rz, ALU.mult))
            g(v.tensor_tensor(zs, rz, p2, ALU.add))
            g(v.tensor_scalar(zs, zs, 1e-20, None, ALU.add))
            g(v.reciprocal(zs, zs))
            g(v.tensor_tensor(w1, rz, zs, ALU.mult))
            g(v.tensor_tensor(w2, p2, zs, ALU.mult))

            def run(R, count, first_tile, experts):
                d = 1 if experts else 0

                def out_(t, b, m):
                    k = m % 2
                    dve.wait_ge(R["y"].sem, R["y"].upto(t))
                    if experts:
                        if not isinstance(t, int) or t >= 2:
                            dve.wait_ge(s_ys[k], 16 * ((t - k) // 2) if isinstance(t, int) else 16 * (2 * b + (m - k) // 2))
                        v.tensor_scalar(yb[:, k, :], banks(6)[:, 0:D], 1.0 / WS, None, ALU.mult).then_inc(R["o"].sem, 1)
                    else:
                        at = t + first_tile
                        v.scalar_tensor_tensor(xs[:, one(at), :], banks(6)[:, 0:D].unsqueeze(1), 1.0 / WS,
                                               xs[:, one(at), :], ALU.mult, ALU.add).then_inc(R["o"].sem, 1)

                def lo(t, b, m):
                    k = m % 2
                    dve.wait_ge(R["hi"].sem, R["hi"].upto(t))
                    v.tensor_tensor(ehT[:, k, LO, :], banks(4 + k), ehT[:, k, HI, :], ALU.subtract).then_inc(R["lo"].sem, 1)

                def h(t, b, m):
                    k = m % 2
                    dve.wait_ge(R["a"].sem, R["a"].upto(t))
                    v.scalar_tensor_tensor(eh[:, k, :], banks(2 + k), 1.0 / WS, eg[:, k, :], ALU.mult,
                                           ALU.mult).then_inc(R["h"].sem, 1)

                def copy_x(t, b, m):
                    dve.wait_ge(x_t.sem, x_t.upto(t))
                    v.tensor_copy(xgT[:, m % 2, :], banks(7).bitcast(f16)[:, 0:2 * D]).then_inc(x_c.sem, 1)

                def split(t, b, m):
                    split_expert(1 + t, (1 + m) % 2)
                stages = [(2 + d, out_), (1 + d, lo), (d, h)]
                if experts:
                    stages.append((0, copy_x))
                elif not first_tile:
                    stages.append((0, split))
                skewed(dve, stages, count, 4)
            run(RUNS["sa"], NT // 2, 0, False)
            run(RUNS["ex"], NS, 0, True)
            run(RUNS["sb"], NT // 2, NT // 2, False)

            def comb_(t, b, m):
                dve.wait_ge(s_yg[m], 32 * (b + 1))
                v.scalar_tensor_tensor(xs[:, one(t), :], yg[:, m, 0, :].unsqueeze(1), r2[:, 8, one(t)], xs[:, one(t), :],
                                       ALU.mult, ALU.add).then_inc(comb.sem, 1)
                dve.wait_ge(comb.sem, comb.upto(t, 1))
                v.scalar_tensor_tensor(xs[:, one(t), :], yg[:, m, 1, :].unsqueeze(1), r2[:, 9, one(t)], xs[:, one(t), :],
                                       ALU.mult, ALU.add).then_inc(comb.sem, 1)
            dve.wait_ge(RUNS["sa"]["o"].sem, NT // 2)
            dve.wait_ge(RUNS["sb"]["o"].sem, NT)
            skewed(dve, [(0, comb_)], NT, YR)

        @block.scalar
        def _(act):
            with nc.allow_non_contiguous_dma(reason="a few short vectors, features onto partitions; the router's rows"):
                for k, vec in enumerate((tab_g, tab_b, vid_g, vid_b)):
                    act.dma_start(vecs[:, k, :], vec.rearrange("(c p) -> p c", p=P)).then_inc(s_vec, 16)
                for k, vec in enumerate((q_g, q_b, k_g, k_b)):
                    act.dma_start(hvec[:, k, :], vec.rearrange("(c p) -> p c", p=P)).then_inc(s_vec, 16)
                act.dma_start(wl_raw[:, 0:2 * D * KC].rearrange("p (k n) -> p k n", n=2 * D),
                              W_l1.rearrange("(k p) n -> p k n", p=P)).then_inc(s_l1, 16)
                act.dma_start(wr_raw, Wr.rearrange("(k p) n -> p k n", p=P)).then_inc(s_l1, 16)
            for dst, vec in ((bl_b, b_l1), (bo_b, bo)):
                act.dma_start(dst[:], vec.rearrange("(o d) -> o d", o=1).to_broadcast([P, D])).then_inc(s_bias, 16)

            def copy(dst, src, scale=1.0):
                return nc.scalar.activation(dst, src, ACT.Copy, scale=scale)

            act.wait_ge(s_vec, VEC_DONE)
            act.wait_ge(ctx_t, 1)
            for k in range(KC):
                nc.scalar.activation(cf[:, k, :], banks(0)[:, k * CT * P:(k + 1) * CT * P], ACT.Identity,
                                     bias=vecs[:, 1, k:k + 1], scale=vecs[:, 0, k:k + 1]).then_inc(cf_ready, 1)
            act.wait_ge(cf_ready, 2)
            copy(cTk[:, HI, :, :], cf[:]).then_inc(cT_hi, 1)
            act.wait_ge(l1_t, 1)
            copy(wl1[:, HI, :, :], banks(2, 2).rearrange("p (k e) -> p k e", e=D), WS).then_inc(l1_hi, 1)
            copy(wr[:, HI, :, :], wr_raw, WS).then_inc(l1_hi, 1)

            def split_high(w, i):
                act.wait_ge(s_w[i], 16)
                copy(w[:, HI, :], att_w(i), WS).then_inc(split_hi.sem, 1)
            split_high(wk, 0)
            split_high(wv, 1)
            act.wait_ge(s_fill2, 1)
            act.wait_ge(s_x, 64)
            act.dma_start(xrows.rearrange("(i p) d -> p i d", p=P),
                          zeros[:].unsqueeze(1).to_broadcast([P, NS, 2 * D])).then_inc(s_zero, 16)
            for c in range(CT):
                act.wait_ge(k_bias, c + 1)
                nc.scalar.activation(nk[:, c, :], banks(2 * c, 2)[:, 0:INNER], ACT.Identity,
                                     bias=small[:, c, 7:8], scale=small[:, c, 6:7]).then_inc(k_norm, 1)
            split_high(wq, 2)
            split_high(wo, 3)

            def a_f(t, b, m):
                act.wait_ge(A_t.sem, A_t.upto(t))
                if not isinstance(t, int) or t >= 2:
                    act.wait_ge(A_lo.sem, A_lo.upto(t - 2))
                for k in range(KC):
                    nc.scalar.activation(zf[:, m, k * P:(k + 1) * P], banks(4 + m)[:, k * P:(k + 1) * P], ACT.Identity,
                                         bias=vecs[:, 3, k:k + 1], scale=vecs[:, 2, k:k + 1]).then_inc(A_f.sem, 1)

            def a_hi(t, b, m):
                wait_apart(act, A_f.sem, A_f.upto(t))
                copy(zT[:, HI, :, tile_cols(t)], zf[:, m, :].rearrange("p (k n) -> p k n", k=KC)).then_inc(A_hi.sem, 1)
            skewed(act, [(3, a_hi), (2, a_f)], NT, 2)

            act.wait_ge(s_const, 7)
            act.wait_ge(v_mm, 1)
            for k in range(2):
                h = slice(k * DH, (k + 1) * DH)
                copy(VTbd[h, HI, :, :, k * DH:(k + 1) * DH], vT_of(h)).then_inc(VK_hi, 1)
            act.wait_ge(kq_ready, QC)
            for k in range(2):
                h = slice(k * DH, (k + 1) * DH)
                copy(Kbd[h, HI, :, :, k * DH:(k + 1) * DH],
                     kq[h, :, :].rearrange("p q (b l) -> p b q l", l=LC)).then_inc(VK_hi, 1)
            for r in range(3):
                act.wait_ge(VW_mm, r + 1)
                copy(VW_part(HI, r), banks(4 * ((r + 1) % 2), 4), 1.0 / WS).then_inc(VW_hi, 1)
            for r in range(2):
                act.wait_ge(qb_mm, r + 1)
                copy(SB_part(slice(0, P), r), qb_of(slice(0, P), r)).then_inc(SB_hi, 1)
            act.wait_ge(s_tern, 48)
            for i in range(3):
                if i >= 1:
                    act.wait_ge(q_sum, i)
                nc.scalar.activation(wk[:].rearrange("p s n -> p (s n)")[:, 0:WF], ffn_w[:, i, :], ACT.Abs,
                                     accum_out=wsc[:, i:i + 1]).then_inc(q_sum, 1)

            def b_n(t, b, m):
                if not isinstance(t, int) or t >= 2:
                    act.wait_ge(B_t.sem, B_t.upto(t - 2))
                act.wait_ge(B_s.sem, B_s.upto(t))
                nc.scalar.activation(nq[:, m, :], banks(2 * m, 2)[:, 0:INNER], ACT.Identity,
                                     bias=small[:, m, 3:4], scale=small[:, m, 2:3]).then_inc(B_n.sem, 1)

            def b_hi(t, b, m):
                wait_apart(act, B_t.sem, B_t.upto(t))
                copy(qT[:, HI, :, tile_cols(t)],
                     banks(4 + 2 * m, 2)[:, 0:INNER].rearrange("p (q n) -> p q n", n=P)).then_inc(B_hi.sem, 1)
            skewed(act, [(3, b_hi), (1, b_n)], NT, 2)

            def c_phi(t, b, m):
                act.wait_ge(C_t.sem, C_t.upto(t))
                if not isinstance(t, int) or t >= 2:
                    act.wait_ge(C_w.sem, C_w.upto(t - 2))
                copy(pT[:, m % 2, HI, :], banks(2, 2)[:, 0:INNER]).then_inc(C_phi.sem, 1)

            def c_e(t, b, m):
                act.wait_ge(C_m.sem, C_m.upto(t))
                nc.scalar.activation(sm[:, m % 2, :], sm[:, m % 2, :], ACT.Exp, scale=DH ** -0.5).then_inc(C_e.sem, 1)

            def q_r(t, b, m):
                k = m % 2
                act.wait_ge(Q_c.sem, Q_c.upto(t))
                if not isinstance(t, int) or t >= 2:
                    act.wait_ge(Q_w.sem, Q_w.upto(t - 2))
                nc.scalar.activation(qr[:, k], qy[:, k], ACT.Copy, bias=MAGIC).then_inc(Q_r.sem, 1)

            def q_w(t, b, m):
                k = m % 2
                act.wait_ge(Q_r.sem, Q_r.upto(t))
                if not isinstance(t, int) or t >= 2:
                    act.wait_ge(Q_t.sem, Q_t.upto(t - 2))
                nc.scalar.activation(w16[:, k], qr[:, k], ACT.Copy, bias=-MAGIC).then_inc(Q_w.sem, 1)

            def q_o(t, b, m):
                wait_apart(act, Q_t.sem, Q_t.upto(t))
                copy(wT[:, :, one(t), :], banks(6 + m % 2).bitcast(f16)[:, 0:3 * P].rearrange(
                    "p (i o n) -> p i o n", i=3, o=1)).then_inc(Q_o.sem, 1)
            skewed(act, [(2, c_phi), (4, q_o), (3, q_w), (2, q_r), (0, c_e)], NT, 4)

            def d_c2(t, b, m):
                act.wait_ge(D_u.sem, D_u.upto(t))
                copy(hqT[:, m % 2, :], banks(7).bitcast(f16)).then_inc(D_v.sem, 1)

            def d_a(t, b, m):
                act.wait_ge(D_g.sem, D_g.upto(t))
                nc.scalar.activation(hg[:], banks(0, 2), ACT.Silu, scale=sc0[:, m % 2, 3:4]).then_inc(D_a.sem, 1)

            def d_1(t, b, m):
                act.wait_ge(D_h.sem, D_h.upto(t))
                nc.scalar.activation(hh[:, m % 2, :], hh[:, m % 2, :], ACT.Copy, bias=MAGIC, scale=sc1[:, m, 2:3]).then_inc(D_1.sem, 1)

            def d_c(t, b, m):
                act.wait_ge(D_t.sem, D_t.upto(t))
                copy(zqT[:, m % 2, :], banks(4 + m % 2).bitcast(f16)[:, 0:D]).then_inc(D_c.sem, 1)
            skewed(act, [(3, d_1), (2, d_a), (1, d_c), (3, d_c2)], NT, 4)
            for S in EF:
                def ef_hi(t, b, m):
                    wait_apart(act, S["t"].sem, S["t"].upto(t))
                    copy(zT[:, HI, :, tile_cols(t)],
                         banks(m % 2)[:, 0:D].rearrange("p (k n) -> p k n", k=KC)).then_inc(S["hi"].sem, 1)
                skewed(act, [(2, ef_hi)], NT, 4)
                if S is EF[0]:
                    act.wait_ge(S["x"].sem, NT)
                    act.wait_ge(s_zero, 16)
                    act.wait_ge(s_stage[0], 48)
                    copy(wexp[:, 0, HI, :], stage[:, 0, :], WS).then_inc(x_hi.sem, 1)

            act.wait_ge(g_chain, 10)
            nc.scalar.activation(r2[:, 5], r2[:, 2], ACT.Exp).then_inc(g_act, 1)
            act.wait_ge(g_chain, 13)
            nc.scalar.activation(r3[:, 1], r3[:, 0], ACT.Exp).then_inc(g_act, 1)

            def run(R, count, first_tile, experts):
                d = 1 if experts else 0

                def hi(t, b, m):
                    k = m % 2
                    act.wait_ge(R["t"].sem, R["t"].upto(t))
                    if not isinstance(t, int) or t >= 2:
                        act.wait_ge(R["y"].sem, R["y"].upto(t - 2))
                    copy(ehT[:, k, HI, :], banks(4 + k)).then_inc(R["hi"].sem, 1)

                def silu(t, b, m):
                    k = m % 2
                    act.wait_ge(R["g"].sem, R["g"].upto(t))
                    nc.scalar.activation(eg[:, k, :], banks(k), ACT.Silu, scale=1.0 / WS).then_inc(R["a"].sem, 1)

                def split_hi_(t, b, m):
                    slot = (1 + m) % 2
                    base = 0 if slot else 48
                    wait_apart(act, s_stage[slot], base + 48 * ((t - m % 2) // 2 + 1) if isinstance(t, int) else
                               base + 48 * (2 * b + m // 2 + 1))
                    if isinstance(t, int) and t == E - 1:
                        act.wait_ge(s_scatter, 16 * TOP * NT)
                    copy(wexp[:, one(1 + t), HI, :], stage[:, slot, :].unsqueeze(1), WS).then_inc(x_hi.sem, 1)
                stages = [(1 + d, hi), (d, silu)]
                if not experts and not first_tile:
                    stages.append((0, split_hi_))
                skewed(act, stages, count, 4)
            run(RUNS["sa"], NT // 2, 0, False)
            run(RUNS["ex"], NS, 0, True)
            run(RUNS["sb"], NT // 2, NT // 2, False)

        @block.tensor
        def _(pe):
            def mm(dst, a, w, start=True, stop=True):
                return nc.tensor.matmul(dst, a, w, start=start, stop=stop)

            def product(dst, parts):
                for n, (ah, al, wh, wl) in enumerate(parts):
                    mm(dst, ah, wh, start=(n == 0), stop=False)
                    mm(dst, ah, wl, start=False, stop=False)
                    last = mm(dst, al, wh, start=False, stop=(n == len(parts) - 1))
                return last

            def transposes(dst, src, n, idn):
                for k in range(n):
                    last = nc.tensor.transpose(dst[:, k * P:(k + 1) * P], src[:, k * P:(k + 1) * P], idn[:])
                return last

            pe.wait_ge(s_const, 4)
            pe.wait_ge(ctx_z, CT)
            for c in range(CT):
                for k in range(KC):
                    at = k * CT * P + c * P
                    nc.tensor.transpose(banks(0)[:, at:at + P], z[:, c, k * P:(k + 1) * P], ident[:])
                    last = nc.tensor.transpose(banks(1)[:, at:at + P], cx[:, c, k * P:(k + 1) * P], ident[:])
            last.then_inc(ctx_t, 1)
            pe.wait_ge(s_l1, 32)
            for k in range(2 * KC):
                for e in range(KC):
                    last = nc.tensor.transpose(banks(2, 2)[:, k * D + e * P:k * D + (e + 1) * P],
                                               wl_raw[:, e * 2 * D + k * P:e * 2 * D + (k + 1) * P], ident[:])
            last.then_inc(l1_t, 1)

            def wide(w, hl):
                return w[:, hl, :].rearrange("p (k n) -> p k n", k=KC)

            def project(dst, a_of, w):
                for lo, hi in ((0, BANK), (BANK, INNER)):
                    last = product(dst[:, lo:hi], [(a_of(HI, k), a_of(LO, k), wide(w, HI)[:, k, lo:hi],
                                                    wide(w, LO)[:, k, lo:hi]) for k in range(KC)])
                return last
            pe.wait_ge(l1_ready, 4)
            for b in range(B):
                last = product(banks(4, 2)[:, b * D:(b + 1) * D],
                               [(crep[:, HI, k, b, :], crep[:, LO, k, b, :], wl1[:, HI, KC + k, :], wl1[:, LO, KC + k, :])
                                for k in range(KC)])
            last.then_inc(bias_mm, 1)
            pe.wait_ge(ctx_sum, 1)
            pe.wait_ge(cT_lo, 1)
            pe.wait_ge(split_lo.sem, 1)
            for c in range(CT):
                project(banks(2 * c, 2), lambda hl, k: cTk[:, hl, k, c * P:(c + 1) * P], wk).then_inc(k_mm, 1)
            pe.wait_ge(bias_done, 1)
            for c in range(CT):
                pe.wait_ge(k_norm, c + 1)
                transposes(banks(4 + 2 * c, 2), nk[:, c, :], QC, ident).then_inc(k_t, 1)
            pe.wait_ge(split_lo.sem, 2)
            for c in range(QC):
                last = product(banks(0, 3)[:, c * CT * P:(c + 1) * CT * P],
                               [(wide(wv, HI)[:, k, c * P:(c + 1) * P], wide(wv, LO)[:, k, c * P:(c + 1) * P],
                                 cTk[:, HI, k, :], cTk[:, LO, k, :]) for k in range(KC)])
            last.then_inc(v_mm, 1)

            def a_t(t, b, m):
                pe.wait_ge(A_z.sem, A_z.upto(t))
                if not isinstance(t, int) or t >= 2:
                    pe.wait_ge(A_f.sem, A_f.upto(t - 2))
                transposes(banks(4 + m), z[:, m, :], KC, ident).then_inc(A_t.sem, 1)
            pe.wait_ge(kf_ready, CT * QC)
            skewed(pe, [(1, a_t)], NT, 2)

            pe.wait_ge(VK_lo, 2)
            pe.wait_ge(split_lo.sem, 4)
            for r in range(3):
                if r == 2:
                    pe.wait_ge(VW_lo, 1)
                for n in range(8):
                    b, c = divmod(8 * r + n, QC)
                    last = product(banks(4 * ((r + 1) % 2), 4)[:, n * D:(n + 1) * D],
                                   [(VTbd[:, HI, b, c, :], VTbd[:, LO, b, c, :],
                                     wo[:, HI, c * D:(c + 1) * D], wo[:, LO, c * D:(c + 1) * D])])
                last.then_inc(VW_mm, 1)
            pe.wait_ge(qb_ready, 2)
            for r in range(2):
                pe.wait_ge(VW_lo, r + 2)
                for hd in range(H // 2):
                    h = r * (H // 2) + hd
                    last = mm(banks(4 * r, 3)[:, hd * B * LC:(hd + 1) * B * LC], qbm[:, h // 2, h % 2, :], kf[:, h // 2, :])
                last.then_inc(qb_mm, 1)
            pe.wait_ge(q_sum, 3)
            mm(banks(7)[:, 0:3], ones[:], wsc[:, 0:3]).then_inc(q_mean, 1)

            pe.wait_ge(split_lo.sem, 3)
            pe.wait_ge(A_lo.sem, NT)
            pe.wait_ge(SB_lo, 2)

            def b_q(t, b, m):
                if not isinstance(t, int) or t >= 2:
                    wait_apart(pe, B_n.sem, B_n.upto(t - 2))
                project(banks(2 * m, 2), lambda hl, k: zT[:, hl, k, tile_cols(t)], wq).then_inc(B_q.sem, 1)

            def b_t(t, b, m):
                pe.wait_ge(B_n.sem, B_n.upto(t))
                if not isinstance(t, int) or t >= 2:
                    pe.wait_ge(B_lo.sem, B_lo.upto(t - 2))
                transposes(banks(4 + 2 * m, 2), nq[:, m, :], QC, ident).then_inc(B_t.sem, 1)
            skewed(pe, [(3, b_t), (0, b_q)], NT, 2)

            def c_w(t, b, m):
                wait_apart(pe, C_plo.sem, C_plo.upto(t))
                if not isinstance(t, int) or t >= 2:
                    wait_apart(pe, C_x.sem, C_x.upto(t - 2))
                product(banks(4 + m % 2)[:, 0:D], [(pT[:, m % 2, HI, c * P:(c + 1) * P], pT[:, m % 2, LO, c * P:(c + 1) * P],
                                                    VW[:, HI, one(b), c, :], VW[:, LO, one(b), c, :])
                                                   for c in range(QC)]).then_inc(C_w.sem, 1)

            def q_t(t, b, m):
                pe.wait_ge(Q_w.sem, Q_w.upto(t))
                if not isinstance(t, int) or t >= 2:
                    pe.wait_ge(Q_o.sem, Q_o.upto(t - 2))
                transposes(banks(6 + m % 2).bitcast(f16), w16[:, m % 2].rearrange("p i n -> p (i n)"), 3,
                           ident16).then_inc(Q_t.sem, 1)

            def c_t(t, b, m):
                pe.wait_ge(C_p.sem, C_p.upto(t))
                if not isinstance(t, int) or t >= 1:
                    pe.wait_ge(C_plo.sem, C_plo.upto(t - 1))
                transposes(banks(2, 2), sm[:, m % 2, :], QC, ident).then_inc(C_t.sem, 1)

            def c_s(t, b, m):
                if not isinstance(t, int) or t >= 1:
                    wait_apart(pe, C_m.sem, C_m.upto(t - 1))
                for lo, hi in ((0, BANK), (BANK, INNER)):
                    mm(banks(0, 2)[:, lo:hi], ones64[:], SB[:, one(b), lo:hi], start=True, stop=False)
                    for c in range(lo // P, hi // P):
                        dst = banks(0, 2)[:, c * P:(c + 1) * P]
                        mm(dst, qT[:, HI, c, tile_cols(t)], Kbd[:, HI, one(b), c, :], start=False, stop=False)
                        mm(dst, qT[:, HI, c, tile_cols(t)], Kbd[:, LO, one(b), c, :], start=False, stop=False)
                        last = mm(dst, qT[:, LO, c, tile_cols(t)], Kbd[:, HI, one(b), c, :], start=False,
                                  stop=(c == hi // P - 1))
                last.then_inc(C_s.sem, 1)
            skewed(pe, [(2, c_t), (0, c_s), (4, q_t), (3, c_w)], NT, 4)

            pe.wait_ge(C_x.sem, NT)
            pe.wait_ge(Q_o.sem, NT)

            def d_y(t, b, m):
                pe.wait_ge(D_v.sem, D_v.upto(t))
                if not isinstance(t, int) or t >= 1:
                    pe.wait_ge(D_x.sem, D_x.upto(t - 1))
                for c in range(IC):
                    last = mm(banks(6)[:, 0:D].rearrange("p (k n) -> p k n", n=P), hqT[:, m % 2, c * P:(c + 1) * P], down_T[:, c],
                              start=(c == 0), stop=(c == IC - 1))
                last.then_inc(D_y.sem, 1)

            def d_u(t, b, m):
                pe.wait_ge(D_2.sem, D_2.upto(t))
                if not isinstance(t, int) or t >= 1:
                    pe.wait_ge(D_v.sem, D_v.upto(t - 1))
                transposes(banks(7).bitcast(f16), hq, IC, ident16).then_inc(D_u.sem, 1)

            def d_g(t, b, m):
                pe.wait_ge(D_c.sem, D_c.upto(t))
                if not isinstance(t, int) or t >= 1:
                    pe.wait_ge(D_h.sem, D_h.upto(t - 1, 1))
                for g in range(2):
                    for half in range(FI // BANK):
                        for k in range(KC):
                            last = mm(banks(2 * g + half).rearrange("p (c n) -> p c n", n=P), zqT[:, m % 2, k * P:(k + 1) * P],
                                      gate_up_T[:, g, k, half * BANK // P:(half + 1) * BANK // P],
                                      start=(k == 0), stop=(k == KC - 1))
                last.then_inc(D_g.sem, 1)

            def d_t(t, b, m):
                pe.wait_ge(D_z.sem, D_z.upto(t))
                if not isinstance(t, int) or t >= 2:
                    pe.wait_ge(D_c.sem, D_c.upto(t - 2))
                transposes(banks(4 + m % 2).bitcast(f16), zq[:, m % 2, :], KC, ident16).then_inc(D_t.sem, 1)
            skewed(pe, [(2, d_g), (1, d_t), (4, d_y), (3, d_u)], NT, 4)

            pe.wait_ge(D_x.sem, NT)
            for S in EF:
                if S is EF[1]:
                    pe.wait_ge(EF[0]["x"].sem, NT)

                def e_m(t, b, m):
                    wait_apart(pe, S["lo"].sem, S["lo"].upto(t))
                    if not isinstance(t, int) or t >= 2:
                        wait_apart(pe, S["x"].sem, S["x"].upto(t - 2))
                    product(banks(2 + m % 2)[:, 0:D], [(zT[:, HI, k, tile_cols(t)], zT[:, LO, k, tile_cols(t)],
                                                        wl1[:, HI, k, :], wl1[:, LO, k, :])
                                                       for k in range(KC)]).then_inc(S["m"].sem, 1)

                def ef_t(t, b, m):
                    pe.wait_ge(S["z"].sem, S["z"].upto(t))
                    if not isinstance(t, int) or t >= 2:
                        pe.wait_ge(S["lo"].sem, S["lo"].upto(t - 2))
                    transposes(banks(m % 2), z[:, m % 2, :], KC, ident).then_inc(S["t"].sem, 1)

                def f_m(t, b, m):
                    wait_apart(pe, S["lo"].sem, S["lo"].upto(t))
                    if not isinstance(t, int) or t >= 2:
                        wait_apart(pe, f_log.sem, f_log.upto(t - 2))
                    product(banks(2 + m % 2)[:, 0:E], [(zT[:, HI, k, tile_cols(t)], zT[:, LO, k, tile_cols(t)],
                                                        wr[:, HI, k, :], wr[:, LO, k, :])
                                                       for k in range(KC)]).then_inc(S["m"].sem, 1)
                skewed(pe, [(2, ef_t), (4, e_m if S is EF[0] else f_m)], NT, 4)

            pe.wait_ge(g_chain, 13)
            pe.wait_ge(s_fill2, 4)
            A = A16[:].rearrange("p t e -> p (t e)")
            mm(banks(4)[:, 0:NT * E], before16[:], A, start=True, stop=False)
            for k in range(1, NT):
                mm(banks(4)[:, k * E:NT * E], ones16[:], A[:, 0:(NT - k) * E], start=False, stop=(k == NT - 1))
            for k in range(NT):
                last = mm(banks(5)[:, 0:E], ones16[:], A[:, k * E:(k + 1) * E], start=(k == 0), stop=(k == NT - 1))
            last.then_inc(g_pe, 1)

            def run(R, count, first_tile, experts, a_of):
                d = 1 if experts else 0

                def expert(t):
                    return pe.value_load(tile_e[0:1, one(t)], min_val=0, max_val=E - 1) + 1 if experts else 0

                def down(t, b, m):
                    k = m % 2
                    e = chosen["down"]
                    wait_apart(pe, R["lo"].sem, R["lo"].upto(t))
                    if not isinstance(t, int) or t >= 1:
                        wait_apart(pe, R["o"].sem, R["o"].upto(t - 1))
                    w = wexp[:, one(e), :, 2 * KC * DE:WIDE].rearrange("p o s (c n) -> p (o s) c n", n=D)
                    product(banks(6)[:, 0:D], [(ehT[:, k, HI, c * P:(c + 1) * P], ehT[:, k, LO, c * P:(c + 1) * P],
                                                w[:, HI, c, :], w[:, LO, c, :]) for c in range(EC)]).then_inc(R["y"].sem, 1)

                def turn(t, b, m):
                    k = m % 2
                    pe.wait_ge(R["h"].sem, R["h"].upto(t))
                    if not isinstance(t, int) or t >= 2:
                        pe.wait_ge(R["lo"].sem, R["lo"].upto(t - 2))
                    transposes(banks(4 + k), eh[:, k, :], EC, ident).then_inc(R["t"].sem, 1)

                def gate_up(t, b, m):
                    k = m % 2
                    e = chosen["gate_up"]
                    if experts:
                        wait_apart(pe, x_c.sem, x_c.upto(t))
                    if not isinstance(t, int) or t >= 2:
                        wait_apart(pe, R["h"].sem, R["h"].upto(t - 2))
                    for g in range(2):
                        w = wexp[:, one(e), :, g * KC * DE:(g + 1) * KC * DE].rearrange("p o s (c n) -> p (o s) c n", n=DE)
                        last = product(banks(2 * g + k), [(a_of(t, k, HI, c), a_of(t, k, LO, c), w[:, HI, c, :], w[:, LO, c, :])
                                                          for c in range(KC)])
                    last.then_inc(R["g"].sem, 1)

                def turn_x(t, b, m):
                    pe.wait_ge(s_xg[m], 16 * (b + 1))
                    if not isinstance(t, int) or t >= 1:
                        pe.wait_ge(x_c.sem, x_c.upto(t - 1))
                    transposes(banks(7).bitcast(f16), xg[:, m, :], 2 * KC, ident16).then_inc(x_t.sem, 1)
                chosen = {}

                def choose(stage):
                    def read(t, b, m):
                        chosen[stage] = expert(t)
                    return read
                stages = [(d, choose("gate_up")), (2 + d, choose("down")), (2 + d, down), (1 + d, turn), (d, gate_up)]
                if experts:
                    stages.append((0, turn_x))
                skewed(pe, stages, count, 4)

            pe.wait_ge(x_lo.sem, 1)
            pe.wait_ge(g_chain, 20)
            run(RUNS["sa"], NT // 2, 0, False, lambda t, k, hl, c: zT[:, hl, c, tile_cols(t)])
            pe.wait_ge(RUNS["sa"]["o"].sem, NT // 2)
            pe.wait_ge(x_lo.sem, E + 1)
            pe.wait_ge(routed, 3)
            run(RUNS["ex"], NS, 0, True, lambda t, k, hl, c: xgT[:, k, hl * D + c * P:hl * D + (c + 1) * P])
            pe.wait_ge(RUNS["ex"]["o"].sem, NS)
            run(RUNS["sb"], NT // 2, NT // 2, False, lambda t, k, hl, c: zT[:, hl, c, tile_cols(t + NT // 2)])


_INS = ['x', 'ctx_1024', 'L0_xattn_tab_g', 'L0_xattn_tab_b', 'L0_xattn_vid_g', 'L0_xattn_vid_b', 'L0_xattn_Wq', 'L0_xattn_Wk', 'L0_xattn_Wv', 'L0_xattn_q_g', 'L0_xattn_q_b', 'L0_xattn_k_g', 'L0_xattn_k_b', 'L0_xattn_Wo', 'L0_xattn_bo', 'L0_ffn_w_gate', 'L0_ffn_w_up', 'L0_ffn_w_down', 'L1_xattn_W', 'L1_xattn_b', 'L1_ffn_Wr', 'L1_ffn_Wg', 'L1_ffn_Wu', 'L1_ffn_Wd', 'L1_ffn_Sg', 'L1_ffn_Su', 'L1_ffn_Sd']
_OUTS = [((4, 512, 256), 'float32')]


def kernel(**inputs):
    import numpy as _np
    import concourse.bacc as _bacc
    from concourse import mybir as _mybir
    from concourse.bass_utils import run_bass_kernel_spmd as _run

    nc = _bacc.Bacc("TRN2", target_bir_lowering=False, num_devices=1)
    arrays, args = {}, []
    for name in _INS:
        a = _np.ascontiguousarray(inputs[name])
        arrays[f"in_{name}_dram"] = a
        args.append(nc.dram_tensor(f"in_{name}_dram", a.shape, _mybir.dt.from_np(a.dtype), kind="ExternalInput").ap())
    for i, (shape, dtype) in enumerate(_OUTS):
        dt = _mybir.dt.from_np(_np.dtype(dtype))
        args.append(nc.dram_tensor(f"out_{i}_dram", shape, dt, kind="ExternalOutput").ap())
    build(nc, *args)
    r = _run(nc, [arrays], core_ids=[0])
    return r.results[0]["out_0_dram"]
```

```python
import concourse.bass as bass
from concourse import mybir
from contextlib import ExitStack


class Steps:

    def __init__(self, sem, per=1, earlier=0):
        self.sem = sem
        self.per = per
        self.earlier = earlier

    def upto(self, tile, step=None):
        return (tile + self.earlier) * self.per + (self.per if step is None else step)


def skewed(engine, stages, count, unroll):
    chained(engine, [(0, count, unroll, stages)])


def chained(engine, phases):
    before, before_steps = None, 0
    for n, (overlap_from, count, unroll, stages) in enumerate(phases):
        step = steps_of(stages, count, unroll)
        deepest = max(lag for lag, _ in stages)
        first = max(deepest + 2, before_steps - overlap_from)
        rounds = max(0, (count - first) // unroll)
        if rounds == 1:
            rounds = 0
        for j in range(first):
            if overlap_from + j < before_steps:
                before(overlap_from + j, None, None)
            step(j, None, None)
        if rounds > 0:
            with engine.Fori(0, rounds) as i:
                for k in range(unroll):
                    step(None, first + k, i)
        steps = count + deepest
        for j in range(first + rounds * unroll, phases[n + 1][0] if n + 1 < len(phases) else steps):
            step(j, None, None)
        before, before_steps = step, steps


def steps_of(stages, count, unroll):

    def step(j, at, block):
        for lag, stage in stages:
            if at is None:
                if 0 <= j - lag < count:
                    stage(j - lag, (j - lag) // unroll, (j - lag) % unroll)
            else:
                tile = at - lag
                stage(unroll * block + tile, block + tile // unroll, tile % unroll)
    return step


def build(nc, x, ctx_in, tab_g, tab_b, vid_g, vid_b, Wq, Wk, Wv, q_g, q_b, k_g, k_b, Wo, bo,
          w_gate, w_up, w_down, W_l1, b_l1, Wr, Wg, Wu, Wd, Sg, Su, Sd, out):
    fp32, f16, i32 = mybir.dt.float32, mybir.dt.float16, mybir.dt.int32
    ALU = mybir.AluOpType
    ACT = mybir.ActivationFunctionType
    X = mybir.AxisListType.X

    P = 128
    B, F, D = x.shape
    LC = ctx_in.shape[1]
    NT = B * F // P
    TB = F // P
    KC = D // P
    INNER = Wq.shape[1]
    DH = 64
    H = INNER // DH
    QC = INNER // P
    CT = B * LC // P
    FI = w_gate.shape[0]
    IC = FI // P
    BANK = 512
    EPS = 1e-5
    MAGIC = 1.5 * 2.0 ** 23
    WS = 2.0 ** 8
    HI, LO = 0, 1
    E, DE = Wr.shape[1], Sg.shape[1]
    EC = DE // P
    PART = KC * DE
    WIDE = 3 * PART
    GD = NT
    NA = 8
    NB = NT - NA
    GS = 3 * (E + 1) - GD - 1
    TOP = 2
    NS = (TOP * B * F) // P + E - 1
    YR = 8

    es = ExitStack()
    with es:
        def sb(name, shape, dt=fp32, scope=None):
            return (scope or es).enter_context(nc.sbuf_tensor(name, shape, dt))

        def sem(name):
            return es.enter_context(nc.semaphore(name))

        def steps(name, per=1):
            return Steps(sem(name), per)

        waits_passed = sem("waits_passed")

        def wait_apart(engine, sem, value):
            engine.wait_ge(sem, value)
            engine.sem_inc(waits_passed, 1)

        def one(t):
            return bass.ds(t, 1)

        def tile_cols(t):
            return bass.ds(t * P, P)

        xs = sb("xs", [P, NT, D])
        zT = sb("zT", [P, 2, KC, NT * P], f16)
        ident = sb("ident", [P, P])
        ident16 = sb("ident16", [P, P], f16)
        ones64 = sb("ones64", [P, P], f16)
        ones16 = sb("ones16", [P, P], f16)
        before16 = sb("before16", [P, P], f16)
        nhalf = sb("nhalf", [P, NT])
        ones = sb("ones", [P, P])
        stage = sb("stage", [P, 2, WIDE])
        scale_w = sb("scale_w", [P, 1])
        wr = sb("wr", [P, 2, KC, E], f16)
        mv = sb("mv", [P, 2, 2])
        st = sb("st", [P, 2, 12])
        small = sb("small", [P, 2, 16])
        z = sb("z", [P, 2, D])

        att = es.enter_context(ExitStack())
        con = att.enter_context(ExitStack())
        pairs = con.enter_context(ExitStack())
        za = sb("za", [P, 2, 2, D], fp32, pairs)
        zf = sb("zf", [P, 2, 2, D], fp32, pairs)
        pairs.close()
        before_cx = sb("before_cx", [P, 2, D], fp32, con)
        cx = sb("cx", [P, CT, D], fp32, con)
        cTk = sb("cTk", [P, 2, KC, CT * P], f16, con)
        cf = sb("cf", [P, KC, CT * P], fp32, con)
        kf = sb("kf", [P, QC, CT * P], fp32, con)
        kq = sb("kq", [P, QC, CT * P], fp32, con)
        wk = sb("wk", [P, 2, KC * INNER], f16, con)
        wv = sb("wv", [P, 2, KC * INNER], f16, con)
        wo = sb("wo", [P, 2, QC * D], f16, con)
        qbm = sb("qbm", [P, QC, 2, P], fp32, con)
        VTbd = sb("VTbd", [P, 2, B, QC, P], f16, con)
        crep = sb("crep", [P, 2, KC, B, P], f16, con)
        con.close()
        qT = sb("qT", [P, 2, QC, NT * P], f16, att)
        nq = sb("nq", [P, 2, INNER], fp32, att)
        sm = sb("sm", [P, 2, INNER], fp32, att)

        f0 = att.enter_context(ExitStack())
        below = sb("below", [P, 2 * PART], f16, f0)
        xc = sb("xc", [P, 2, D], fp32, f0)
        zq = sb("zq", [P, 2, D], f16, f0)
        zqT = sb("zqT", [P, 2, D], f16, f0)
        hg = sb("hg", [P, FI], fp32, f0)
        hh = sb("hh", [P, 2, FI], fp32, f0)
        hq = sb("hq", [P, FI], f16, f0)
        hqT = sb("hqT", [P, 2, FI], f16, f0)
        sc0 = sb("sc0", [P, 2, 8], fp32, f0)
        sc1 = sb("sc1", [P, 4, 4], fp32, f0)
        f0.close()
        VW = sb("VW", [P, 2, B, QC, D], f16, att)
        qy = sb("qy", [P, 2, 3, P], fp32, att)

        wT = sb("wT", [P, 3, KC * IC, P], f16, att)
        wl1 = sb("wl1", [P, 2, 2 * KC, D], f16, att)
        bias_l1 = sb("bias_l1", [P, B, D], fp32, att)
        bo_b = sb("bo_b", [P, D], fp32, att)
        bl_b = sb("bl_b", [P, D], fp32, att)
        wsc = sb("wsc", [P, 12], fp32, att)
        vecs = sb("vecs", [P, 4, KC], fp32, att)
        hvec = sb("hvec", [P, 4, QC], fp32, att)
        csum = sb("csum", [P, KC, B], fp32, att)
        st_all = sb("st_all", [P, NT, 6], fp32, att)
        ln_all = sb("ln_all", [P, 10, NT], fp32, att)
        zeros = sb("zeros", [P, 2 * D], f16, att)

        con2 = att.enter_context(ExitStack())
        wl_raw = sb("wl_raw", [P, 2 * D * KC + KC * E], fp32, con2)
        nk = sb("nk", [P, CT, INNER], fp32, con2)
        con2.close()
        qr = sb("qr", [P, 2, 3, P], fp32, att)
        w16 = sb("w16", [P, 2, 3, P], f16, att)
        pT = sb("pT", [P, 2, 2, INNER], f16, att)
        wq = sb("wq", [P, 2, KC * INNER], f16, att)
        Kbd = sb("Kbd", [P, 2, B, QC, P], f16, att)
        SB = sb("SB", [P, B, INNER], f16, att)
        red = sb("red", [P, 2, 2, H], fp32, att)
        att.close()

        ROWS_AT = (3 * (E + 1) - 1) * 2 * PART
        wflat = sb("wflat", [P, ROWS_AT + NT * 2 * D], f16)
        wpart = wflat[:, 0:(E + 1) * 2 * WIDE].rearrange("p (g s n) -> p g s n", s=2, n=PART)
        wexp = wflat[:, 0:(E + 1) * 2 * WIDE].rearrange("p (e k s n) -> p e k s n", k=3, s=2, n=PART)
        zrow = wflat[:, ROWS_AT:ROWS_AT + NT * 2 * D].rearrange("p (t n) -> p t n", t=NT)
        xg = sb("xg", [P, 4, 2 * D], f16)
        xgT = sb("xgT", [P, 2, 2 * D], f16)
        eg = sb("eg", [P, 2, DE])
        eh = sb("eh", [P, 2, DE])
        ehT = sb("ehT", [P, 2, 2, DE], f16)
        yb = sb("yb", [P, 2, D])
        logits = sb("logits", [P, NT, E])
        r3 = sb("r3", [P, 5, NT, E])
        r2 = sb("r2", [P, 12, NT])
        r1 = sb("r1", [P, 6, E])
        w8i = sb("w8i", [P, E], i32)
        w8 = sb("w8", [P, E])
        A16 = sb("A16", [P, NT, E], f16)
        idx = sb("idx", [P, 2, NT], i32)
        tile_no = sb("tile_no", [P, NS])
        tcmp = sb("tcmp", [P, NS, E - 1])
        tsum = sb("tsum", [P, NS])
        tile_e = sb("tile_e", [P, NS], i32)
        yg = stage[:].rearrange("p a n -> p (a n)")[:, 0:YR * 2 * D].rearrange("p (r k d) -> p r k d", k=2, d=D)

        ps = es.enter_context(nc.psum_tensor("ps", [P, 8 * BANK], fp32))

        def banks(a, n=1):
            return ps[:, a * BANK:(a + n) * BANK]

        s_x, s_ctx, s_vec, s_bias = sem("s_x"), sem("s_ctx"), sem("s_vec"), sem("s_bias")
        s_tab = sem("s_tab")
        s_w = [sem(f"s_w{i}") for i in range(4)]
        s_tern, s_l1 = sem("s_tern"), sem("s_l1")
        l1_t, l1_hi, l1_ready = sem("l1_t"), sem("l1_hi"), sem("l1_ready")
        bias_mm, bias_done, x_stats = sem("bias_mm"), sem("bias_done"), sem("x_stats")
        VW_mm = sem("VW_mm")
        q_sum, q_mean, q_scale = sem("q_sum"), sem("q_mean"), sem("q_scale")
        Q_y, Q_c, Q_r, Q_w, Q_t, Q_o = (steps(n) for n in ("Q_y", "Q_c", "Q_r", "Q_w", "Q_t", "Q_o"))
        s_part = [sem(f"s_part{i}") for i in range(4)]
        s_const, s_fill, s_fill2, s_late = sem("s_const"), sem("s_fill"), sem("s_fill2"), sem("s_late")
        split_hi, split_lo = steps("split_hi"), steps("split_lo")
        d_chain = sem("d_chain")
        ctx_var, ctx_rstd, ctx_z, ctx_t, ctx_sum = (sem(n) for n in ("ctx_var", "ctx_rstd", "ctx_z", "ctx_t", "ctx_sum"))
        cT_ready, cT_lo = sem("cT_ready"), sem("cT_lo")
        k_mm, k_var, k_rstd, k_bias, k_norm, k_t = (sem(n) for n in ("k_mm", "k_var", "k_rstd", "k_bias", "k_norm", "k_t"))
        kfq_ready, v_mm, VK_hi, VK_lo = (sem(n) for n in ("kfq_ready", "v_mm", "VK_hi", "VK_lo"))
        qb_ready, qb_mm, VS_hi, VS_lo = sem("qb_ready"), sem("qb_mm"), sem("VS_hi"), sem("VS_lo")
        lnb_dve, lnb_pool = steps("lnb_dve"), steps("lnb_pool")
        A_z, A_t, A_f, A_hi, A_lo = steps("A_z", 2), steps("A_t"), steps("A_f", 2), steps("A_hi"), steps("A_lo")
        B_q, B_s, B_r, B_n, B_t, B_hi, B_lo = (steps("B_q"), steps("B_s", 6), steps("B_r"), steps("B_n"),
                                               steps("B_t"), steps("B_hi"), steps("B_lo"))
        C_s, C_m, C_e, C_r, C_p, C_t = (steps("C_s"), steps("C_m", 2), steps("C_e"), steps("C_r", 2),
                                        steps("C_p"), steps("C_t"))
        C_phi, C_plo, C_w, C_x = steps("C_phi"), steps("C_plo"), steps("C_w"), steps("C_x")
        C_b = steps("C_b")
        D_s, D_r, D_z, D_t, D_c, D_g = (steps("D_s", 3), steps("D_r"), steps("D_z", 7), steps("D_t"),
                                        steps("D_c"), steps("D_g"))
        D_a, D_h, D_1, D_2, D_u, D_v, D_y, D_x = (steps("D_a"), steps("D_h", 5), steps("D_1"), steps("D_2"),
                                                  steps("D_u"), steps("D_v"), steps("D_y"), steps("D_x"))
        E_ = {k: steps(f"EF_{k}", per) for k, per in
              (("s", 3), ("r", 1), ("z", 1), ("t", 1), ("hi", 1), ("lo", 1), ("b", 1), ("m", 1), ("x", 1))}
        EF = [E_, {k: Steps(c.sem, c.per, NT) for k, c in E_.items()}]
        s_out = sem("s_out")

        f_row_hi, f_row, f_log = steps("f_row_hi"), steps("f_row"), steps("f_log")
        g_chain, g_pe, g_act = sem("g_chain"), sem("g_pe"), sem("g_act")
        routed = sem("routed")
        s_zero, s_scatter = sem("s_zero"), sem("s_scatter")
        X_m, X_hi, X_lo = steps("X_m"), steps("X_hi"), steps("X_lo")
        x_hi, x_lo = steps("x_hi"), steps("x_lo")
        RUNS = {}
        for n in ("sa", "ex"):
            RUNS[n] = {k: steps(f"{n}_{k}") for k in ("g", "a", "h", "t", "hi", "lo", "y", "o")}
        RUNS["sb"] = {k: Steps(c.sem, 1, NA) for k, c in RUNS["sa"].items()}
        x_t, x_c = steps("x_t"), steps("x_c")
        s_xg = [sem(f"s_xg{i}") for i in range(4)]
        s_ys = [sem(f"s_ys{i}") for i in range(2)]
        s_yg = [sem(f"s_yg{i}") for i in range(YR)]
        comb = steps("comb", 2)

        xrows = nc.dram_tensor("xrows", [NS * P, 2 * D], f16, kind="Internal").ap()
        yrows = nc.dram_tensor("yrows", [NS * P, D], fp32, kind="Internal").ap()

        wr_raw = wl_raw[:, 2 * D * KC:].rearrange("p (k e) -> p k e", k=KC)
        gate_up_T = wT[:, 0:2].rearrange("p i (c k) n -> p i k c n", k=KC)
        down_T = wT[:, 2].rearrange("p (k c) n -> p c k n", k=KC)

        def vT_of(h):
            return banks(0, 3)[h, :].rearrange("p (c b l) -> p b c l", c=QC, l=LC)

        def VW_part(hl, r):
            return VW[:, hl].rearrange("p b c d -> p (b c d)")[:, r * 8 * D:(r + 1) * 8 * D]

        def SB_part(parts, r):
            return SB[parts, :, r * H // 2 * DH:(r + 1) * H // 2 * DH].rearrange("p b (h l) -> p b h l", l=LC)

        def qb_of(parts, r):
            return banks((5, 4)[r], 3)[parts, :].rearrange("p (h b l) -> p b h l", b=B, l=LC)

        block = es.enter_context(nc.Block())

        xt = x.rearrange("b (t p) d -> p (b t) d", p=P)
        ctx_v = ctx_in.rearrange("(t two) l d -> (two l) t d", t=CT)

        flat = stage[:].rearrange("p a n -> p (a n)")
        WA, WF = KC * INNER, FI * D // P

        def att_w(i):
            return flat[:, i * WA:(i + 1) * WA]
        VEC_DONE = 16 * 4
        part_in = flat[:, 0:4 * PART].rearrange("p (r n) -> p r n", n=PART)
        ffn_w = flat[:, 0:3 * WF].rearrange("p (i n) -> p i n", n=WF)

        @block.sync
        def _(sp):
            sp.dma_start(cx[:], ctx_v).then_inc(s_ctx, 16)
            for g in range(4):
                sp.dma_start(xs[:, g * NT // 4:(g + 1) * NT // 4, :],
                             xt[:, g * NT // 4:(g + 1) * NT // 4, :]).then_inc(s_x, 16)

            def rows(w):
                return w.rearrange("(k p) n -> p k n", p=P)
            for i, w in enumerate((Wk, Wv, Wq, Wo)):
                sp.dma_start(att_w(i).rearrange("p (k n) -> p k n", n=w.shape[1]), rows(w)).then_inc(s_w[i], 16)
            for i, w in enumerate((w_gate, w_up, w_down)):
                sp.wait_ge(split_lo.sem, i + 2)
                sp.dma_start(ffn_w[:, i, :].rearrange("p (k n) -> p k n", n=w.shape[1]), rows(w)).then_inc(s_tern, 16)

            sp.wait_ge(Q_y.sem, NT)
            parts = [Sg, Su, Sd] + [w[one(e)].rearrange("e h n -> (e h) n") for e in range(E) for w in (Wg, Wu, Wd)]
            for g, w in enumerate(parts):
                if g >= 4 and g - 4 < GD:
                    sp.wait_ge(X_lo.sem, X_lo.upto(g - 4))
                elif g >= 4:
                    sp.wait_ge(x_lo.sem, x_lo.upto(g - 4 - GD))
                sp.dma_start(part_in[:, g % 4, :].rearrange("p (k n) -> p k n", n=w.shape[1]), rows(w)).then_inc(s_part[g % 4], 16)

            def load_rows(t, b, m):
                if not isinstance(t, int) or t >= 4:
                    sp.wait_ge(x_t.sem, x_t.upto(t - 4))
                sp.dma_start(xg[:, m, :], xrows[bass.ds(t * P, P), :]).then_inc(s_xg[m], 16)

            def store_rows(t, b, m):
                sp.wait_ge(RUNS["ex"]["o"].sem, RUNS["ex"]["o"].upto(t))
                sp.dma_start(yrows[bass.ds(t * P, P), :], yb[:, m % 2, :]).then_inc(s_ys[m % 2], 16)
            sp.wait_ge(s_scatter, 16 * TOP * NT)
            skewed(sp, [(0, load_rows), (6, store_rows)], NS, 4)
            ot = out.rearrange("b (t p) d -> p (b t) d", p=P)

            def store_out(t, b, m):
                sp.wait_ge(comb.sem, comb.upto(t))
                sp.dma_start(ot[:, one(t), :], xs[:, one(t), :]).then_inc(s_out, 16)
            skewed(sp, [(0, store_out)], NT, 2)
            sp.wait_ge(s_out, 16 * NT)

        @block.gpsimd
        def _(pool):
            nc.gpsimd.memset(ident[:], 0.0).then_inc(s_fill, 1)
            nc.gpsimd.memset(ones[:], 1.0).then_inc(s_const, 1)
            nc.gpsimd.memset(ones64[:], 2.0 ** -6).then_inc(s_const, 1)
            nc.gpsimd.memset(scale_w[:], WS).then_inc(s_const, 1)
            nc.gpsimd.memset(nhalf[:], -0.5).then_inc(s_const, 1)
            nc.gpsimd.memset(zeros[:], 0.0).then_inc(s_fill2, 1)
            pool.wait_ge(s_fill, 1)
            nc.gpsimd.affine_select(out=ident[:], in_=ident[:], compare_op=ALU.not_equal, fill=1.0,
                                    base=0, pattern=[[-1, P]], channel_multiplier=1).then_inc(s_fill, 1)
            pool.wait_ge(s_fill, 2)
            nc.gpsimd.tensor_copy(ident16[:], ident[:]).then_inc(s_const, 1)
            nc.gpsimd.memset(ones16[:], 1.0).then_inc(s_fill2, 1)
            nc.gpsimd.memset(before16[:], 1.0).then_inc(s_fill2, 1)
            pool.wait_ge(s_fill2, 3)
            nc.gpsimd.affine_select(out=before16[:], in_=before16[:], compare_op=ALU.is_ge, fill=0.0,
                                    base=-1, pattern=[[1, P]], channel_multiplier=-1).then_inc(s_fill2, 1)

            def rsqrt(dst, src):
                return nc.gpsimd.tensor_tensor(dst, src, nhalf[:, 0:src.shape[-1]], ALU.pow)

            pool.wait_ge(ctx_var, 1)
            rsqrt(small[:, 0, 2:4], small[:, 0, 0:2]).then_inc(ctx_rstd, 1)
            nc.gpsimd.memset(VTbd[:].bitcast(fp32), 0.0).then_inc(s_const, 1)
            nc.gpsimd.memset(Kbd[:].bitcast(fp32), 0.0).then_inc(s_const, 1)
            nc.gpsimd.memset(qbm[:], 0.0).then_inc(s_const, 1)
            pool.wait_ge(lnb_dve.sem, 6)
            rsqrt(ln_all[:, 5, :], ln_all[:, 4, :]).then_inc(lnb_pool.sem, 1)
            pool.wait_ge(lnb_dve.sem, 9)
            rsqrt(ln_all[:, 7, :], ln_all[:, 6, :]).then_inc(lnb_pool.sem, 1)
            for c in range(CT):
                pool.wait_ge(k_var, c + 1)
                rsqrt(small[:, c, 5:6], small[:, c, 4:5]).then_inc(k_rstd, 1)
            pool.wait_ge(s_vec, VEC_DONE)
            pool.wait_ge(s_const, 8)
            for k in range(2):
                h = slice(k * DH, (k + 1) * DH)
                if k == 0:
                    pool.wait_ge(k_rstd, CT)
                else:
                    pool.wait_ge(qb_ready, 1)
                nc.gpsimd.tensor_copy(qbm[h, :, k, :],
                                      hvec[h, 1, :].unsqueeze(2).to_broadcast([DH, QC, P])).then_inc(qb_ready, 1)
            pool.wait_ge(qb_ready, 2)

            def b_r(t, b, m):
                pool.wait_ge(B_s.sem, B_s.upto(t, 4))
                rsqrt(small[:, m, 1:2], small[:, m, 0:1]).then_inc(B_r.sem, 1)
            B_stages = [(0, b_r)]

            def c_p(t, b, m):
                k = m % 2
                pool.wait_ge(C_r.sem, C_r.upto(t))
                nc.gpsimd.tensor_tensor(sm[:, k, :].rearrange("p (h j) -> p h j", j=DH),
                                        sm[:, k, :].rearrange("p (h j) -> p h j", j=DH),
                                        red[:, k, 1, :].unsqueeze(2).to_broadcast([P, H, DH]),
                                        ALU.mult).then_inc(C_p.sem, 1)
                nc.gpsimd.tensor_tensor(xs[:, one(t), :], xs[:, one(t), :], bo_b[:].unsqueeze(1),
                                        ALU.add).then_inc(C_b.sem, 1)

            def q_y(t, b, m):
                k = m % 2
                if isinstance(t, int) and t == 0:
                    pool.wait_ge(q_scale, 2)
                if not isinstance(t, int) or t >= 2:
                    wait_apart(pool, Q_r.sem, Q_r.upto(t - 2))
                nc.gpsimd.tensor_tensor(qy[:, k], ffn_w[:, :, tile_cols(t)], wsc[:, 8:11].unsqueeze(2).to_broadcast([P, 3, P]),
                                        ALU.mult).then_inc(Q_y.sem, 1)
                wait_apart(pool, Q_y.sem, Q_y.upto(t))
                nc.gpsimd.tensor_scalar(qy[:, k], qy[:, k], 1.0, -1.0, ALU.min, ALU.max).then_inc(Q_c.sem, 1)
            chained(pool, [(0, NT, 2, B_stages), (NT, NT, 4, [(1, c_p), (1, q_y)])])
            pool.wait_ge(C_x.sem, NT)
            nc.gpsimd.iota(w8i[:], pattern=[[-1, E]], base=E, channel_multiplier=0).then_inc(s_late, 1)
            nc.gpsimd.iota(tile_e[:], pattern=[[1, NS]], base=0, channel_multiplier=0).then_inc(s_late, 1)
            pool.wait_ge(s_late, 2)
            nc.gpsimd.tensor_copy(w8[:], w8i[:]).then_inc(s_late, 1)
            nc.gpsimd.tensor_copy(tile_no[:], tile_e[:]).then_inc(s_late, 1)

            def d_r(t, b, m):
                pool.wait_ge(D_s.sem, D_s.upto(t))
                rsqrt(small[:, m % 2, 1:2], small[:, m % 2, 0:1]).then_inc(D_r.sem, 1)

            def x_m(t, b, m):
                pool.wait_ge(s_part[m], 16 * (b + 1))
                nc.gpsimd.tensor_tensor(part_in[:, m, :], part_in[:, m, :], scale_w[:].to_broadcast([P, PART]),
                                        ALU.mult).then_inc(X_m.sem, 1)

            def x_s(t, b, m):
                wait_apart(pool, X_hi.sem, X_hi.upto(t))
                nc.gpsimd.tensor_tensor(wpart[:, one(t), LO, :], part_in[:, m, :].unsqueeze(1), wpart[:, one(t), HI, :],
                                        ALU.subtract).then_inc(X_lo.sem, 1)
            phases = [(0, NT, 4, [(0, d_r), (1, x_m), (3, x_s)])]
            def layernorm_phase(S):
                def ef_r(t, b, m):
                    pool.wait_ge(S["s"].sem, S["s"].upto(t))
                    rsqrt(small[:, m % 2, 1:2], small[:, m % 2, 0:1]).then_inc(S["r"].sem, 1)

                def e_b(t, b, m):
                    wait_apart(pool, S["z"].sem, S["z"].upto(t))
                    nc.gpsimd.tensor_tensor(xs[:, one(t), :], xs[:, one(t), :], bias_l1[:, one(b), :],
                                            ALU.add).then_inc(S["b"].sem, 1)

                def f_r(t, b, m):
                    k = m % 2
                    wait_apart(pool, f_row_hi.sem, f_row_hi.upto(t))
                    nc.gpsimd.tensor_tensor(zrow[:, one(t), D:2 * D], z[:, k, :].unsqueeze(1), zrow[:, one(t), 0:D],
                                            ALU.subtract).then_inc(f_row.sem, 1)
                if S is EF[0]:
                    phases.append((NT, NT, 4, [(0, ef_r), (2, e_b)]))
                else:
                    phases.append((NT, NT, 4, [(0, ef_r), (2, f_r)]))
            for layer in EF:
                layernorm_phase(layer)
            chained(pool, phases)

            pool.wait_ge(f_row.sem, NT)
            pool.wait_ge(routed, 3)
            pool.wait_ge(s_zero, 16)
            for t in range(NT):
                for k in range(TOP):
                    nc.gpsimd.indirect_dma_start(xrows, bass.IndirectOffsetOnAxis(idx[:, k, t:t + 1], 0),
                                                 zrow[:, t, :], None).then_inc(s_scatter, 16)
            for i in range(2):
                pool.wait_ge(s_ys[i], 16 * ((NS + 1 - i) // 2))
            pool.wait_ge(x_lo.sem, 3 * (E + 1) - GD)
            for t in range(NT):
                if t >= YR:
                    pool.wait_ge(comb.sem, comb.upto(t - YR))
                for k in range(TOP):
                    nc.gpsimd.indirect_dma_start(yg[:, t % YR, k, :], None, yrows,
                                                 bass.IndirectOffsetOnAxis(idx[:, k, t:t + 1], 0)).then_inc(s_yg[t % YR], 16)

        @block.vector
        def _(dve):
            v = nc.vector
            n = [0]

            def chain(ins):
                n[0] += 1
                ins.then_inc(d_chain, 1)
                dve.wait_ge(d_chain, n[0])

            dve.wait_ge(s_ctx, 16)
            for c in range(CT):
                chain(v.bn_stats(st[:, c, 0:6], cx[:, c, :]))
                chain(v.bn_aggr(mv[:, c, :], st[:, c, 0:6]))
            v.tensor_scalar(small[:, 0, 0:2], mv[:, :, 1], EPS, None, ALU.add).then_inc(ctx_var, 1)
            dve.wait_ge(ctx_rstd, 1)
            for c in range(CT):
                v.tensor_scalar(z[:, c, :], cx[:, c, :], mv[:, c, 0:1], small[:, 0, 2 + c:3 + c],
                                ALU.subtract, ALU.mult).then_inc(ctx_z, 1)

            ln = 0

            def link(ins):
                nonlocal ln
                ln += 1
                ins.then_inc(lnb_dve.sem, 1)
                dve.wait_ge(lnb_dve.sem, ln)
            dve.wait_ge(s_x, 64)
            with dve.Fori(0, NT // 4) as i:
                for k in range(4):
                    v.bn_stats(st_all[:, one(4 * i + k), :], xs[:, one(4 * i + k), :]).then_inc(x_stats, 1)
            dve.wait_ge(x_stats, NT)
            link(v.tensor_tensor(ln_all[:, 0, :], st_all[:, :, 1], st_all[:, :, 4], ALU.add))
            link(v.tensor_tensor(ln_all[:, 1, :], st_all[:, :, 1], st_all[:, :, 4], ALU.subtract))
            link(v.tensor_tensor(ln_all[:, 2, :], st_all[:, :, 2], st_all[:, :, 5], ALU.add))
            link(v.scalar_tensor_tensor(ln_all[:, 3, :], ln_all[:, 1, :], 0.25, ln_all[:, 1, :], ALU.mult, ALU.mult))
            link(v.scalar_tensor_tensor(ln_all[:, 8, :], ln_all[:, 2, :], 1.0 / D, ln_all[:, 3, :], ALU.mult, ALU.add))
            link(v.tensor_scalar(ln_all[:, 4, :], ln_all[:, 8, :], EPS, None, ALU.add))

            dve.wait_ge(ctx_t, 1)
            v.tensor_reduce(csum[:], banks(1).rearrange("p (k b l) -> p k b l", k=KC, l=LC), X,
                            ALU.add).then_inc(ctx_sum, 1)
            dve.wait_ge(cT_ready, KC + 1)
            v.tensor_tensor(cTk[:, LO, :, :], cf[:], cTk[:, HI, :, :], ALU.subtract).then_inc(cT_lo, 1)
            dve.wait_ge(ctx_sum, 1)
            chain(v.tensor_scalar(csum[:], csum[:], 1.0 / LC, None, ALU.mult))

            def split_low(w, i):
                dve.wait_ge(split_hi.sem, i + 1)
                v.scalar_tensor_tensor(w[:, LO, :], att_w(i), WS, w[:, HI, :], ALU.mult,
                                       ALU.subtract).then_inc(split_lo.sem, 1)
            split_low(wk, 0)
            dve.wait_ge(lnb_pool.sem, 1)
            link(v.tensor_tensor(ln_all[:, 9, :], ln_all[:, 8, :], ln_all[:, 5, :], ALU.mult))
            link(v.tensor_tensor(ln_all[:, 9, :], ln_all[:, 9, :], ln_all[:, 5, :], ALU.mult))
            link(v.tensor_scalar(ln_all[:, 6, :], ln_all[:, 9, :], EPS, None, ALU.add))
            link(v.tensor_scalar(ln_all[:, 0, :], ln_all[:, 0, :], 0.5, None, ALU.mult))
            csum_rep = csum[:].unsqueeze(3).to_broadcast([P, KC, B, P])
            v.tensor_copy(crep[:, HI], csum_rep).then_inc(l1_ready, 1)
            split_low(wv, 1)
            dve.wait_ge(l1_ready, 1)
            v.tensor_tensor(crep[:, LO], csum_rep, crep[:, HI], ALU.subtract).then_inc(l1_ready, 1)
            for c in range(CT):
                dve.wait_ge(k_mm, c + 1)
                chain(v.bn_stats(st[:, c, 0:6], banks(2 * c)))
                chain(v.bn_stats(st[:, c, 6:12], banks(2 * c, 2)[:, BANK:INNER]))
                chain(v.bn_aggr(mv[:, c, :], st[:, c, :]))
                v.tensor_scalar(small[:, c, 4:5], mv[:, c, 1:2], WS ** -2, EPS, ALU.mult,
                                ALU.add).then_inc(k_var, 1)
            dve.wait_ge(l1_hi, 2)
            v.scalar_tensor_tensor(wl1[:, LO, :, :], banks(4, 2).rearrange("p (k e) -> p k e", e=D), WS,
                                   wl1[:, HI, :, :], ALU.mult, ALU.subtract).then_inc(l1_ready, 1)
            v.scalar_tensor_tensor(wr[:, LO, :, :], wr_raw, WS, wr[:, HI, :, :], ALU.mult, ALU.subtract).then_inc(l1_ready, 1)
            for c in range(CT):
                dve.wait_ge(k_rstd, c + 1)
                chain(v.tensor_scalar(small[:, c, 6:7], small[:, c, 5:6], 1.0 / WS, None, ALU.mult))
                v.scalar_tensor_tensor(small[:, c, 7:8], mv[:, c, 0:1], -1.0, small[:, c, 6:7], ALU.mult,
                                       ALU.mult).then_inc(k_bias, 1)
            split_low(wq, 2)
            split_low(wo, 3)
            dve.wait_ge(bias_mm, 1)
            dve.wait_ge(s_bias, 32)
            v.scalar_tensor_tensor(bias_l1[:], banks(6, 2).rearrange("p (b d) -> p b d", d=D), 1.0 / WS,
                                   bl_b[:].unsqueeze(1).to_broadcast([P, B, D]), ALU.mult, ALU.add).then_inc(bias_done, 1)
            dve.wait_ge(s_vec, VEC_DONE)
            for c in range(CT):
                dve.wait_ge(k_t, c + 1)
                T = banks(4 + 2 * c, 2)[:, 0:INNER].rearrange("p (q n) -> p q n", n=P)
                for q in range(QC):
                    v.tensor_scalar(kf[:, q, c * P:(c + 1) * P], T[:, q, :], hvec[:, 2, q:q + 1],
                                    hvec[:, 3, q:q + 1], ALU.mult, ALU.add).then_inc(kfq_ready, 1)
            dve.wait_ge(lnb_pool.sem, 2)
            link(v.tensor_tensor(ln_all[:, 9, :], ln_all[:, 5, :], ln_all[:, 7, :], ALU.mult))

            def a_lo(t, b, m):
                dve.wait_ge(A_hi.sem, A_hi.upto(t))
                v.tensor_tensor(zT[:, LO, :, bass.ds(t * 2 * P, 2 * P)], zf[:, m],
                                zT[:, HI, :, bass.ds(t * 2 * P, 2 * P)], ALU.subtract).then_inc(A_lo.sem, 1)

            def a_z(t, b, m):
                if not isinstance(t, int) or t >= 2:
                    dve.wait_ge(A_t.sem, A_t.upto(t - 2))
                for i in range(2):
                    tile = 2 * t + i
                    v.tensor_scalar(za[:, m, i, :].unsqueeze(1), xs[:, one(tile), :], ln_all[:, 0, one(tile)],
                                    ln_all[:, 9, one(tile)], ALU.subtract, ALU.mult).then_inc(A_z.sem, 1)
            skewed(dve, [(4, a_lo), (0, a_z)], NT // 2, 2)

            dve.wait_ge(kfq_ready, CT * QC)
            for q in range(QC):
                v.tensor_scalar(kq[:, q, :], kf[:, q, :], hvec[:, 0, q:q + 1], None, ALU.mult).then_inc(kfq_ready, 1)
            dve.wait_ge(VK_hi, 2)
            for k in range(2):
                h = slice(k * DH, (k + 1) * DH)
                v.tensor_tensor(VTbd[h, LO, :, :, k * DH:(k + 1) * DH], vT_of(h),
                                VTbd[h, HI, :, :, k * DH:(k + 1) * DH], ALU.subtract).then_inc(VK_lo, 1)

            def q_bias_low(r):
                dve.wait_ge(VS_hi, (1, 5)[r])
                v.tensor_tensor(SB_part(slice(DH, P), r), qb_of(slice(DH, P), r), SB_part(slice(DH, P), r),
                                ALU.subtract).then_inc(VS_lo, 1)
            q_bias_low(0)
            dve.wait_ge(VK_hi, 4)
            for k in range(2):
                h = slice(k * DH, (k + 1) * DH)
                v.tensor_tensor(Kbd[h, LO, :, :, k * DH:(k + 1) * DH],
                                kq[h, :, :].rearrange("p q (b l) -> p b q l", l=LC),
                                Kbd[h, HI, :, :, k * DH:(k + 1) * DH], ALU.subtract).then_inc(VK_lo, 1)
            for r in range(3):
                dve.wait_ge(VS_hi, r + 2)
                v.scalar_tensor_tensor(VW_part(LO, r), banks(4 * (r % 2), 4), 1.0 / WS, VW_part(HI, r), ALU.mult,
                                       ALU.subtract).then_inc(VS_lo, 1)
            q_bias_low(1)
            dve.wait_ge(q_mean, 1)
            v.tensor_scalar(wsc[:, 4:7], banks(7)[:, 0:3], 1.0 / (FI * D), 1e-5, ALU.mult, ALU.max).then_inc(q_scale, 1)
            dve.wait_ge(q_scale, 1)
            v.reciprocal(wsc[:, 8:11], wsc[:, 4:7]).then_inc(q_scale, 1)

            def b_s(t, b, m):
                dve.wait_ge(B_q.sem, B_q.upto(t))
                q = banks(2 * m, 2)
                v.bn_stats(st[:, m, 0:6], q[:, 0:BANK]).then_inc(B_s.sem, 1)
                v.bn_stats(st[:, m, 6:12], q[:, BANK:INNER]).then_inc(B_s.sem, 1)
                wait_apart(dve, B_s.sem, B_s.upto(t, 2))
                v.bn_aggr(mv[:, m, :], st[:, m, :]).then_inc(B_s.sem, 1)
                dve.wait_ge(B_s.sem, B_s.upto(t, 3))
                v.tensor_scalar(small[:, m, 0:1], mv[:, m, 1:2], WS ** -2, EPS, ALU.mult, ALU.add).then_inc(B_s.sem, 1)

            def b_s2(t, b, m):
                dve.wait_ge(B_r.sem, B_r.upto(t))
                v.tensor_scalar(small[:, m, 2:3], small[:, m, 1:2], 1.0 / WS, None, ALU.mult).then_inc(B_s.sem, 1)
                dve.wait_ge(B_s.sem, B_s.upto(t, 5))
                v.scalar_tensor_tensor(small[:, m, 3:4], mv[:, m, 0:1], -1.0, small[:, m, 2:3],
                                       ALU.mult, ALU.mult).then_inc(B_s.sem, 1)

            def b_lo(t, b, m):
                dve.wait_ge(B_hi.sem, B_hi.upto(t))
                v.tensor_tensor(qT[:, LO, :, tile_cols(t)],
                                banks(4 + 2 * m, 2)[:, 0:INNER].rearrange("p (q n) -> p q n", n=P),
                                qT[:, HI, :, tile_cols(t)], ALU.subtract).then_inc(B_lo.sem, 1)
            B_stages = [(1, b_s), (3, b_lo), (1, b_s2)]

            def c_r(t, b, m):
                k = m % 2
                dve.wait_ge(C_e.sem, C_e.upto(t))
                v.tensor_reduce(red[:, k, 0, :], sm[:, k, :].rearrange("p (h j) -> p h j", j=DH), X,
                                ALU.add).then_inc(C_r.sem, 1)
                dve.wait_ge(C_r.sem, C_r.upto(t, 1))
                v.reciprocal(red[:, k, 1, :], red[:, k, 0, :]).then_inc(C_r.sem, 1)

            def c_x(t, b, m):
                dve.wait_ge(C_b.sem, C_b.upto(t))
                dve.wait_ge(C_w.sem, C_w.upto(t))
                v.scalar_tensor_tensor(xs[:, one(t), :], banks(4 + m % 2)[:, 0:D].unsqueeze(1), 1.0 / WS,
                                       xs[:, one(t), :], ALU.mult, ALU.add).then_inc(C_x.sem, 1)

            def c_plo(t, b, m):
                dve.wait_ge(C_phi.sem, C_phi.upto(t))
                v.tensor_tensor(pT[:, m % 2, LO, :], banks(2, 2)[:, 0:INNER], pT[:, m % 2, HI, :], ALU.subtract).then_inc(C_plo.sem, 1)

            def c_m(t, b, m):
                k = m % 2
                dve.wait_ge(C_s.sem, C_s.upto(t))
                S = banks(0, 2)[:, 0:INNER].rearrange("p (h j) -> p h j", j=DH)
                v.tensor_reduce(red[:, k, 0, :], S, X, ALU.max).then_inc(C_m.sem, 1)
                dve.wait_ge(C_m.sem, C_m.upto(t, 1))
                v.tensor_tensor(sm[:, k, :].rearrange("p (h j) -> p h j", j=DH), S,
                                red[:, k, 0, :].unsqueeze(2).to_broadcast([P, H, DH]),
                                ALU.subtract).then_inc(C_m.sem, 1)
            chained(dve, [(0, NT, 2, B_stages), (NT, NT, 4, [(4, c_x), (1, c_r), (2, c_plo), (0, c_m)])])

            def d_x(t, b, m):
                dve.wait_ge(D_y.sem, D_y.upto(t))
                v.scalar_tensor_tensor(xs[:, one(t), :], banks(6)[:, 0:D].unsqueeze(1), sc1[:, m, 3:4], xs[:, one(t), :],
                                       ALU.mult, ALU.add).then_inc(D_x.sem, 1)

            def d_h1(t, b, m):
                dve.wait_ge(D_a.sem, D_a.upto(t))
                if not isinstance(t, int) or t >= 2:
                    dve.wait_ge(D_2.sem, D_2.upto(t - 2))
                v.scalar_tensor_tensor(hh[:, m % 2, :], banks(2, 2), sc0[:, m % 2, 4:5], hg[:], ALU.mult,
                                       ALU.mult).then_inc(D_h.sem, 1)

            def d_h2(t, b, m):
                dve.wait_ge(D_h.sem, D_h.upto(t, 1))
                v.tensor_reduce(sc1[:, m, 0:1], hh[:, m % 2, :], X, ALU.max, apply_absolute_value=True).then_inc(D_h.sem, 1)

            def d_h3(t, b, m):
                dve.wait_ge(D_h.sem, D_h.upto(t, 2))
                v.tensor_scalar(sc1[:, m, 1:2], sc1[:, m, 0:1], 1.0 / 127.0, 1e-5 / 127.0, ALU.mult,
                                ALU.max).then_inc(D_h.sem, 1)

            def d_h4(t, b, m):
                dve.wait_ge(D_h.sem, D_h.upto(t, 3))
                v.reciprocal(sc1[:, m, 2:3], sc1[:, m, 1:2]).then_inc(D_h.sem, 1)
                v.tensor_scalar(sc1[:, m, 3:4], sc1[:, m, 1:2], wsc[:, 6:7], None, ALU.mult).then_inc(D_h.sem, 1)

            def d_z1(t, b, m):
                k = m % 2
                dve.wait_ge(D_r.sem, D_r.upto(t))
                v.tensor_scalar(xc[:, k, :], xs[:, one(t), :].rearrange("p o d -> p (o d)"), mv[:, k, 0:1],
                                small[:, k, 1:2], ALU.subtract, ALU.mult).then_inc(D_z.sem, 1)

            def d_z2(t, b, m):
                dve.wait_ge(D_z.sem, D_z.upto(t, 1))
                v.tensor_reduce(sc0[:, m % 2, 0:1], xc[:, m % 2, :], X, ALU.max, apply_absolute_value=True).then_inc(D_z.sem, 1)

            def d_z3(t, b, m):
                dve.wait_ge(D_z.sem, D_z.upto(t, 2))
                v.tensor_scalar(sc0[:, m % 2, 1:2], sc0[:, m % 2, 0:1], 1.0 / 127.0, 1e-5 / 127.0, ALU.mult,
                                ALU.max).then_inc(D_z.sem, 1)

            def d_z4(t, b, m):
                k = m % 2
                dve.wait_ge(D_z.sem, D_z.upto(t, 3))
                v.reciprocal(sc0[:, k, 2:3], sc0[:, k, 1:2]).then_inc(D_z.sem, 1)
                v.tensor_scalar(sc0[:, k, 3:5], wsc[:, 4:6], sc0[:, k, 1:2], None, ALU.mult).then_inc(D_z.sem, 1)

            def d_z5(t, b, m):
                k = m % 2
                dve.wait_ge(D_z.sem, D_z.upto(t, 5))
                v.tensor_scalar(xc[:, k, :], xc[:, k, :], sc0[:, k, 2:3], MAGIC, ALU.mult, ALU.add).then_inc(D_z.sem, 1)

            def d_z6(t, b, m):
                k = m % 2
                dve.wait_ge(D_z.sem, D_z.upto(t, 6))
                if not isinstance(t, int) or t >= 2:
                    dve.wait_ge(D_t.sem, D_t.upto(t - 2))
                v.tensor_scalar(zq[:, k, :], xc[:, k, :], MAGIC + 127.0, MAGIC, ALU.min, ALU.subtract).then_inc(D_z.sem, 1)

            def layer_stats(S):
                def first(t, b, m):
                    v.bn_stats(st[:, m % 2, 0:6], xs[:, one(t), :]).then_inc(S.sem, 1)

                def second(t, b, m):
                    wait_apart(dve, S.sem, S.upto(t, 1))
                    v.bn_aggr(mv[:, m % 2, :], st[:, m % 2, 0:6]).then_inc(S.sem, 1)

                def third(t, b, m):
                    dve.wait_ge(S.sem, S.upto(t, 2))
                    v.tensor_scalar(small[:, m % 2, 0:1], mv[:, m % 2, 1:2], EPS, None, ALU.add).then_inc(S.sem, 1)
                return first, second, third
            dve.wait_ge(C_x.sem, NT)
            dve.wait_ge(Q_r.sem, NT)
            d_s1, d_s2, d_s3 = layer_stats(D_s)
            phases = [(0, NT, 4, [(1, d_z1), (0, d_s1), (3, d_h1), (1, d_z2), (0, d_s2), (3, d_h2), (1, d_z3), (0, d_s3), (3, d_h3),
                         (1, d_z4), (3, d_h4), (1, d_z5), (6, d_x), (1, d_z6)])]

            def layernorm_phase(S):
                def ef_x(t, b, m):
                    dve.wait_ge(S["b"].sem, S["b"].upto(t))
                    dve.wait_ge(S["m"].sem, S["m"].upto(t))
                    v.scalar_tensor_tensor(xs[:, one(t), :], banks(2 + m % 2)[:, 0:D].unsqueeze(1), 1.0 / WS, xs[:, one(t), :],
                                           ALU.mult, ALU.add).then_inc(S["x"].sem, 1)

                def ef_lo(t, b, m):
                    dve.wait_ge(S["hi"].sem, S["hi"].upto(t))
                    v.tensor_tensor(zT[:, LO, :, tile_cols(t)], banks(m % 2)[:, 0:D].rearrange("p (k n) -> p k n", k=KC),
                                    zT[:, HI, :, tile_cols(t)], ALU.subtract).then_inc(S["lo"].sem, 1)

                def ef_z(t, b, m):
                    k = m % 2
                    if not isinstance(t, int) or t >= 2 or S is EF[1]:
                        dve.wait_ge(S["t"].sem, S["t"].upto(t - 2))
                    dve.wait_ge(S["r"].sem, S["r"].upto(t))
                    v.tensor_scalar(z[:, k, :], xs[:, one(t), :].rearrange("p o d -> p (o d)"), mv[:, k, 0:1],
                                    small[:, k, 1:2], ALU.subtract, ALU.mult).then_inc(S["z"].sem, 1)

                def f_l(t, b, m):
                    dve.wait_ge(S["m"].sem, S["m"].upto(t))
                    v.tensor_scalar(logits[:, one(t), :], banks(2 + m % 2)[:, 0:E].unsqueeze(1), 1.0 / WS, None,
                                    ALU.mult).then_inc(f_log.sem, 1)
                def ef_order(z_stage, last):
                    s1, s2, s3 = layer_stats(S["s"])
                    written = D_x if S is EF[0] else EF[0]["x"]

                    def ready(t, b, m):
                        wait_apart(dve, written.sem, written.upto(t))
                    return [(0, ready), (0, s1), (5, last), (0, s2), (3, ef_lo), (0, s3), (1, z_stage)]
                if S is EF[0]:
                    phases.append((NT, NT, 4, ef_order(ef_z, ef_x)))
                else:
                    def ef_z2(t, b, m):
                        if not isinstance(t, int) or t >= 2:
                            dve.wait_ge(f_row.sem, f_row.upto(t - 2))
                        ef_z(t, b, m)
                    phases.append((NT, NT, 4, ef_order(ef_z2, f_l)))
            for layer in EF:
                layernorm_phase(layer)
            chained(dve, phases)

            gn = [0]

            def g(ins):
                gn[0] += 1
                ins.then_inc(g_chain, 1)
                dve.wait_ge(g_chain, gn[0])

            def over_e(a):
                return a.unsqueeze(2).to_broadcast([P, NT, E])

            def over_t(a):
                return a.unsqueeze(1).to_broadcast([P, NT, E])
            sh, eq, oh1, oh2, sl = (r3[:, k] for k in range(5))
            m1, b1, m2, b2, zs, e2, rz, p2, w1, w2, sl1, sl2 = (r2[:, k] for k in range(12))
            dve.wait_ge(f_log.sem, NT)
            dve.wait_ge(s_late, 4)
            g(v.tensor_reduce(m1, logits[:], X, ALU.max))
            g(v.tensor_tensor(sh, logits[:], over_e(m1), ALU.subtract))
            g(v.tensor_scalar(eq, sh, 0.0, None, ALU.is_equal))
            g(v.tensor_tensor(eq, eq, over_t(w8[:]), ALU.mult))
            g(v.tensor_reduce(b1, eq, X, ALU.max))
            g(v.tensor_tensor(oh1, over_t(w8[:]), over_e(b1), ALU.is_equal))
            g(v.scalar_tensor_tensor(sl, oh1, -1e30, sh, ALU.mult, ALU.add))
            g(v.tensor_reduce(m2, sl, X, ALU.max))
            g(v.tensor_tensor(eq, sl, over_e(m2), ALU.is_equal))
            g(v.tensor_tensor(eq, eq, over_t(w8[:]), ALU.mult))
            g(v.tensor_reduce(b2, eq, X, ALU.max))
            g(v.tensor_tensor(oh2, over_t(w8[:]), over_e(b2), ALU.is_equal))
            g(v.tensor_tensor(A16[:], oh1, oh2, ALU.add))
            n8, t8, i8, s8, o8 = (r1[:, k] for k in range(5))
            dve.wait_ge(g_pe, 1)
            g(v.tensor_scalar(n8, banks(7)[:, NT * E:(NT + 1) * E], 1.0 / P, (P - 1.0) / P - 0.5 + 0.5 / P, ALU.mult, ALU.add))
            g(v.tensor_scalar(n8, n8, MAGIC, None, ALU.add))
            g(v.tensor_scalar(t8, n8, MAGIC, None, ALU.subtract))
            g(v.tensor_tensor_scan(i8, ones[:, 0:E], t8, 0.0, ALU.mult, ALU.add))
            g(v.tensor_tensor(s8, i8, t8, ALU.subtract))
            g(v.tensor_scalar(o8, s8, float(P), None, ALU.mult))
            g(v.tensor_tensor(sl, banks(7)[:, 0:NT * E].rearrange("p (t e) -> p t e", e=E), over_t(o8), ALU.add))
            g(v.tensor_tensor(oh1, oh1, sl, ALU.mult))
            g(v.tensor_tensor(oh2, oh2, sl, ALU.mult))
            g(v.tensor_reduce(sl1, oh1, X, ALU.add))
            g(v.tensor_reduce(sl2, oh2, X, ALU.add))
            v.tensor_copy(idx[:, 0, :], sl1).then_inc(routed, 1)
            v.tensor_copy(idx[:, 1, :], sl2).then_inc(routed, 1)
            g(v.tensor_tensor(tcmp[:], tile_no[:].unsqueeze(2).to_broadcast([P, NS, E - 1]),
                              s8[:, 1:E].unsqueeze(1).to_broadcast([P, NS, E - 1]), ALU.is_ge))
            g(v.tensor_reduce(tsum[:], tcmp[:], X, ALU.add))
            v.tensor_copy(tile_e[:], tsum[:]).then_inc(routed, 1)
            def run(R, count, first_tile, experts, more=()):
                d = 1 if experts else 0

                def out_(t, b, m):
                    k = m % 2
                    dve.wait_ge(R["y"].sem, R["y"].upto(t))
                    if experts:
                        if not isinstance(t, int) or t >= 2:
                            dve.wait_ge(s_ys[k], 16 * ((t - k) // 2) if isinstance(t, int) else 16 * (2 * b + (m - k) // 2))
                        v.tensor_scalar(yb[:, k, :], banks(6)[:, 0:D], 1.0 / WS, None, ALU.mult).then_inc(R["o"].sem, 1)
                    else:
                        at = t + first_tile
                        v.scalar_tensor_tensor(xs[:, one(at), :], banks(6)[:, 0:D].unsqueeze(1), 1.0 / WS,
                                               xs[:, one(at), :], ALU.mult, ALU.add).then_inc(R["o"].sem, 1)

                def lo(t, b, m):
                    k = m % 2
                    dve.wait_ge(R["hi"].sem, R["hi"].upto(t))
                    v.tensor_tensor(ehT[:, k, LO, :], banks(4 + k), ehT[:, k, HI, :], ALU.subtract).then_inc(R["lo"].sem, 1)

                def h(t, b, m):
                    k = m % 2
                    dve.wait_ge(R["a"].sem, R["a"].upto(t))
                    v.scalar_tensor_tensor(eh[:, k, :], banks(2 + k), 1.0 / WS, eg[:, k, :], ALU.mult,
                                           ALU.mult).then_inc(R["h"].sem, 1)

                def copy_x(t, b, m):
                    dve.wait_ge(x_t.sem, x_t.upto(t))
                    v.tensor_copy(xgT[:, m % 2, :], banks(7).bitcast(f16)[:, 0:2 * D]).then_inc(x_c.sem, 1)

                stages = [(2 + d, out_), (1 + d, lo), (d, h)]
                if experts:
                    stages.append((0, copy_x))
                return 0, count, 4, stages + list(more)

            def split_part(t, b, m):
                dve.wait_ge(x_hi.sem, x_hi.upto(t))
                v.scalar_tensor_tensor(wpart[:, one(t + GD), LO, :], part_in[:, m, :].unsqueeze(1), WS,
                                       wpart[:, one(t + GD), HI, :], ALU.mult, ALU.subtract).then_inc(x_lo.sem, 1)

            def split_parts(t, b, m):
                for part in range(t * GS // (NA - 2), min(GS, (t + 1) * GS // (NA - 2))):
                    split_part(part, part // 4, part % 4)

            def two_weights(t, b, m):
                if t != NA - 2:
                    return
                dve.wait_ge(g_act, 2)
                g(v.tensor_reduce(zs, r3[:, 1], X, ALU.add))
                g(v.reciprocal(rz, zs))
                g(v.tensor_tensor(p2, e2, rz, ALU.mult))
                g(v.tensor_tensor(zs, rz, p2, ALU.add))
                g(v.tensor_scalar(zs, zs, 1e-20, None, ALU.add))
                g(v.reciprocal(zs, zs))
                g(v.tensor_tensor(w1, rz, zs, ALU.mult))
                g(v.tensor_tensor(w2, p2, zs, ALU.mult))

            def last_part(t, b, m):
                if isinstance(t, int) and t == 0:
                    split_part(GS, GS // 4, GS % 4)

            def combine(t, b, m):
                if t == 0:
                    dve.wait_ge(RUNS["sa"]["o"].sem, NA)
                for c in range(t * NT // NB, (t + 1) * NT // NB):
                    dve.wait_ge(s_yg[c % YR], 32 * (c // YR + 1))
                    if c >= NA:
                        dve.wait_ge(RUNS["sb"]["o"].sem, RUNS["sb"]["o"].upto(c - NA))
                    v.scalar_tensor_tensor(xs[:, one(c), :], yg[:, c % YR, 0, :].unsqueeze(1), r2[:, 8, one(c)], xs[:, one(c), :],
                                           ALU.mult, ALU.add).then_inc(comb.sem, 1)
                    dve.wait_ge(comb.sem, comb.upto(c, 1))
                    v.scalar_tensor_tensor(xs[:, one(c), :], yg[:, c % YR, 1, :].unsqueeze(1), r2[:, 9, one(c)], xs[:, one(c), :],
                                           ALU.mult, ALU.add).then_inc(comb.sem, 1)
            chained(dve, [run(RUNS["sa"], NA, 0, False, [(0, split_parts), (0, two_weights)]),
                          (NA,) + run(RUNS["ex"], NS, 0, True, [(0, last_part)])[1:],
                          (NS + 1,) + run(RUNS["sb"], NB, NA, False, [(3, combine)])[1:]])

        @block.scalar
        def _(act):
            with nc.allow_non_contiguous_dma(reason="a few short vectors, features onto partitions; the router's rows"):
                for k, vec in enumerate((tab_g, tab_b, vid_g, vid_b)):
                    act.dma_start(vecs[:, k, :], vec.rearrange("(c p) -> p c", p=P)).then_inc(s_tab, 16)
                for k, vec in enumerate((q_g, q_b, k_g, k_b)):
                    act.dma_start(hvec[:, k, :], vec.rearrange("(c p) -> p c", p=P)).then_inc(s_vec, 16)
                act.dma_start(wl_raw[:, 0:2 * D * KC].rearrange("p (k n) -> p k n", n=2 * D),
                              W_l1.rearrange("(k p) n -> p k n", p=P)).then_inc(s_l1, 16)
                act.dma_start(wr_raw, Wr.rearrange("(k p) n -> p k n", p=P)).then_inc(s_l1, 16)
            for dst, vec in ((bl_b, b_l1), (bo_b, bo)):
                act.dma_start(dst[:], vec.rearrange("(o d) -> o d", o=1).to_broadcast([P, D])).then_inc(s_bias, 16)

            def copy(dst, src, scale=1.0):
                return nc.scalar.activation(dst, src, ACT.Copy, scale=scale)

            act.wait_ge(s_tab, 64)
            act.wait_ge(ctx_t, 1)
            for k in range(KC):
                nc.scalar.activation(cf[:, k, :], banks(0)[:, k * CT * P:(k + 1) * CT * P], ACT.Identity,
                                     bias=vecs[:, 1, k:k + 1], scale=vecs[:, 0, k:k + 1]).then_inc(cT_ready, 1)
            act.wait_ge(cT_ready, KC)
            copy(cTk[:, HI, :, :], cf[:]).then_inc(cT_ready, 1)
            for i, w in enumerate((wk, wv, wq, wo)):
                act.wait_ge(s_w[i], 16)
                copy(w[:, HI, :], att_w(i), WS).then_inc(split_hi.sem, 1)
            act.wait_ge(l1_t, 1)
            copy(wl1[:, HI, :, :], banks(4, 2).rearrange("p (k e) -> p k e", e=D), WS).then_inc(l1_hi, 1)
            copy(wr[:, HI, :, :], wr_raw, WS).then_inc(l1_hi, 1)
            for c in range(CT):
                act.wait_ge(k_bias, c + 1)
                nc.scalar.activation(nk[:, c, :], banks(2 * c, 2)[:, 0:INNER], ACT.Identity,
                                     bias=small[:, c, 7:8], scale=small[:, c, 6:7]).then_inc(k_norm, 1)
            act.wait_ge(s_fill2, 1)
            act.dma_start(xrows.rearrange("(i p) d -> p i d", p=P),
                          zeros[:].unsqueeze(1).to_broadcast([P, NS, 2 * D])).then_inc(s_zero, 16)

            def a_f(t, b, m):
                act.wait_ge(A_t.sem, A_t.upto(t))
                if not isinstance(t, int) or t >= 2:
                    act.wait_ge(A_lo.sem, A_lo.upto(t - 2))
                for k in range(KC):
                    nc.scalar.activation(zf[:, m, k, :], banks(3 + m)[:, k * 2 * P:(k + 1) * 2 * P], ACT.Identity,
                                         bias=vecs[:, 3, k:k + 1], scale=vecs[:, 2, k:k + 1]).then_inc(A_f.sem, 1)

            def a_hi(t, b, m):
                wait_apart(act, A_f.sem, A_f.upto(t))
                copy(zT[:, HI, :, bass.ds(t * 2 * P, 2 * P)], zf[:, m]).then_inc(A_hi.sem, 1)
            skewed(act, [(3, a_hi), (2, a_f)], NT // 2, 2)

            act.wait_ge(s_const, 8)
            act.wait_ge(v_mm, 1)
            for k in range(2):
                h = slice(k * DH, (k + 1) * DH)
                copy(VTbd[h, HI, :, :, k * DH:(k + 1) * DH], vT_of(h)).then_inc(VK_hi, 1)

            def q_bias_high(r):
                act.wait_ge(qb_mm, r + 1)
                copy(SB_part(slice(0, P), r), qb_of(slice(0, P), r)).then_inc(VS_hi, 1)
            q_bias_high(0)
            act.wait_ge(kfq_ready, (CT + 1) * QC)
            for k in range(2):
                h = slice(k * DH, (k + 1) * DH)
                copy(Kbd[h, HI, :, :, k * DH:(k + 1) * DH],
                     kq[h, :, :].rearrange("p q (b l) -> p b q l", l=LC)).then_inc(VK_hi, 1)
            act.wait_ge(s_tern, 48)
            for i in range(3):
                if i >= 1:
                    act.wait_ge(q_sum, i)
                nc.scalar.activation(wk[:].rearrange("p s n -> p (s n)")[:, 0:WF], ffn_w[:, i, :], ACT.Abs,
                                     accum_out=wsc[:, i:i + 1]).then_inc(q_sum, 1)
            for r in range(3):
                act.wait_ge(VW_mm, r + 1)
                copy(VW_part(HI, r), banks(4 * (r % 2), 4), 1.0 / WS).then_inc(VS_hi, 1)
            q_bias_high(1)

            def b_n(t, b, m):
                if not isinstance(t, int) or t >= 2:
                    act.wait_ge(B_t.sem, B_t.upto(t - 2))
                act.wait_ge(B_s.sem, B_s.upto(t))
                nc.scalar.activation(nq[:, m, :], banks(2 * m, 2)[:, 0:INNER], ACT.Identity,
                                     bias=small[:, m, 3:4], scale=small[:, m, 2:3]).then_inc(B_n.sem, 1)

            def b_hi(t, b, m):
                wait_apart(act, B_t.sem, B_t.upto(t))
                copy(qT[:, HI, :, tile_cols(t)],
                     banks(4 + 2 * m, 2)[:, 0:INNER].rearrange("p (q n) -> p q n", n=P)).then_inc(B_hi.sem, 1)
            B_stages = [(3, b_hi), (1, b_n)]

            def c_phi(t, b, m):
                act.wait_ge(C_t.sem, C_t.upto(t))
                if not isinstance(t, int) or t >= 2:
                    act.wait_ge(C_w.sem, C_w.upto(t - 2))
                copy(pT[:, m % 2, HI, :], banks(2, 2)[:, 0:INNER]).then_inc(C_phi.sem, 1)

            def c_e(t, b, m):
                act.wait_ge(C_m.sem, C_m.upto(t))
                nc.scalar.activation(sm[:, m % 2, :], sm[:, m % 2, :], ACT.Exp, scale=DH ** -0.5).then_inc(C_e.sem, 1)

            def q_r(t, b, m):
                k = m % 2
                act.wait_ge(Q_c.sem, Q_c.upto(t))
                if not isinstance(t, int) or t >= 2:
                    act.wait_ge(Q_w.sem, Q_w.upto(t - 2))
                nc.scalar.activation(qr[:, k], qy[:, k], ACT.Copy, bias=MAGIC).then_inc(Q_r.sem, 1)

            def q_w(t, b, m):
                k = m % 2
                act.wait_ge(Q_r.sem, Q_r.upto(t))
                if not isinstance(t, int) or t >= 2:
                    act.wait_ge(Q_t.sem, Q_t.upto(t - 2))
                nc.scalar.activation(w16[:, k], qr[:, k], ACT.Copy, bias=-MAGIC).then_inc(Q_w.sem, 1)

            def q_o(t, b, m):
                wait_apart(act, Q_t.sem, Q_t.upto(t))
                copy(wT[:, :, one(t), :], banks(6 + m % 2).bitcast(f16)[:, 0:3 * P].rearrange(
                    "p (i o n) -> p i o n", i=3, o=1)).then_inc(Q_o.sem, 1)
            chained(act, [(0, NT, 2, B_stages), (NT, NT, 4, [(2, c_phi), (4, q_o), (3, q_w), (2, q_r), (0, c_e)])])

            def d_c2(t, b, m):
                act.wait_ge(D_u.sem, D_u.upto(t))
                copy(hqT[:, m % 2, :], banks(7).bitcast(f16)).then_inc(D_v.sem, 1)

            def d_a(t, b, m):
                act.wait_ge(D_g.sem, D_g.upto(t))
                nc.scalar.activation(hg[:], banks(0, 2), ACT.Silu, scale=sc0[:, m % 2, 3:4]).then_inc(D_a.sem, 1)

            def d_1(t, b, m):
                act.wait_ge(D_h.sem, D_h.upto(t))
                nc.scalar.activation(hh[:, m % 2, :], hh[:, m % 2, :], ACT.Copy, bias=MAGIC, scale=sc1[:, m, 2:3]).then_inc(D_1.sem, 1)

            def d_q(t, b, m):
                act.wait_ge(D_1.sem, D_1.upto(t))
                if not isinstance(t, int) or t >= 1:
                    act.wait_ge(D_u.sem, D_u.upto(t - 1))
                nc.scalar.activation(hq[:], hh[:, m % 2, :], ACT.Copy, bias=-MAGIC).then_inc(D_2.sem, 1)

            def d_c(t, b, m):
                act.wait_ge(D_t.sem, D_t.upto(t))
                copy(zqT[:, m % 2, :], banks(4 + m % 2).bitcast(f16)[:, 0:D]).then_inc(D_c.sem, 1)

            def x_h(t, b, m):
                wait_apart(act, X_m.sem, X_m.upto(t))
                copy(wpart[:, one(t), HI, :], part_in[:, m, :].unsqueeze(1)).then_inc(X_hi.sem, 1)
            act.wait_ge(C_x.sem, NT)
            phases = [(0, NT, 4, [(4, d_1), (4, d_q), (5, d_c2), (2, x_h), (2, d_a), (1, d_c)])]
            def layernorm_phase(S):
                def ef_hi(t, b, m):
                    wait_apart(act, S["t"].sem, S["t"].upto(t))
                    copy(zT[:, HI, :, tile_cols(t)],
                         banks(m % 2)[:, 0:D].rearrange("p (k n) -> p k n", k=KC)).then_inc(S["hi"].sem, 1)

                def f_rh(t, b, m):
                    if isinstance(t, int) and t == 0:
                        act.wait_ge(s_zero, 16)
                        act.wait_ge(EF[0]["b"].sem, NT)
                    if isinstance(t, int) and t == 2:
                        act.wait_ge(EF[0]["m"].sem, NT)
                    wait_apart(act, S["z"].sem, S["z"].upto(t))
                    copy(zrow[:, one(t), 0:D], z[:, m % 2, :].unsqueeze(1)).then_inc(f_row_hi.sem, 1)
                phases.append((NT, NT, 4, [(2, ef_hi)]) if S is EF[0] else (NT, NT, 4, [(2, ef_hi), (1, f_rh)]))
            for layer in EF:
                layernorm_phase(layer)
            chained(act, phases)

            act.wait_ge(g_chain, 10)
            nc.scalar.activation(r2[:, 5], r2[:, 2], ACT.Exp).then_inc(g_act, 1)
            act.wait_ge(g_chain, 13)
            nc.scalar.activation(r3[:, 1], r3[:, 0], ACT.Exp).then_inc(g_act, 1)

            def run(R, count, first_tile, experts, more=()):
                d = 1 if experts else 0

                def hi(t, b, m):
                    k = m % 2
                    act.wait_ge(R["t"].sem, R["t"].upto(t))
                    if not isinstance(t, int) or t >= 2:
                        act.wait_ge(R["y"].sem, R["y"].upto(t - 2))
                    copy(ehT[:, k, HI, :], banks(4 + k)).then_inc(R["hi"].sem, 1)

                def silu(t, b, m):
                    k = m % 2
                    act.wait_ge(R["g"].sem, R["g"].upto(t))
                    nc.scalar.activation(eg[:, k, :], banks(k), ACT.Silu, scale=1.0 / WS).then_inc(R["a"].sem, 1)

                return 0, count, 4, [(1 + d, hi), (d, silu)] + list(more)

            def split_part(t, b, m):
                wait_apart(act, s_part[m], 16 * (GD // 4 + b + 1))
                copy(wpart[:, one(t + GD), HI, :], part_in[:, m, :].unsqueeze(1), WS).then_inc(x_hi.sem, 1)

            def split_parts(t, b, m):
                for part in range(t * GS // (NA - 2), min(GS, (t + 1) * GS // (NA - 2))):
                    split_part(part, part // 4, part % 4)

            def last_part(t, b, m):
                if isinstance(t, int) and t == 0:
                    act.wait_ge(s_scatter, 16 * TOP * NT)
                    split_part(GS, GS // 4, GS % 4)
            chained(act, [run(RUNS["sa"], NA, 0, False, [(0, split_parts)]),
                          (NA,) + run(RUNS["ex"], NS, 0, True, [(0, last_part)])[1:], (NS + 1,) + run(RUNS["sb"], NB, NA, False)[1:]])

        @block.tensor
        def _(pe):
            def mm(dst, a, w, start=True, stop=True):
                return nc.tensor.matmul(dst, a, w, start=start, stop=stop)

            def product(dst, parts):
                for n, (ah, al, wh, wl) in enumerate(parts):
                    mm(dst, ah, wh, start=(n == 0), stop=False)
                    mm(dst, ah, wl, start=False, stop=False)
                    last = mm(dst, al, wh, start=False, stop=(n == len(parts) - 1))
                return last

            def transposes(dst, src, n, idn):
                for k in range(n):
                    last = nc.tensor.transpose(dst[:, k * P:(k + 1) * P], src[:, k * P:(k + 1) * P], idn[:])
                return last

            pe.wait_ge(s_const, 5)
            pe.wait_ge(ctx_z, CT)
            for c in range(CT):
                for k in range(KC):
                    at = k * CT * P + c * P
                    nc.tensor.transpose(banks(0)[:, at:at + P], z[:, c, k * P:(k + 1) * P], ident[:])
                    last = nc.tensor.transpose(banks(1)[:, at:at + P], cx[:, c, k * P:(k + 1) * P], ident[:])
            last.then_inc(ctx_t, 1)
            def wide(w, hl):
                return w[:, hl, :].rearrange("p (k n) -> p k n", k=KC)

            def project(dst, a_of, w):
                for lo, hi in ((0, BANK), (BANK, INNER)):
                    last = product(dst[:, lo:hi], [(a_of(HI, k), a_of(LO, k), wide(w, HI)[:, k, lo:hi],
                                                    wide(w, LO)[:, k, lo:hi]) for k in range(KC)])
                return last
            pe.wait_ge(ctx_sum, 1)
            pe.wait_ge(cT_lo, 1)
            pe.wait_ge(split_lo.sem, 1)
            for c in range(CT):
                project(banks(2 * c, 2), lambda hl, k: cTk[:, hl, k, c * P:(c + 1) * P], wk).then_inc(k_mm, 1)
            pe.wait_ge(s_l1, 32)
            for k in range(2 * KC):
                for e in range(KC):
                    last = nc.tensor.transpose(banks(4, 2)[:, k * D + e * P:k * D + (e + 1) * P],
                                               wl_raw[:, e * 2 * D + k * P:e * 2 * D + (k + 1) * P], ident[:])
            last.then_inc(l1_t, 1)
            pe.wait_ge(l1_ready, 4)
            for b in range(B):
                last = product(banks(6, 2)[:, b * D:(b + 1) * D],
                               [(crep[:, HI, k, b, :], crep[:, LO, k, b, :], wl1[:, HI, KC + k, :], wl1[:, LO, KC + k, :])
                                for k in range(KC)])
            last.then_inc(bias_mm, 1)
            for c in range(CT):
                pe.wait_ge(k_norm, c + 1)
                if c == 1:
                    pe.wait_ge(bias_done, 1)
                transposes(banks(4 + 2 * c, 2), nk[:, c, :], QC, ident).then_inc(k_t, 1)
            pe.wait_ge(split_lo.sem, 2)
            for c in range(QC):
                last = product(banks(0, 3)[:, c * CT * P:(c + 1) * CT * P],
                               [(wide(wv, HI)[:, k, c * P:(c + 1) * P], wide(wv, LO)[:, k, c * P:(c + 1) * P],
                                 cTk[:, HI, k, :], cTk[:, LO, k, :]) for k in range(KC)])
            last.then_inc(v_mm, 1)

            def q_bias(r):
                for hd in range(H // 2):
                    h = r * (H // 2) + hd
                    last = mm(banks((5, 4)[r], 3)[:, hd * B * LC:(hd + 1) * B * LC], qbm[:, h // 2, h % 2, :], kf[:, h // 2, :])
                last.then_inc(qb_mm, 1)
            pe.wait_ge(qb_ready, 2)
            pe.wait_ge(kfq_ready, CT * QC)
            q_bias(0)

            def a_t(t, b, m):
                pe.wait_ge(A_z.sem, A_z.upto(t))
                if not isinstance(t, int) or t >= 2:
                    pe.wait_ge(A_f.sem, A_f.upto(t - 2))
                for i in range(2):
                    for k in range(KC):
                        last = nc.tensor.transpose(banks(3 + m)[:, (k * 2 + i) * P:(k * 2 + i + 1) * P],
                                                   za[:, m, i, k * P:(k + 1) * P], ident[:])
                last.then_inc(A_t.sem, 1)
            skewed(pe, [(1, a_t)], NT // 2, 2)

            pe.wait_ge(VK_lo, 2)
            pe.wait_ge(split_lo.sem, 4)
            for r in range(3):
                if r >= 1:
                    pe.wait_ge(VS_lo, r)
                for n in range(8):
                    b, c = divmod(8 * r + n, QC)
                    last = product(banks(4 * (r % 2), 4)[:, n * D:(n + 1) * D],
                                   [(VTbd[:, HI, b, c, :], VTbd[:, LO, b, c, :],
                                     wo[:, HI, c * D:(c + 1) * D], wo[:, LO, c * D:(c + 1) * D])])
                last.then_inc(VW_mm, 1)
            pe.wait_ge(VS_lo, 3)
            q_bias(1)
            pe.wait_ge(q_sum, 3)
            mm(banks(7)[:, 0:3], ones[:], wsc[:, 0:3]).then_inc(q_mean, 1)

            pe.wait_ge(split_lo.sem, 3)
            pe.wait_ge(A_lo.sem, NT // 2)
            pe.wait_ge(VS_lo, 5)

            def b_q(t, b, m):
                if not isinstance(t, int) or t >= 2:
                    wait_apart(pe, B_n.sem, B_n.upto(t - 2))
                project(banks(2 * m, 2), lambda hl, k: zT[:, hl, k, tile_cols(t)], wq).then_inc(B_q.sem, 1)

            def b_t(t, b, m):
                pe.wait_ge(B_n.sem, B_n.upto(t))
                if not isinstance(t, int) or t >= 2:
                    pe.wait_ge(B_lo.sem, B_lo.upto(t - 2))
                transposes(banks(4 + 2 * m, 2), nq[:, m, :], QC, ident).then_inc(B_t.sem, 1)
            B_stages = [(3, b_t), (0, b_q)]

            def c_w(t, b, m):
                if isinstance(t, int) and t == 0:
                    pe.wait_ge(B_lo.sem, B_lo.upto(NT - 1))
                wait_apart(pe, C_plo.sem, C_plo.upto(t))
                if not isinstance(t, int) or t >= 2:
                    wait_apart(pe, C_x.sem, C_x.upto(t - 2))
                product(banks(4 + m % 2)[:, 0:D], [(pT[:, m % 2, HI, c * P:(c + 1) * P], pT[:, m % 2, LO, c * P:(c + 1) * P],
                                                    VW[:, HI, one(b), c, :], VW[:, LO, one(b), c, :])
                                                   for c in range(QC)]).then_inc(C_w.sem, 1)

            def q_t(t, b, m):
                pe.wait_ge(Q_w.sem, Q_w.upto(t))
                if not isinstance(t, int) or t >= 2:
                    pe.wait_ge(Q_o.sem, Q_o.upto(t - 2))
                transposes(banks(6 + m % 2).bitcast(f16), w16[:, m % 2].rearrange("p i n -> p (i n)"), 3,
                           ident16).then_inc(Q_t.sem, 1)

            def c_t(t, b, m):
                if isinstance(t, int) and t == 0:
                    pe.wait_ge(B_n.sem, B_n.upto(NT - 1))
                pe.wait_ge(C_p.sem, C_p.upto(t))
                if not isinstance(t, int) or t >= 1:
                    pe.wait_ge(C_plo.sem, C_plo.upto(t - 1))
                transposes(banks(2, 2), sm[:, m % 2, :], QC, ident).then_inc(C_t.sem, 1)

            def c_s(t, b, m):
                if isinstance(t, int) and t == 0:
                    pe.wait_ge(B_n.sem, B_n.upto(NT - 2))
                    pe.wait_ge(B_lo.sem, B_lo.upto(3))
                if isinstance(t, int) and t == 4:
                    pe.wait_ge(B_lo.sem, B_lo.upto(NT - 1))
                if not isinstance(t, int) or t >= 1:
                    wait_apart(pe, C_m.sem, C_m.upto(t - 1))
                for lo, hi in ((0, BANK), (BANK, INNER)):
                    mm(banks(0, 2)[:, lo:hi], ones64[:], SB[:, one(b), lo:hi], start=True, stop=False)
                    for c in range(lo // P, hi // P):
                        dst = banks(0, 2)[:, c * P:(c + 1) * P]
                        mm(dst, qT[:, HI, c, tile_cols(t)], Kbd[:, HI, one(b), c, :], start=False, stop=False)
                        mm(dst, qT[:, HI, c, tile_cols(t)], Kbd[:, LO, one(b), c, :], start=False, stop=False)
                        last = mm(dst, qT[:, LO, c, tile_cols(t)], Kbd[:, HI, one(b), c, :], start=False,
                                  stop=(c == hi // P - 1))
                last.then_inc(C_s.sem, 1)
            chained(pe, [(0, NT, 2, B_stages), (NT, NT, 4, [(2, c_t), (0, c_s), (4, q_t), (3, c_w)])])

            pe.wait_ge(C_x.sem, NT)
            pe.wait_ge(Q_o.sem, NT)

            def d_y(t, b, m):
                pe.wait_ge(D_v.sem, D_v.upto(t))
                if not isinstance(t, int) or t >= 1:
                    pe.wait_ge(D_x.sem, D_x.upto(t - 1))
                for c in range(IC):
                    last = mm(banks(6)[:, 0:D].rearrange("p (k n) -> p k n", n=P), hqT[:, m % 2, c * P:(c + 1) * P], down_T[:, c],
                              start=(c == 0), stop=(c == IC - 1))
                last.then_inc(D_y.sem, 1)

            def d_u(t, b, m):
                pe.wait_ge(D_2.sem, D_2.upto(t))
                if not isinstance(t, int) or t >= 1:
                    pe.wait_ge(D_v.sem, D_v.upto(t - 1))
                transposes(banks(7).bitcast(f16), hq, IC, ident16).then_inc(D_u.sem, 1)

            def d_g(t, b, m):
                pe.wait_ge(D_c.sem, D_c.upto(t))
                if not isinstance(t, int) or t >= 1:
                    pe.wait_ge(D_h.sem, D_h.upto(t - 1, 1))
                for g in range(2):
                    for half in range(FI // BANK):
                        for k in range(KC):
                            last = mm(banks(2 * g + half).rearrange("p (c n) -> p c n", n=P), zqT[:, m % 2, k * P:(k + 1) * P],
                                      gate_up_T[:, g, k, half * BANK // P:(half + 1) * BANK // P],
                                      start=(k == 0), stop=(k == KC - 1))
                last.then_inc(D_g.sem, 1)

            def d_t(t, b, m):
                pe.wait_ge(D_z.sem, D_z.upto(t))
                if not isinstance(t, int) or t >= 2:
                    pe.wait_ge(D_c.sem, D_c.upto(t - 2))
                transposes(banks(4 + m % 2).bitcast(f16), zq[:, m % 2, :], KC, ident16).then_inc(D_t.sem, 1)
            phases = [(0, NT, 4, [(5, d_u), (6, d_y), (2, d_g), (1, d_t)])]

            def layernorm_phase(S):
                def e_m(t, b, m):
                    wait_apart(pe, S["lo"].sem, S["lo"].upto(t))
                    if not isinstance(t, int) or t >= 2:
                        wait_apart(pe, S["x"].sem, S["x"].upto(t - 2))
                    product(banks(2 + m % 2)[:, 0:D], [(zT[:, HI, k, tile_cols(t)], zT[:, LO, k, tile_cols(t)],
                                                        wl1[:, HI, k, :], wl1[:, LO, k, :])
                                                       for k in range(KC)]).then_inc(S["m"].sem, 1)

                def ef_t(t, b, m):
                    pe.wait_ge(S["z"].sem, S["z"].upto(t))
                    if isinstance(t, int) and t == 0 and S is EF[0]:
                        pe.wait_ge(D_h.sem, D_h.upto(NT - 1, 1))
                    if not isinstance(t, int) or t >= 2 or S is EF[1]:
                        pe.wait_ge(S["lo"].sem, S["lo"].upto(t - 2))
                    transposes(banks(m % 2), z[:, m % 2, :], KC, ident).then_inc(S["t"].sem, 1)

                def f_m(t, b, m):
                    wait_apart(pe, S["lo"].sem, S["lo"].upto(t))
                    if isinstance(t, int) and t < 2:
                        wait_apart(pe, EF[0]["x"].sem, EF[0]["x"].upto(NT - 2 + t))
                    if not isinstance(t, int) or t >= 2:
                        wait_apart(pe, f_log.sem, f_log.upto(t - 2))
                    product(banks(2 + m % 2)[:, 0:E], [(zT[:, HI, k, tile_cols(t)], zT[:, LO, k, tile_cols(t)],
                                                        wr[:, HI, k, :], wr[:, LO, k, :])
                                                       for k in range(KC)]).then_inc(S["m"].sem, 1)
                phases.append((NT, NT, 4, [(2, ef_t), (4, e_m)]) if S is EF[0] else (NT, NT, 4, [(2, ef_t), (4, f_m)]))
            for layer in EF:
                layernorm_phase(layer)
            chained(pe, phases)

            pe.wait_ge(g_chain, 13)
            pe.wait_ge(s_fill2, 4)
            A = A16[:].rearrange("p t e -> p (t e)")
            mm(banks(7)[:, 0:NT * E], before16[:], A, start=True, stop=False)
            for k in range(1, NT):
                mm(banks(7)[:, k * E:NT * E], ones16[:], A[:, 0:(NT - k) * E], start=False, stop=(k == NT - 1))
            for k in range(NT):
                last = mm(banks(7)[:, NT * E:(NT + 1) * E], ones16[:], A[:, k * E:(k + 1) * E], start=(k == 0), stop=(k == NT - 1))
            last.then_inc(g_pe, 1)

            def run(R, count, first_tile, experts, a_of):
                d = 1 if experts else 0
                last_run, last_count = ("sa", NA) if experts else ("ex", NS)

                def expert(t):
                    return pe.value_load(tile_e[0:1, one(t)], min_val=0, max_val=E - 1) + 1 if experts else 0

                def down(t, b, m):
                    k = m % 2
                    e = chosen["down"]
                    if (experts or first_tile) and isinstance(t, int) and t < 1:
                        pe.wait_ge(RUNS[last_run]["o"].sem, last_count)
                    wait_apart(pe, R["lo"].sem, R["lo"].upto(t))
                    if not isinstance(t, int) or t >= 1:
                        wait_apart(pe, R["o"].sem, R["o"].upto(t - 1))
                    w = wexp[:, one(e), 2].rearrange("p o s (c n) -> p (o s) c n", n=D)
                    product(banks(6)[:, 0:D], [(ehT[:, k, HI, c * P:(c + 1) * P], ehT[:, k, LO, c * P:(c + 1) * P],
                                                w[:, HI, c, :], w[:, LO, c, :]) for c in range(EC)]).then_inc(R["y"].sem, 1)

                def turn(t, b, m):
                    k = m % 2
                    if (experts or first_tile) and isinstance(t, int) and t < 1:
                        pe.wait_ge(RUNS[last_run]["lo"].sem, last_count)
                    pe.wait_ge(R["h"].sem, R["h"].upto(t))
                    if not isinstance(t, int) or t >= 2:
                        pe.wait_ge(R["lo"].sem, R["lo"].upto(t - 2))
                    transposes(banks(4 + k), eh[:, k, :], EC, ident).then_inc(R["t"].sem, 1)

                def gate_up(t, b, m):
                    k = m % 2
                    e = chosen["gate_up"]
                    if (experts or first_tile) and isinstance(t, int) and t < 1:
                        pe.wait_ge(RUNS[last_run]["h"].sem, last_count)
                    if experts:
                        if isinstance(t, int) and t < 1:
                            pe.wait_ge(x_lo.sem, GS + 1)
                        wait_apart(pe, x_c.sem, x_c.upto(t))
                    if not isinstance(t, int) or t >= 2:
                        wait_apart(pe, R["h"].sem, R["h"].upto(t - 2))
                    for g in range(2):
                        w = wexp[:, one(e), g].rearrange("p o s (c n) -> p (o s) c n", n=DE)
                        last = product(banks(2 * g + k), [(a_of(t, k, HI, c), a_of(t, k, LO, c), w[:, HI, c, :], w[:, LO, c, :])
                                                          for c in range(KC)])
                    last.then_inc(R["g"].sem, 1)

                def turn_x(t, b, m):
                    pe.wait_ge(s_xg[m % 4], 16 * (2 * b + m // 4 + 1))
                    if not isinstance(t, int) or t >= 1:
                        pe.wait_ge(x_c.sem, x_c.upto(t - 1))
                    transposes(banks(7).bitcast(f16), xg[:, m % 4, :], 2 * KC, ident16).then_inc(x_t.sem, 1)
                chosen = {}

                def choose(stage):
                    def read(t, b, m):
                        chosen[stage] = expert(t)
                    return read
                stages = [(d, choose("gate_up")), (2 + d, choose("down")), (2 + d, down), (1 + d, turn), (d, gate_up)]
                if experts:
                    stages.append((0, turn_x))
                return 0, count, 8, stages

            pe.wait_ge(X_lo.sem, X_lo.upto(2))
            def choices_there(t, b, m):
                if t == NA - 1:
                    pe.wait_ge(routed, 3)
            sa = run(RUNS["sa"], NA, 0, False, lambda t, k, hl, c: zT[:, hl, c, tile_cols(t)])
            chained(pe, [sa[:3] + (sa[3] + [(0, choices_there)],),
                         (NA,) + run(RUNS["ex"], NS, 0, True, lambda t, k, hl, c: xgT[:, k, hl * D + c * P:hl * D + (c + 1) * P])[1:],
                         (NS + 1,) + run(RUNS["sb"], NB, NA, False, lambda t, k, hl, c: zT[:, hl, c, tile_cols(t + NA)])[1:]])


_INS = ['x', 'ctx_1024', 'L0_xattn_tab_g', 'L0_xattn_tab_b', 'L0_xattn_vid_g', 'L0_xattn_vid_b', 'L0_xattn_Wq', 'L0_xattn_Wk', 'L0_xattn_Wv', 'L0_xattn_q_g', 'L0_xattn_q_b', 'L0_xattn_k_g', 'L0_xattn_k_b', 'L0_xattn_Wo', 'L0_xattn_bo', 'L0_ffn_w_gate', 'L0_ffn_w_up', 'L0_ffn_w_down', 'L1_xattn_W', 'L1_xattn_b', 'L1_ffn_Wr', 'L1_ffn_Wg', 'L1_ffn_Wu', 'L1_ffn_Wd', 'L1_ffn_Sg', 'L1_ffn_Su', 'L1_ffn_Sd']
_OUTS = [((4, 512, 256), 'float32')]


def kernel(**inputs):
    import numpy as _np
    import concourse.bacc as _bacc
    from concourse import mybir as _mybir
    from concourse.bass_utils import run_bass_kernel_spmd as _run

    nc = _bacc.Bacc("TRN2", target_bir_lowering=False, num_devices=1)
    arrays, args = {}, []
    for name in _INS:
        a = _np.ascontiguousarray(inputs[name])
        arrays[f"in_{name}_dram"] = a
        args.append(nc.dram_tensor(f"in_{name}_dram", a.shape, _mybir.dt.from_np(a.dtype), kind="ExternalInput").ap())
    for i, (shape, dtype) in enumerate(_OUTS):
        dt = _mybir.dt.from_np(_np.dtype(dtype))
        args.append(nc.dram_tensor(f"out_{i}_dram", shape, dt, kind="ExternalOutput").ap())
    build(nc, *args)
    r = _run(nc, [arrays], core_ids=[0])
    return r.results[0]["out_0_dram"]
```
